# Optimizing a Trainium2 kernel written in Bass

```python
import numpy as np
import jax
import jax.numpy as jnp

def _softmax(x, axis=-1):
    return jax.nn.softmax(x, axis=axis)

def _gelu(x):
    return jax.nn.gelu(x, approximate=True)

def _silu(x):
    return jax.nn.silu(x)

def _sigmoid(x):
    return jax.nn.sigmoid(x)

def _layernorm(x, axis=-1, eps=1e-05):
    m = jnp.mean(x, axis=axis, keepdims=True)
    v = jnp.var(x, axis=axis, keepdims=True)
    return (x - m) / jnp.sqrt(v + eps)

def _scatter_add(tgt, idx, src, axis=0):
    return tgt.at[idx].add(src)

def _segment_sum(src, seg, n):
    return jax.ops.segment_sum(src, seg, n)
kernel_name = 'mk_adj_resnorm_d4_adj_r2_861291'

def setup_inputs(seed: int=0):
    np.random.seed(seed)
    _w = jnp.asarray

    def _rec_inputs():
        import jax
        import jax.numpy as jnp
        _gk = jax.random.key(seed)
        x = 7.22e-05 + 1 * jax.random.normal(jax.random.fold_in(_gk, 1), (8, 1024, 128), jnp.float32)
        _w = (1.0 + jnp.arange(1024, dtype=jnp.float32)) ** (-0.5)
        _w = _w / _w.mean()
        _pij = jnp.clip(0.00390625 * _w[:, None] * _w[None, :], 0.0, 1.0)
        _a = jax.random.uniform(jax.random.fold_in(_gk, 2), (8, 1024, 1024)) < _pij
        _a = jnp.logical_or(_a, jnp.swapaxes(_a, -1, -2))
        _a = jnp.logical_or(_a, jnp.eye(1024, dtype=bool))
        _af = _a.astype(jnp.float32)
        _af = _af / jnp.maximum(_af.sum(-1, keepdims=True), 1.0)
        adj = _af
        return (x, adj)
    x, adj = _rec_inputs()

    def _L0_gnn_setup():
        import jax, jax.numpy as jnp
        import numpy as np
        key = jax.random.key(seed)
        k1, k2, k3 = jax.random.split(key, 3)
        b, n, d, f = (16, 1024, 128, 128)
        features = jax.random.normal(k1, (b, n, d), dtype=jnp.float32)
        A = jax.random.uniform(k2, (b, n, n), dtype=jnp.float32)
        A = A / jnp.sum(A, axis=-1, keepdims=True)
        weight = jax.random.normal(k3, (2 * d, f), dtype=jnp.float32) * (1.0 / np.sqrt(2 * d))
        bias = jnp.zeros((f,), dtype=jnp.float32)
        return {'features': features, 'A': A, 'weight': weight, 'bias': bias}
    _L0_gnn_all = _L0_gnn_setup()
    _L0_gnn_in = {k: v for k, v in _L0_gnn_all.items() if k in ('weight', 'bias')}
    del _L0_gnn_all

    def _L1_gnn_setup():
        import jax, jax.numpy as jnp
        import numpy as np
        from jax import lax
        DIM = 128
        EPS = 1e-05

        def _bn(h, g, b, m, v):
            scale = g / jnp.sqrt(v + EPS)
            return h * scale[None, :, None] + (b - m * scale)[None, :, None]

        def _conv1d(h, w, pad):
            return lax.conv_general_dilated(h, w, window_strides=(1,), padding=[(pad, pad)], dimension_numbers=('NCH', 'OIH', 'NCH'))
        key = jax.random.key(seed)
        ks = jax.random.split(key, 16)
        bs, n, d = (16, 1024, DIM)
        s = 0.05
        return {'x': jax.random.normal(ks[0], (bs, n, d), jnp.float32), 'mask': jnp.ones((bs, n, n), jnp.float32), 'w_se': jax.random.normal(ks[1], (3, d), jnp.float32) * s, 'b_se': jnp.zeros((3,), jnp.float32), 'conv1_w': jax.random.normal(ks[2], (d, d, 1), jnp.float32) * s, 'bn1_g': jnp.ones((d,), jnp.float32), 'bn1_b': jnp.zeros((d,), jnp.float32), 'bn1_m': jnp.zeros((d,), jnp.float32), 'bn1_v': jnp.ones((d,), jnp.float32), 'conv2_w': jax.random.normal(ks[3], (d, d, 17), jnp.float32) * s, 'bn2_g': jnp.ones((d,), jnp.float32), 'bn2_b': jnp.zeros((d,), jnp.float32), 'bn2_m': jnp.zeros((d,), jnp.float32), 'bn2_v': jnp.ones((d,), jnp.float32), 'w_msg': jax.random.normal(ks[4], (d, d), jnp.float32) * s, 'b_msg': jnp.zeros((d,), jnp.float32), 'w_ih': jax.random.normal(ks[5], (3 * d, 2 * d), jnp.float32) * s, 'b_ih': jnp.zeros((3 * d,), jnp.float32), 'w_hh': jax.random.normal(ks[6], (3 * d, d), jnp.float32) * s, 'b_hh': jnp.zeros((3 * d,), jnp.float32)}
    _L1_gnn_all = _L1_gnn_setup()
    _L1_gnn_in = {k: v for k, v in _L1_gnn_all.items() if k in ('w_se', 'b_se', 'conv1_w', 'bn1_g', 'bn1_b', 'bn1_m', 'bn1_v', 'conv2_w', 'bn2_g', 'bn2_b', 'bn2_m', 'bn2_v', 'w_msg', 'b_msg', 'w_ih', 'b_ih', 'w_hh', 'b_hh')}
    del _L1_gnn_all

    def _L2_gnn_setup():
        import jax, jax.numpy as jnp
        import numpy as np
        H = 4
        NEG = -9000000000000000.0
        key = jax.random.key(seed)
        k1, k2, k3, k4 = jax.random.split(key, 4)
        B, N, D = (8, 512, 128)
        dh = D // H
        return {'node_features': jax.random.normal(k1, (B, N, D), dtype=jnp.float32), 'adjacency': jax.random.uniform(k2, (B, N, N), dtype=jnp.float32), 'W_proj': jax.random.normal(k3, (D, D), dtype=jnp.float32) * (1.0 / np.sqrt(D)), 'a_w': jax.random.normal(k4, (1, 2 * dh + 1), dtype=jnp.float32) * 0.1, 'bias': jnp.zeros((D,), dtype=jnp.float32)}
    _L2_gnn_all = _L2_gnn_setup()
    _L2_gnn_in = {k: v for k, v in _L2_gnn_all.items() if k in ('W_proj', 'a_w', 'bias')}
    del _L2_gnn_all

    def _L3_gnn_setup():
        import jax, jax.numpy as jnp
        import numpy as np
        K = 4
        EPS = 1e-09
        LEAKY_SLOPE = 0.2
        key = jax.random.key(seed)
        k1, k2, k3, k4, k5 = jax.random.split(key, 5)
        B, N, IN, OUT = (8, 1024, 128, 128)
        h = jax.random.normal(k1, (B, N, IN), dtype=jnp.float32)
        adj = jax.random.uniform(k2, (B, N, N), dtype=jnp.float32)
        W = jax.random.normal(k3, (OUT, IN), dtype=jnp.float32) * 0.05
        conv_w = jax.random.normal(k4, (K,), dtype=jnp.float32)
        conv_b = jax.random.normal(k5, (1,), dtype=jnp.float32)
        return {'h': h, 'adj': adj, 'W': W, 'conv_w': conv_w, 'conv_b': conv_b}
    _L3_gnn_all = _L3_gnn_setup()
    _L3_gnn_in = {k: v for k, v in _L3_gnn_all.items() if k in ('W', 'conv_w', 'conv_b')}
    del _L3_gnn_all
    return {'x': x, 'adj': adj, 'L0_gnn_weight': _L0_gnn_in['weight'], 'L0_gnn_bias': _L0_gnn_in['bias'], 'L1_gnn_w_se': _L1_gnn_in['w_se'], 'L1_gnn_b_se': _L1_gnn_in['b_se'], 'L1_gnn_conv1_w': _L1_gnn_in['conv1_w'], 'L1_gnn_bn1_g': _L1_gnn_in['bn1_g'], 'L1_gnn_bn1_b': _L1_gnn_in['bn1_b'], 'L1_gnn_bn1_m': _L1_gnn_in['bn1_m'], 'L1_gnn_bn1_v': _L1_gnn_in['bn1_v'], 'L1_gnn_conv2_w': _L1_gnn_in['conv2_w'], 'L1_gnn_bn2_g': _L1_gnn_in['bn2_g'], 'L1_gnn_bn2_b': _L1_gnn_in['bn2_b'], 'L1_gnn_bn2_m': _L1_gnn_in['bn2_m'], 'L1_gnn_bn2_v': _L1_gnn_in['bn2_v'], 'L1_gnn_w_msg': _L1_gnn_in['w_msg'], 'L1_gnn_b_msg': _L1_gnn_in['b_msg'], 'L1_gnn_w_ih': _L1_gnn_in['w_ih'], 'L1_gnn_b_ih': _L1_gnn_in['b_ih'], 'L1_gnn_w_hh': _L1_gnn_in['w_hh'], 'L1_gnn_b_hh': _L1_gnn_in['b_hh'], 'L2_gnn_W_proj': _L2_gnn_in['W_proj'], 'L2_gnn_a_w': _L2_gnn_in['a_w'], 'L2_gnn_bias': _L2_gnn_in['bias'], 'L3_gnn_W': _L3_gnn_in['W'], 'L3_gnn_conv_w': _L3_gnn_in['conv_w'], 'L3_gnn_conv_b': _L3_gnn_in['conv_b']}

def reference(x, adj, L0_gnn_weight, L0_gnn_bias, L1_gnn_w_se, L1_gnn_b_se, L1_gnn_conv1_w, L1_gnn_bn1_g, L1_gnn_bn1_b, L1_gnn_bn1_m, L1_gnn_bn1_v, L1_gnn_conv2_w, L1_gnn_bn2_g, L1_gnn_bn2_b, L1_gnn_bn2_m, L1_gnn_bn2_v, L1_gnn_w_msg, L1_gnn_b_msg, L1_gnn_w_ih, L1_gnn_b_ih, L1_gnn_w_hh, L1_gnn_b_hh, L2_gnn_W_proj, L2_gnn_a_w, L2_gnn_bias, L3_gnn_W, L3_gnn_conv_w, L3_gnn_conv_b):
    import jax
    import jax.numpy as jnp

    def _L0_gnn_ref(features, A, weight, bias):
        import jax, jax.numpy as jnp
        import numpy as np
        agg = jnp.einsum('bnm,bmd->bnd', A, features)
        d = features.shape[-1]
        out = jnp.einsum('bnd,df->bnf', features, weight[:d]) + jnp.einsum('bnd,df->bnf', agg, weight[d:]) + bias
        return jax.nn.relu(out)

    def _L1_gnn_ref(x, mask, w_se, b_se, conv1_w, bn1_g, bn1_b, bn1_m, bn1_v, conv2_w, bn2_g, bn2_b, bn2_m, bn2_v, w_msg, b_msg, w_ih, b_ih, w_hh, b_hh):
        import jax, jax.numpy as jnp
        import numpy as np
        from jax import lax
        DIM = 128
        EPS = 1e-05

        def _bn(h, g, b, m, v):
            scale = g / jnp.sqrt(v + EPS)
            return h * scale[None, :, None] + (b - m * scale)[None, :, None]

        def _conv1d(h, w, pad):
            return lax.conv_general_dilated(h, w, window_strides=(1,), padding=[(pad, pad)], dimension_numbers=('NCH', 'OIH', 'NCH'))
        d = x.shape[-1]
        xc = jnp.transpose(x, (0, 2, 1))
        h = _bn(_conv1d(xc, conv1_w, 0), bn1_g, bn1_b, bn1_m, bn1_v)
        h = jax.nn.relu(h)
        h = _bn(_conv1d(h, conv2_w, 8), bn2_g, bn2_b, bn2_m, bn2_v)
        x_conv = jnp.transpose(jax.nn.relu(h + xc), (0, 2, 1))
        s = x @ w_se.T + b_se
        sq = jnp.sum(s * s, axis=-1)
        dist = sq[:, :, None] + sq[:, None, :] - 2.0 * jnp.einsum('bnd,bmd->bnm', s, s)
        A = jnp.exp(-dist) * mask
        msg = jax.nn.relu(x @ w_msg.T + b_msg)
        x_nmp = jnp.einsum('bnm,bmd->bnd', A, msg)
        x_in = jnp.concatenate([x_conv, x_nmp], axis=-1)
        gi = x_in @ w_ih.T + b_ih
        gh = x @ w_hh.T + b_hh
        gi_r, gi_z, gi_n = (gi[..., :d], gi[..., d:2 * d], gi[..., 2 * d:])
        gh_r, gh_z, gh_n = (gh[..., :d], gh[..., d:2 * d], gh[..., 2 * d:])
        r = jax.nn.sigmoid(gi_r + gh_r)
        z = jax.nn.sigmoid(gi_z + gh_z)
        nn_ = jnp.tanh(gi_n + r * gh_n)
        return (1.0 - z) * nn_ + z * x

    def _L2_gnn_ref(node_features, adjacency, W_proj, a_w, bias):
        import jax, jax.numpy as jnp
        import numpy as np
        H = 4
        NEG = -9000000000000000.0
        B, N, D = node_features.shape
        dh = D // H
        h = (node_features @ W_proj.T).reshape(B, N, H, dh)
        w = a_w[0]
        wl, wr, we = (w[:dh], w[dh:2 * dh], w[2 * dh])
        s_left = jnp.einsum('bihd,d->bih', h, wl)
        s_right = jnp.einsum('bjhd,d->bjh', h, wr)
        scores = s_left[:, :, None, :] + s_right[:, None, :, :] + adjacency[..., None] * we
        scores = jax.nn.leaky_relu(scores, negative_slope=0.2)
        pad = (adjacency <= 1e-05).astype(scores.dtype)
        scores = scores + (NEG * pad)[..., None]
        attn = jax.nn.softmax(scores, axis=2)
        agg = jnp.einsum('bijh,bjhd->bihd', attn, h).reshape(B, N, D)
        out = jax.nn.leaky_relu(node_features + agg + bias, negative_slope=0.5)
        return out

    def _L3_gnn_ref(h, adj, W, conv_w, conv_b):
        import jax, jax.numpy as jnp
        import numpy as np
        K = 4
        EPS = 1e-09
        LEAKY_SLOPE = 0.2
        h_trans = jnp.einsum('bni,oi->bno', h, W)
        row_sum = adj.sum(axis=2, keepdims=True) + EPS
        adj_norm = adj / row_sum
        curr = h_trans
        out = conv_w[0] * curr
        for k in range(1, K):
            curr = jnp.einsum('bnm,bmo->bno', adj_norm, curr)
            out = out + conv_w[k] * curr
        out = out + conv_b[0]
        return jnp.where(out >= 0, out, LEAKY_SLOPE * out)
    x = _layernorm(x + _L0_gnn_ref(x, adj, L0_gnn_weight, L0_gnn_bias), axis=-1)
    x = _layernorm(x + _L1_gnn_ref(x, adj, L1_gnn_w_se, L1_gnn_b_se, L1_gnn_conv1_w, L1_gnn_bn1_g, L1_gnn_bn1_b, L1_gnn_bn1_m, L1_gnn_bn1_v, L1_gnn_conv2_w, L1_gnn_bn2_g, L1_gnn_bn2_b, L1_gnn_bn2_m, L1_gnn_bn2_v, L1_gnn_w_msg, L1_gnn_b_msg, L1_gnn_w_ih, L1_gnn_b_ih, L1_gnn_w_hh, L1_gnn_b_hh), axis=-1)
    x = _layernorm(x + _L2_gnn_ref(x, adj, L2_gnn_W_proj, L2_gnn_a_w, L2_gnn_bias), axis=-1)
    x = _layernorm(x + _L3_gnn_ref(x, adj, L3_gnn_W, L3_gnn_conv_w, L3_gnn_conv_b), axis=-1)
    return x

_drawn_inputs = setup_inputs


def setup_inputs(seed=0):
    import zlib

    import numpy as np

    out = dict(_drawn_inputs(seed))
    spreads = {'L0_gnn_bias': (0.0, 0.1),
     'L1_gnn_b_se': (0.0, 2.0),
     'L1_gnn_bn1_g': (1.0, 0.595),
     'L1_gnn_bn1_b': (0.0, 0.407),
     'L1_gnn_bn1_m': (0.0, 0.374),
     'L1_gnn_bn1_v': (1.0, 0.6),
     'L1_gnn_bn2_g': (1.0, 0.2),
     'L1_gnn_bn2_b': (0.0, 0.72),
     'L1_gnn_bn2_m': (0.0, 0.531),
     'L1_gnn_bn2_v': (1.0, 0.6),
     'L1_gnn_b_msg': (0.0, 2.0),
     'L1_gnn_b_ih': (0.0, 0.3),
     'L1_gnn_b_hh': (0.0, 0.376),
     'L2_gnn_bias': (0.0, 0.1)}
    factors = {'L1_gnn_w_se': 64.0, 'L1_gnn_w_msg': 4.058}
    for name, (base, spread) in spreads.items():
        noise = np.random.default_rng([zlib.crc32(name.encode()), seed]).standard_normal(out[name].shape)
        drawn = base * np.exp(spread * noise) if base else spread * noise
        out[name] = jnp.asarray(drawn.astype(out[name].dtype))
    for name, factor in factors.items():
        out[name] = (out[name] * factor).astype(out[name].dtype)
    return out
```

```python
import concourse.bass as bass
from concourse import mybir
from contextlib import ExitStack


def gnn_stack_kernel(nc: bass.Bass, a, out: bass.AP):
    f32 = mybir.dt.float32
    f16 = mybir.dt.float16
    ALU = mybir.AluOpType
    ACT = mybir.ActivationFunctionType

    B, N, D = a["x"].shape
    P = 128
    T = N // P
    H = 4
    DH = D // H
    TAPS = a["L1_gnn_conv2_w"].shape[2]
    PAD = TAPS // 2
    HALF = 512
    NS = float(N)
    WS = 64.0
    LN_EPS = 1e-5
    BN_EPS = 1e-5
    ROW_EPS = 1e-9
    SLOPE2 = 0.2
    SLOPE2_OUT = 0.5
    SLOPE3 = 0.2
    MASKED = -float(2 ** 55)

    W_SELF, W_AGG = 0, 1
    W_CONV1 = 2
    W_CONV2 = 3
    W_MSG = W_CONV2 + TAPS
    W_IH = W_MSG + 1
    W_HH = W_IH + 6
    W_PROJ = W_HH + 3
    W_HOP = W_PROJ + 1
    NW = W_HOP + 1
    NT = NW - 2

    R_B0, R_BM, R_B2, R_CW, R_CB, R_AW = 0, D, 2 * D, 3 * D, 3 * D + 4, 3 * D + 5
    NR = R_AW + 2 * DH + 1

    USES = {
        "QA": ["x0T", "y", "l0_0", "l0_1", "x1T", "conv1", "conv2", "msg", "nmp", "gate_r",
               "hid_n", "l1r", "x2T", "h2", "sr_0", "sr_1", "sr_2", "sr_3", "x3T", "h3"],
        "QB0": [f"adj{t}" for t in range(0, T, 2)] + [f"dist{t}" for t in range(T)] + ["gate_z"]
               + [f"pT{i}" for i in range(0, T * H, 2)],
        "QB1": [f"adj{t}" for t in range(1, T, 2)] + [f"mask{t}" for t in range(T)] + ["in_n"]
               + [f"pT{i}" for i in range(1, T * H, 2)],
        "R0": ["s0", "nsq"] + [f"att{t}" for t in range(T)] + [f"hop{k}_0" for k in range(3)],
        "R1": ["s1", "sl"] + [f"attT{t}" for t in range(T)] + [f"hop{k}_1" for k in range(3)],
    }
    WHERE = {use: (slot, j) for slot, uses in USES.items() for j, use in enumerate(uses)}

    ctx = ExitStack()
    with ctx:
        def sb(name, shape, dt=f32):
            return ctx.enter_context(nc.sbuf_tensor(name, shape, dt))

        def sem(name):
            return ctx.enter_context(nc.semaphore(name))

        slot = {q: ctx.enter_context(nc.psum_tensor(q, [P, N if q[0] == "Q" else HALF], f32))
                for q in USES}
        filled = {q: sem(f"filled_{q}") for q in USES}

        ident = sb("ident", [P, P])
        ident16 = sb("ident16", [P, P], f16)
        ones_row = sb("ones_row", [1, P])
        neg3 = sb("neg3", [3, P])
        w_hi = sb("w_hi", [P, NW, P], f16)
        w_lo = sb("w_lo", [P, NW, P], f16)
        w_seT = sb("w_seT", [P, 3])
        rows = sb("rows", [1, NR])
        rowc = sb("rowc", [P, NR])
        bn = sb("bn", [P, 4, 2])
        bn_scale = sb("bn_scale", [P, 2])
        bn_shift = sb("bn_shift", [P, 2])
        bn_tmp = sb("bn_tmp", [P, 2])
        minus_half = sb("minus_half", [P, T])
        gate_b = sb("gate_b", [P, 2, 3])
        half_b = sb("half_b", [P, 2])
        hid_b = sb("hid_b", [P, 1])
        b_se = sb("b_se", [3, 1])
        a_blk = sb("a_blk", [P, 2 * H])
        v_lr = sb("v_lr", [P, 2 * H])
        vr_f = sb("vr_f", [P, H, P])
        vr_hi = sb("vr_hi", [P, H, P], f16)
        vr_lo = sb("vr_lo", [P, H, P], f16)

        adj_in = sb("adj_in", [P, 2, N])
        t_hi = sb("t_hi", [P, T, N], f16)
        t_lo = sb("t_lo", [P, T, N], f16)
        xa = sb("xa", [P, T, D])
        xb = sb("xb", [P, T, D])
        xT = sb("xT", [P, N])
        xT_hi = sb("xT_hi", [P, N], f16)
        xT_lo = sb("xT_lo", [P, N], f16)
        y_hi = sb("y_hi", [P, T, D + 1], f16)
        y_lo = sb("y_lo", [P, T, D], f16)
        rinv = sb("rinv", [P, T])
        stats = sb("stats", [P, T, 6])
        mv = sb("mv", [P, T, 2])
        rstd = sb("rstd", [P, T])
        fa = sb("fa", [P, N])
        c_hi = sb("c_hi", [P, N + 2 * PAD], f16)
        c_lo = sb("c_lo", [P, N + 2 * PAD], f16)
        xc_hi = sb("xc_hi", [P, N], f16)
        xc_lo = sb("xc_lo", [P, N], f16)
        xn_hi = sb("xn_hi", [P, N], f16)
        xn_lo = sb("xn_lo", [P, N], f16)
        m_hi = sb("m_hi", [P, T, D], f16)
        m_lo = sb("m_lo", [P, T, D], f16)
        nsq = sb("nsq", [P, T])
        work = sb("work", [P, 10, N])
        expd, gw = work[:, 0:2, :], work[:, 2:4, :]
        g_hl = work[:, 4:6, :].bitcast(f16).rearrange("p k (h n) -> p k h n", h=2)
        gate_t, hid, cand = work[:, 0:2, :], work[:, 2, :], work[:, 3, :]
        zbuf, relu, pT = work[:, 0:4, :], work[:, 4:6, :], work[:, 6:10, :]
        sr = sb("sr", [P, H, N])
        sT, s2T, sqT = sr[0:3, 0, :], sr[0:3, 1, :], sr[0:3, 2, :]
        escore = sb("escore", [P, 2, N])
        padv = sb("padv", [P, N])
        h2 = sb("h2", [P, T, D])
        sl = sb("sl", [P, T, H])
        sl4 = sb("sl4", [P, T, H])
        zmax = sb("zmax", [P, T, H])
        ebias = sb("ebias", [P, T, H])
        etmp = sb("etmp", [P, T, H])
        rsum = sb("rsum", [P, T, H])
        attT = sb("attT", [P, P])
        attn = sb("attn", [P, P])
        h3 = sb("h3", [P, T, D])
        vk = sb("vk", [P, T, D])
        vk_hi = sb("vk_hi", [P, T, D], f16)
        vk_lo = sb("vk_lo", [P, T, D], f16)

        S = {n: sem(n) for n in (
            "const_loaded small_loaded pool_const w_filled w_hi_made w_lo_made vec_made bn_ready "
            "adj_loaded0 adj_loaded1 x_loaded e_loaded0 e_loaded1 out_stored "
            "t_hi_made t_lo_made xT_made xT_hi_made xT_lo_made y_hi_made y_lo_made l0_pre l0_sum "
            "ln_stats ln_mv ln_eps ln_rstd ln_done fa_made c_hi_made c_lo_made c2_made xc_made rs_made hop_read wh_made dve_once apart rinv_made x2b_made g_used sl4_made "
            "xc_hi_made xc_lo_made msg_pre m_hi_made m_lo_made s_made s2_made sq_made nsq_made "
            "exp_made g_made g_hi_made g_lo_made xn_made xn_hi_made xn_lo_made tanh_r tanh_z "
            "hid_made u_made v_made cand_made w_made w2_made o_made r1_made r1_nat "
            "h2_made sl_made sr_made pad_made e_made z_made relu_made zr_made zsum leak eb p_made "
            "pT_made attT_made rs_inv att_scaled att_pre att_leak r2_made "
            "h3_made vk_pre vk_made vk_hi_made vk_lo_made out_pre out_leak r3_made").split()}

        N_CONST = 34
        N_GROUPS = (NT + T - 1) // T
        W_DONE = N_GROUPS + 3

        PER = {"ln_done": 4, "ln_stats": 4, "ln_mv": 4, "ln_eps": 4, "ln_rstd": 4, "t_hi_made": T,
               "t_lo_made": T, "xT_made": 4, "xT_hi_made": 4, "xT_lo_made": 4, "rs_made": 2,
               "l0_pre": 2, "l0_sum": 2, "s_made": 2, "exp_made": T, "g_made": T, "g_used": T - 1,
               "g_hi_made": T, "g_lo_made": T, "sr_made": H, "pad_made": T, "e_made": T,
               "z_made": T * H, "relu_made": T * H, "zr_made": T * H, "zsum": T, "leak": T, "eb": T,
               "p_made": T * H, "pT_made": T * H, "attT_made": T, "att_scaled": T, "att_pre": T,
               "att_leak": T, "r2_made": T, "wh_made": 3, "vk_made": 2, "hop_read": 6, "vk_hi_made": 6,
               "vk_lo_made": 6}
        READ_BY = {"x0T": ("xT_made", 1), "y": ("y_lo_made", 1), "l0_0": ("rs_made", 1),
                   "l0_1": ("rs_made", 2), "x1T": ("xT_made", 2), "conv1": ("fa_made", 1),
                   "conv2": ("c2_made", 1), "msg": ("msg_pre", 1), "nmp": ("xn_made", 1),
                   "gate_r": ("tanh_r", 1), "hid_n": ("hid_made", 1), "l1r": ("r1_nat", 1),
                   "x2T": ("xT_made", 3), "h2": ("h2_made", 1), "x3T": ("xT_made", 4),
                   "h3": ("h3_made", 1), "gate_z": ("tanh_z", 1), "in_n": ("v_made", 1),
                   "s0": ("s_made", 1), "s1": ("s_made", 2), "nsq": ("nsq_made", 1),
                   "sl": ("sl_made", 1)}
        READ_BY |= {f"sr_{h}": ("sr_made", h + 1) for h in range(H)}
        READ_BY |= {f"adj{t}": ("t_lo_made", t + 1) for t in range(T)}
        READ_BY |= {f"dist{t}": ("exp_made", t + 1) for t in range(T)}
        READ_BY |= {f"mask{t}": ("g_made", t + 1) for t in range(T)}
        READ_BY |= {f"pT{i}": ("pT_made", i + 1) for i in range(T * H)}
        READ_BY |= {f"att{t}": ("attT_made", t + 1) for t in range(T)}
        READ_BY |= {f"attT{t}": ("att_scaled", t + 1) for t in range(T)}
        READ_BY |= {f"hop{k}_{g}": ("hop_read", 2 * k + g + 1) for k in range(3) for g in range(2)}

        ACT_START = ("t_hi_made", "h3_made", "pT_made", "relu_made")
        DVE_START = ("ln_done", "z_made", "xT_lo_made", "zr_made", "hop_read")
        PE_START = ("g_used",)
        START_AT_1 = ACT_START + DVE_START + PE_START

        block = ctx.enter_context(nc.Block())

        def wait_apart(eng, *waits):
            for semaphore, value in waits:
                eng.wait_ge(semaphore, value)
            eng.sem_inc(S["apart"], 1)

        def count(name, b, k):
            return b * PER.get(name, 1) + k + (name in START_AT_1)

        def start(eng, *names):
            for name in names:
                assert name in START_AT_1
                eng.sem_inc(S[name], 1)

        def may_fill(eng, b, use):
            q, j = WHERE[use]
            name, k = READ_BY[USES[q][j - 1]]
            eng.wait_ge(S[name], count(name, b, k if j else 0))
            return slot[q]

        def fill_done(ins, use):
            ins.then_inc(filled[WHERE[use][0]], 1)

        def wait_full(eng, b, use):
            q, j = WHERE[use]
            eng.wait_ge(filled[q], b * len(USES[q]) + j + 1)
            return slot[q]

        def made(eng, name, b, k):
            eng.wait_ge(S[name], count(name, b, k))

        x_dram, adj_dram = a["x"], a["adj"]

        @block.sync
        def _(sp):
            raw = work[:, 0:4, :].rearrange("p a n -> p (a n)")
            w0raw = escore[:, 0, 0:2 * P].rearrange("p (a f) -> p a f", a=2)

            def load(dst, src, to="const_loaded"):
                sp.dma_start(dst, src).then_inc(S[to], 16)

            o = P * (1 + TAPS)
            load(raw[:, 0:P], a["L1_gnn_conv1_w"].rearrange("o c k -> o (c k)"))
            load(raw[:, P:o], a["L1_gnn_conv2_w"].rearrange("o c k -> o (c k)"))
            load(raw[:, o:o + P], a["L1_gnn_w_msg"])
            load(raw[:, o + P:o + 7 * P].rearrange("p (g k) -> p g k", g=3),
                 a["L1_gnn_w_ih"].rearrange("(g p) k -> p g k", p=P))
            load(raw[:, o + 7 * P:o + 10 * P].rearrange("p (g k) -> p g k", g=3),
                 a["L1_gnn_w_hh"].rearrange("(g p) k -> p g k", p=P))
            load(raw[:, o + 10 * P:o + 11 * P], a["L2_gnn_W_proj"])
            load(raw[:, o + 11 * P:o + 12 * P], a["L3_gnn_W"])
            load(w0raw, a["L0_gnn_weight"].rearrange("(a p) f -> p a f", p=P))
            load(padv[0:3, 0:P], a["L1_gnn_w_se"])
            for off, name in ((R_B0, "L0_gnn_bias"), (R_BM, "L1_gnn_b_msg"), (R_B2, "L2_gnn_bias"),
                              (R_CW, "L3_gnn_conv_w"), (R_CB, "L3_gnn_conv_b")):
                load(rows[0:1, off:off + a[name].shape[0]], a[name].rearrange("(a n) -> a n", a=1))
            load(rows[0:1, R_AW:NR], a["L2_gnn_a_w"])
            for i, kind in enumerate("gbmv"):
                for j in (1, 2):
                    load(bn[:, i, j - 1:j], a[f"L1_gnn_bn{j}_{kind}"].rearrange("(p a) -> p a", a=1))
            with nc.allow_non_contiguous_dma(reason="768 bias values, once"):
                load(gate_b[:, 0, :], a["L1_gnn_b_ih"].rearrange("(g p) -> p g", p=P))
                load(gate_b[:, 1, :], a["L1_gnn_b_hh"].rearrange("(g p) -> p g", p=P))
            load(b_se[:, :], a["L1_gnn_b_se"].rearrange("(p a) -> p a", a=1))
            sp.wait_ge(S["pool_const"], 1)
            for h in range(H):
                for side in range(2):
                    load(a_blk[h * DH:(h + 1) * DH, side * H + h:side * H + h + 1],
                         a["L2_gnn_a_w"][0:1, side * DH:(side + 1) * DH].rearrange("a p -> p a"))
            sp.wait_ge(S["w_lo_made"], W_DONE)

            with sp.Fori(0, B) as b:
                made(sp, "ln_done", b, 0)
                sp.dma_start(xa[:, :, :], x_dram[bass.ds(b, 1), :, :].rearrange(
                    "a (t p) d -> p (a t) d", p=P)).then_inc(S["x_loaded"], 16)
                for t in range(T):
                    made(sp, "t_hi_made", b, max(t - 1, 0))
                    sp.dma_start(adj_in[:, t % 2, :], adj_dram[bass.ds(b, 1), t * P:(t + 1) * P, :]
                                 .rearrange("a p m -> p (a m)")).then_inc(S[f"adj_loaded{t % 2}"], 16)
                for t in range(T):
                    made(sp, "z_made", b, H * max(t - 1, 0))
                    sp.dma_start(escore[:, t % 2, :], adj_dram[bass.ds(b, 1), t * P:(t + 1) * P, :]
                                 .rearrange("a p m -> p (a m)")).then_inc(S[f"e_loaded{t % 2}"], 16)
                made(sp, "ln_done", b, 4)
                sp.dma_start(out[bass.ds(b, 1), :, :].rearrange("a (t p) d -> p (a t) d", p=P),
                             xb[:, :, :]).then_inc(S["out_stored"], 16)
            sp.wait_ge(S["out_stored"], 16 * B)

        @block.gpsimd
        def _(pool):
            pool.memset(a_blk[:, :], 0.0).then_inc(S["pool_const"], 1)
            pool.memset(ident[:, :], 0.0).then_inc(S["pool_const"], 1)
            pool.memset(ones_row[:, :], 1.0).then_inc(S["pool_const"], 1)
            pool.memset(neg3[:, :], -1.0).then_inc(S["pool_const"], 1)
            pool.memset(minus_half[:, :], -0.5).then_inc(S["pool_const"], 1)
            pool.memset(c_hi[:, :], 0.0).then_inc(S["pool_const"], 1)
            pool.memset(c_lo[:, :], 0.0).then_inc(S["pool_const"], 1)
            pool.memset(y_hi[:, :, D:D + 1], 1.0).then_inc(S["pool_const"], 1)
            pool.wait_ge(S["pool_const"], 2)
            pool.affine_select(out=ident[:, :], in_=ident[:, :], compare_op=ALU.not_equal, fill=1.0,
                               base=0, pattern=[[-1, P]], channel_multiplier=1)\
                .then_inc(S["pool_const"], 1)
            pool.wait_ge(S["const_loaded"], 16 * N_CONST)
            pool.wait_ge(S["pool_const"], 5)
            pool.tensor_scalar(bn_tmp[:, :], bn[:, 3, :], BN_EPS, None, ALU.add)\
                .then_inc(S["bn_ready"], 1)
            pool.wait_ge(S["bn_ready"], 1)
            pool.tensor_tensor(bn_tmp[:, :], bn_tmp[:, :], minus_half[:, 0:2], ALU.pow)\
                .then_inc(S["bn_ready"], 1)

            def inv_std(b, k):
                wait_apart(pool, (S["ln_mv"], count("ln_mv", b, k + 1)))
                pool.tensor_scalar(rstd[:, :], mv[:, :, 1], LN_EPS, None, ALU.add)\
                    .then_inc(S["ln_eps"], 1)
                made(pool, "ln_eps", b, k + 1)
                pool.tensor_tensor(rstd[:, :], rstd[:, :], minus_half[:, :], ALU.pow)\
                    .then_inc(S["ln_rstd"], 1)

            with pool.Fori(0, B) as b:
                for k in range(4):
                    inv_std(b, k)

        @block.tensor
        def _(pe):
            raw = work[:, 0:4, :].rearrange("p a n -> p (a n)")
            start(pe, *PE_START)

            def mm(o, lhsT, rhs, start, stop):
                return pe.matmul(o, lhsT, rhs, start=start, stop=stop)

            def three(o, l_hi, l_lo, r_hi, r_lo, start=True, stop=True):
                mm(o, l_hi, r_hi, start, False)
                mm(o, l_hi, r_lo, False, False)
                return mm(o, l_lo, r_hi, False, stop)

            def col(t):
                return slice(t * P, (t + 1) * P)

            def half(i):
                return slice(i * HALF, (i + 1) * HALF)

            pe.wait_ge(S["const_loaded"], 16 * N_CONST)
            pe.wait_ge(S["pool_const"], 9)
            for g in range(0, NT, T):
                q = slot["QB0"] if g // T % 2 == 0 else slot["QB1"]
                if g >= 2 * T:
                    pe.wait_ge(S["w_lo_made"], g // T - 1)
                for i in range(g, min(g + T, NT)):
                    if 1 <= i <= TAPS:
                        src = raw[:, P:P * (1 + TAPS)].rearrange("p (c k) -> p k c", k=TAPS)[:, i - 1, :]
                    else:
                        src = raw[:, col(i)]
                    last = pe.transpose(q[:, col(i - g)], src, ident[:, :])
                last.then_inc(S["w_filled"], 1)
            pe.transpose(slot["QA"][:, 0:3], padv[0:3, 0:P], ident[0:3, 0:3])
            mm(slot["QA"][:, HALF:HALF + NR], ones_row[:, :], rows[:, :], True, True)
            proj = raw[:, col(NT - 2)]
            mm(slot["R0"][:, 0:2 * H], proj, a_blk[:, :], True, True).then_inc(S["w_filled"], 1)

            def transposed(b, use, src):
                q = may_fill(pe, b, use)
                for t in range(T):
                    last = pe.transpose(q[:, col(t)], src[:, t, :], ident[:, :])
                fill_done(last, use)

            def xT_is_split(b, k):
                made(pe, "xT_hi_made", b, k + 1)
                made(pe, "xT_lo_made", b, k + 1)

            def rows_times(b, use, w):
                q = may_fill(pe, b, use)
                for t in range(T):
                    last = three(q[:, col(t)], xT_hi[:, col(t)], xT_lo[:, col(t)],
                                 w_hi[:, w, :], w_lo[:, w, :])
                fill_done(last, use)

            with pe.Fori(0, B) as b:
                pe.wait_ge(S["x_loaded"], b * 16 + 16)
                transposed(b, "x0T", xa)
                for t in range(T):
                    pe.wait_ge(S[f"adj_loaded{t % 2}"], b * (8 * T) + 16 * (t // 2 + 1))
                    q = may_fill(pe, b, f"adj{t}")
                    for m in range(T):
                        last = pe.transpose(q[:, col(m)], adj_in[:, t % 2, col(m)], ident[:, :])
                    fill_done(last, f"adj{t}")
                xT_is_split(b, 0)
                rows_times(b, "y", W_AGG)
                made(pe, "y_hi_made", b, 1)
                made(pe, "y_lo_made", b, 1)
                made(pe, "t_hi_made", b, T)
                made(pe, "t_lo_made", b, T)
                for g in range(2):
                    q = may_fill(pe, b, f"l0_{g}")
                    for i in range(4):
                        t = 4 * g + i
                        o = q[:, 256 * i:256 * i + D + 1]
                        for m in range(T):
                            mm(o, t_hi[:, m, col(t)], y_hi[:, m, :], m == 0, False)
                            mm(o[:, 0:D], t_hi[:, m, col(t)], y_lo[:, m, :], False, False)
                            mm(o, t_lo[:, m, col(t)], y_hi[:, m, :], False, False)
                        last = three(o[:, 0:D], xT_hi[:, col(t)], xT_lo[:, col(t)],
                                     w_hi[:, W_SELF, :], w_lo[:, W_SELF, :], start=False)
                    fill_done(last, f"l0_{g}")

                made(pe, "ln_done", b, 1)
                transposed(b, "x1T", xa)
                xT_is_split(b, 1)
                q = may_fill(pe, b, "conv1")
                for i in range(2):
                    last = three(q[:, half(i)], w_hi[:, W_CONV1, :], w_lo[:, W_CONV1, :],
                                 xT_hi[:, half(i)], xT_lo[:, half(i)])
                fill_done(last, "conv1")
                for i in range(2):
                    q = may_fill(pe, b, f"s{i}")
                    fill_done(mm(q[0:3, :], w_seT[:, :], xT[:, half(i)], True, True), f"s{i}")
                made(pe, "c_hi_made", b, 1)
                made(pe, "c_lo_made", b, 1)
                q = may_fill(pe, b, "conv2")
                for i in range(2):
                    for k in range(TAPS):
                        at = slice(i * HALF + k, i * HALF + k + HALF)
                        last = three(q[:, half(i)], w_hi[:, W_CONV2 + k, :], w_lo[:, W_CONV2 + k, :],
                                     c_hi[:, at], c_lo[:, at], start=k == 0, stop=k == TAPS - 1)
                fill_done(last, "conv2")
                rows_times(b, "msg", W_MSG)
                made(pe, "sq_made", b, 1)
                q = may_fill(pe, b, "nsq")
                for t in range(T):
                    last = mm(q[:, t:t + 1], sqT[:, col(t)], neg3[:, 0:1], True, True)
                fill_done(last, "nsq")
                made(pe, "s2_made", b, 1)

                def distance(t):
                    q = may_fill(pe, b, f"dist{t}")
                    for i in range(2):
                        mm(q[:, half(i)], s2T[:, col(t)], sT[:, half(i)], True, False)
                        last = mm(q[:, half(i)], neg3[:, :], sqT[:, half(i)], False, True)
                    fill_done(last, f"dist{t}")
                    q = may_fill(pe, b, f"mask{t}")
                    for i in range(2):
                        mm(q[:, half(i)], ident16[:, :], t_hi[:, t, half(i)], True, False)
                        last = mm(q[:, half(i)], ident16[:, :], t_lo[:, t, half(i)], False, True)
                    fill_done(last, f"mask{t}")

                def message(t):
                    made(pe, "g_hi_made", b, t + 1)
                    made(pe, "g_lo_made", b, t + 1)
                    for i in range(2):
                        last = three(q_nmp[:, half(i)], m_hi[:, t, :], m_lo[:, t, :],
                                     g_hl[:, t % 2, 0, half(i)], g_hl[:, t % 2, 1, half(i)],
                                     start=t == 0, stop=t == T - 1)
                    if t < T - 1:
                        last.then_inc(S["g_used"], 1)
                    else:
                        fill_done(last, "nmp")

                distance(0)
                made(pe, "m_hi_made", b, 1)
                made(pe, "m_lo_made", b, 1)
                q_nmp = may_fill(pe, b, "nmp")
                for t in range(T):
                    if t + 1 < T:
                        distance(t + 1)
                    message(t)
                made(pe, "xc_hi_made", b, 1)
                made(pe, "xc_lo_made", b, 1)
                made(pe, "xn_hi_made", b, 1)
                made(pe, "xn_lo_made", b, 1)

                def gate(use, blocks):
                    q = may_fill(pe, b, use)
                    for i in range(2):
                        for j, (w, r_hi, r_lo) in enumerate(blocks):
                            last = three(q[:, half(i)], w_hi[:, w, :], w_lo[:, w, :],
                                         r_hi[:, half(i)], r_lo[:, half(i)],
                                         start=j == 0, stop=j == len(blocks) - 1)
                    fill_done(last, use)

                gate("gate_r", [(W_IH, xc_hi, xc_lo), (W_IH + 1, xn_hi, xn_lo), (W_HH, xT_hi, xT_lo)])
                gate("gate_z", [(W_IH + 2, xc_hi, xc_lo), (W_IH + 3, xn_hi, xn_lo),
                                (W_HH + 1, xT_hi, xT_lo)])
                gate("hid_n", [(W_HH + 2, xT_hi, xT_lo)])
                gate("in_n", [(W_IH + 4, xc_hi, xc_lo), (W_IH + 5, xn_hi, xn_lo)])
                made(pe, "r1_made", b, 1)
                q = may_fill(pe, b, "l1r")
                for t in range(T):
                    last = pe.transpose(q[:, col(t)], fa[:, col(t)], ident[:, :])
                fill_done(last, "l1r")

                made(pe, "ln_done", b, 2)
                transposed(b, "x2T", xb)
                xT_is_split(b, 2)
                rows_times(b, "h2", W_PROJ)
                q = may_fill(pe, b, "sl")
                for t in range(T):
                    last = mm(q[:, H * t:H * t + H], xT[:, col(t)], v_lr[:, 0:H], True, True)
                fill_done(last, "sl")
                for h in range(H):
                    q = may_fill(pe, b, f"sr_{h}")
                    for i in range(2):
                        last = three(q[:, half(i)], vr_hi[:, h, :], vr_lo[:, h, :],
                                     xT_hi[:, half(i)], xT_lo[:, half(i)])
                    fill_done(last, f"sr_{h}")

                def attend(t):
                    made(pe, "pT_made", b, H * (t + 1))
                    q = may_fill(pe, b, f"att{t}")
                    for j in range(T):
                        for h in range(H):
                            last = mm(q[h * DH:(h + 1) * DH, 0:P], h2[:, j, h * DH:(h + 1) * DH],
                                      pT[:, h, col(j)], j == 0, j == T - 1)
                    fill_done(last, f"att{t}")
                    made(pe, "attT_made", b, t + 1)
                    q = may_fill(pe, b, f"attT{t}")
                    fill_done(pe.transpose(q[:, 0:P], attT[:, :], ident[:, :]), f"attT{t}")

                made(pe, "h2_made", b, 1)
                for t in range(T):
                    for h in range(H):
                        i = t * H + h
                        made(pe, "p_made", b, i + 1)
                        q = may_fill(pe, b, f"pT{i}")
                        for j in range(T):
                            last = pe.transpose(q[:, col(j)], zbuf[:, h, col(j)], ident[:, :])
                        fill_done(last, f"pT{i}")
                    attend(t)

                made(pe, "ln_done", b, 3)
                transposed(b, "x3T", xb)
                xT_is_split(b, 3)
                rows_times(b, "h3", W_HOP)
                for k in range(3):
                    made(pe, "vk_hi_made", b, 2 * k + 2)
                    made(pe, "vk_lo_made", b, 2 * k + 2)
                    for g in range(2):
                        q = may_fill(pe, b, f"hop{k}_{g}")
                        for i in range(4):
                            t = 4 * g + i
                            for m in range(T):
                                last = three(q[:, col(i)], t_hi[:, m, col(t)], t_lo[:, m, col(t)],
                                             vk_hi[:, m, :], vk_lo[:, m, :], m == 0, m == T - 1)
                        fill_done(last, f"hop{k}_{g}")

        @block.scalar
        def _(act):
            start(act, *ACT_START)
            for g in range(0, NT, T):
                q = slot["QB0"] if g // T % 2 == 0 else slot["QB1"]
                n = min(T, NT - g)
                act.wait_ge(S["w_filled"], g // T + 1)
                act.activation(w_hi[:, 2 + g:2 + g + n, :].rearrange("p a f -> p (a f)"),
                               q[:, 0:n * P], ACT.Copy, scale=WS).then_inc(S["w_hi_made"], 1)
            act.wait_ge(S["w_filled"], 5)
            act.activation(w_seT[:, :], slot["QA"][:, 0:3], ACT.Copy).then_inc(S["vec_made"], 1)
            act.activation(rowc[:, :], slot["QA"][:, HALF:HALF + NR], ACT.Copy)\
                .then_inc(S["vec_made"], 1)
            act.activation(v_lr[:, :], slot["R0"][:, 0:2 * H], ACT.Copy).then_inc(S["vec_made"], 1)
            act.activation(ident16[:, :], ident[:, :], ACT.Copy).then_inc(S["vec_made"], 1)

            def copy(dst, src, name, scale=1.0, use=None):
                ins = act.activation(dst, src, ACT.Copy, scale=scale)
                ins.then_inc(S[name], 1)
                return ins

            def xT_copy(b, use, k):
                q = wait_full(act, b, use)
                made(act, "xT_lo_made", b, k)
                copy(xT[:, :], q[:, :], "xT_made")

            flat = lambda x: x.rearrange("p t d -> p (t d)")

            with act.Fori(0, B) as b:
                xT_copy(b, "x0T", 0)
                for t in range(T):
                    q = wait_full(act, b, f"adj{t}")
                    copy(t_hi[:, :, t * P:(t + 1) * P], q[:, :].rearrange("p (m n) -> p m n", m=T),
                         "t_hi_made", scale=NS)
                q = wait_full(act, b, "y")
                copy(y_hi[:, :, 0:D], q[:, :].rearrange("p (t d) -> p t d", t=T), "y_hi_made",
                     scale=1 / WS)

                xT_copy(b, "x1T", 1)
                q = wait_full(act, b, "conv1")
                act.activation(fa[:, :], q[:, :], ACT.Relu, bias=bn_shift[:, 0:1],
                               scale=bn_scale[:, 0:1]).then_inc(S["fa_made"], 1)
                for i in range(2):
                    q = wait_full(act, b, f"s{i}")
                    act.activation(sT[:, i * HALF:(i + 1) * HALF], q[0:3, :], ACT.Identity,
                                   bias=b_se[:, 0:1]).then_inc(S["s_made"], 1)
                made(act, "c2_made", b, 1)
                act.activation(fa[:, :], fa[:, :], ACT.Relu, bias=bn_shift[:, 1:2])\
                    .then_inc(S["xc_made"], 1)
                made(act, "msg_pre", b, 1)
                act.activation(flat(m_hi[:, :, :]), padv[:, :], ACT.Relu).then_inc(S["m_hi_made"], 1)
                q = wait_full(act, b, "nsq")
                copy(nsq[:, :], q[:, 0:T], "nsq_made")
                made(act, "nsq_made", b, 1)
                for t in range(T):
                    q = wait_full(act, b, f"dist{t}")
                    if t >= 2:
                        made(act, "g_made", b, t - 1)
                    act.activation(expd[:, t % 2, :], q[:, :], ACT.Exp, bias=nsq[:, t:t + 1])\
                        .then_inc(S["exp_made"], 1)
                    made(act, "g_made", b, t + 1)
                    made(act, "g_used", b, max(t - 1, 0))
                    copy(g_hl[:, t % 2, 0, :], gw[:, t % 2, :], "g_hi_made")
                q = wait_full(act, b, "nmp")
                copy(fa[:, :], q[:, :], "xn_made", scale=1 / NS)
                q = wait_full(act, b, "gate_r")
                act.activation(gate_t[:, 0, :], q[:, :], ACT.Tanh, bias=half_b[:, 0:1],
                               scale=0.5 / WS).then_inc(S["tanh_r"], 1)
                q = wait_full(act, b, "gate_z")
                act.activation(gate_t[:, 1, :], q[:, :], ACT.Tanh, bias=half_b[:, 1:2],
                               scale=0.5 / WS).then_inc(S["tanh_z"], 1)
                made(act, "v_made", b, 1)
                act.activation(cand[:, :], hid[:, :], ACT.Tanh, bias=gate_b[:, 0, 2:3],
                               scale=1 / WS).then_inc(S["cand_made"], 1)
                q = wait_full(act, b, "l1r")
                copy(flat(xb[:, :, :]), q[:, :], "r1_nat")

                xT_copy(b, "x2T", 2)
                q = wait_full(act, b, "h2")
                copy(flat(h2[:, :, :]), q[:, :], "h2_made", scale=1 / WS)
                q = wait_full(act, b, "sl")
                copy(flat(sl[:, :, :]), q[:, 0:T * H], "sl_made")
                made(act, "sl_made", b, 1)
                copy(flat(sl4[:, :, :]), flat(sl[:, :, :]), "sl4_made", scale=4.0)
                for h in range(H):
                    q = wait_full(act, b, f"sr_{h}")
                    copy(sr[:, h, :], q[:, :], "sr_made", scale=1 / WS)
                made(act, "sl4_made", b, 1)
                for t in range(T):
                    for h in range(H):
                        i = t * H + h
                        made(act, "z_made", b, i + 1)
                        made(act, "zr_made", b, max(i - 1, 0))
                        act.activation(relu[:, h % 2, :], zbuf[:, h, :], ACT.Relu,
                                       bias=sl4[:, t, h:h + 1], scale=4.0)\
                            .then_inc(S["relu_made"], 1)
                    made(act, "eb", b, t + 1)
                    for h in range(H):
                        i = t * H + h
                        made(act, "zr_made", b, i + 1)
                        act.activation(zbuf[:, h, :], zbuf[:, h, :], ACT.Exp, bias=ebias[:, t, h:h + 1],
                                       scale=SLOPE2, accum_out=rsum[:, t, h:h + 1])\
                            .then_inc(S["p_made"], 1)
                        q = wait_full(act, b, f"pT{i}")
                        if t >= 1:
                            wait_full(act, b, f"att{t - 1}")
                        copy(pT[:, h, :], q[:, :], "pT_made")
                    q = wait_full(act, b, f"att{t}")
                    copy(attT[:, :], q[:, 0:P], "attT_made")

                xT_copy(b, "x3T", 3)
                q = wait_full(act, b, "h3")
                copy(flat(h3[:, :, :]), q[:, :], "h3_made", scale=1 / WS)
                for k in range(3):
                    for g in range(2):
                        if k == 0:
                            made(act, "vk_made", b, g + 1)
                        else:
                            made(act, "hop_read", b, 2 * (k - 1) + g + 1)
                            made(act, "vk_lo_made", b, 2 * (k - 1) + g + 1)
                            wait_full(act, b, f"hop{k - 1}_1")
                        copy(flat(vk_hi[:, 4 * g:4 * g + 4, :]), flat(vk[:, 4 * g:4 * g + 4, :]),
                             "vk_hi_made")

        @block.vector
        def _(dve):
            mul, add, sub, mx = ALU.mult, ALU.add, ALU.subtract, ALU.max

            start(dve, *DVE_START)
            def once(ins, name):
                ins.then_inc(S[name], 1)

            for g in range(0, NT, T):
                q = slot["QB0"] if g // T % 2 == 0 else slot["QB1"]
                n = min(T, NT - g)
                dve.wait_ge(S["w_hi_made"], g // T + 1)
                fl = lambda w: w[:, 2 + g:2 + g + n, :].rearrange("p a f -> p (a f)")
                once(dve.scalar_tensor_tensor(fl(w_lo), q[:, 0:n * P], WS, fl(w_hi), mul, sub),
                     "w_lo_made")
            dve.wait_ge(S["const_loaded"], 16 * N_CONST)
            for j, scale in ((W_SELF, NS), (W_AGG, WS)):
                w0raw = escore[:, 0, j * P:(j + 1) * P]
                once(dve.tensor_scalar(w_hi[:, j, :], w0raw, scale, None, mul), "dve_once")
                dve.wait_ge(S["dve_once"], j + 1)
                once(dve.scalar_tensor_tensor(w_lo[:, j, :], w0raw, scale, w_hi[:, j, :], mul, sub),
                     "w_lo_made")
            dve.wait_ge(S["vec_made"], 4)
            for h in range(H):
                vec = v_lr[:, H + h:H + h + 1].to_broadcast([P, P])
                once(dve.tensor_scalar(vr_hi[:, h, :], vec, WS, None, mul), "dve_once")
                dve.wait_ge(S["dve_once"], 3 + h)
                ins = dve.scalar_tensor_tensor(vr_lo[:, h, :], vec, WS, vr_hi[:, h, :], mul, sub)
            once(ins, "w_lo_made")
            dve.wait_ge(S["bn_ready"], 2)
            once(dve.tensor_tensor(bn_tmp[:, :], bn_tmp[:, :], bn[:, 0, :], mul), "dve_once")
            dve.wait_ge(S["dve_once"], 7)
            once(dve.tensor_scalar(bn_scale[:, :], bn_tmp[:, :], 1 / WS, None, mul), "dve_once")
            once(dve.tensor_tensor(bn_tmp[:, :], bn_tmp[:, :], bn[:, 2, :], mul), "dve_once")
            dve.wait_ge(S["dve_once"], 9)
            once(dve.tensor_tensor(bn_shift[:, :], bn[:, 1, :], bn_tmp[:, :], sub), "dve_once")
            once(dve.tensor_tensor(half_b[:, :], gate_b[:, 0, 0:2], gate_b[:, 1, 0:2], add), "dve_once")
            once(dve.tensor_scalar(hid_b[:, :], gate_b[:, 1, 2:3], WS, None, mul), "dve_once")
            dve.wait_ge(S["dve_once"], 12)
            once(dve.tensor_scalar(half_b[:, :], half_b[:, :], 0.5, None, mul), "dve_once")
            dve.wait_ge(S["dve_once"], 13)

            flat = lambda x: x.rearrange("p t d -> p (t d)")

            def bias_row(at, n=T):
                return rowc[:, at:at + D].unsqueeze(1).to_broadcast([P, n, D])

            def low(dst, src, scale, hi, name, use=None):
                ins = dve.scalar_tensor_tensor(dst, src, scale, hi, mul, sub)
                if use is None:
                    ins.then_inc(S[name], 1)
                return ins

            def split_xT(b, k):
                made(dve, "xT_made", b, k + 1)
                dve.tensor_copy(xT_hi[:, :], xT[:, :]).then_inc(S["xT_hi_made"], 1)
                made(dve, "xT_hi_made", b, k + 1)
                dve.tensor_tensor(xT_lo[:, :], xT[:, :], xT_hi[:, :], sub).then_inc(S["xT_lo_made"], 1)

            def layer_norm(b, k, x):
                for t in range(T):
                    ins = dve.bn_stats(stats[:, t, :], x[:, t, :])
                ins.then_inc(S["ln_stats"], 1)
                wait_apart(dve, (S["ln_stats"], b * 4 + k + 1))
                for t in range(T):
                    ins = dve.bn_aggr(mv[:, t, :], stats[:, t, :])
                ins.then_inc(S["ln_mv"], 1)
                made(dve, "ln_rstd", b, k + 1)
                for t in range(T):
                    ins = dve.tensor_scalar(x[:, t, :], x[:, t, :], mv[:, t, 0:1], rstd[:, t:t + 1],
                                            sub, mul)
                ins.then_inc(S["ln_done"], 1)

            with dve.Fori(0, B) as b:
                split_xT(b, 0)
                for t in range(T):
                    made(dve, "t_hi_made", b, t + 1)
                    q = slot[WHERE[f"adj{t}"][0]]
                    at = slice(t * P, (t + 1) * P)
                    low(t_lo[:, :, at], q[:, :].rearrange("p (m n) -> p m n", m=T), NS,
                        t_hi[:, :, at], "t_lo_made")
                made(dve, "y_hi_made", b, 1)
                low(y_lo[:, :, :], slot["QA"][:, :].rearrange("p (t d) -> p t d", t=T), 1 / WS,
                    y_hi[:, :, 0:D], "y_lo_made")
                for g in range(2):
                    q = wait_full(dve, b, f"l0_{g}")[:, :].rearrange("p (t c) -> p t c", c=256)
                    tiles = slice(4 * g, 4 * g + 4)
                    pre = fa[:, 0:HALF].rearrange("p (t d) -> p t d", t=4)
                    if g:
                        made(dve, "l0_sum", b, g)
                    dve.scalar_tensor_tensor(pre, q[:, :, 0:D], 1 / NS, bias_row(R_B0, 4), mul, add)\
                        .then_inc(S["l0_pre"], 1)
                    dve.tensor_scalar(rinv[:, tiles], q[:, :, D], NS * ROW_EPS, None, add)\
                        .then_inc(S["rs_made"], 1)
                    made(dve, "l0_pre", b, g + 1)
                    dve.scalar_tensor_tensor(xa[:, tiles, :], pre, 0.0, xa[:, tiles, :], mx, add)\
                        .then_inc(S["l0_sum"], 1)
                made(dve, "rs_made", b, 2)
                dve.reciprocal(rinv[:, :], rinv[:, :]).then_inc(S["rinv_made"], 1)
                made(dve, "l0_sum", b, 2)
                layer_norm(b, 0, xa)

                split_xT(b, 1)
                inner = slice(PAD, PAD + N)
                made(dve, "fa_made", b, 1)
                dve.tensor_copy(c_hi[:, inner], fa[:, :]).then_inc(S["c_hi_made"], 1)
                made(dve, "c_hi_made", b, 1)
                dve.tensor_tensor(c_lo[:, inner], fa[:, :], c_hi[:, inner], sub)\
                    .then_inc(S["c_lo_made"], 1)
                made(dve, "s_made", b, 2)
                dve.tensor_scalar(s2T[:, :], sT[:, :], 2.0, None, mul).then_inc(S["s2_made"], 1)
                dve.tensor_tensor(sqT[:, :], sT[:, :], sT[:, :], mul).then_inc(S["sq_made"], 1)
                q = wait_full(dve, b, "conv2")
                made(dve, "c_lo_made", b, 1)
                dve.scalar_tensor_tensor(fa[:, :], q[:, :], bn_scale[:, 1:2], xT[:, :], mul, add)\
                    .then_inc(S["c2_made"], 1)
                made(dve, "xc_made", b, 1)
                dve.tensor_copy(xc_hi[:, :], fa[:, :]).then_inc(S["xc_hi_made"], 1)
                made(dve, "xc_hi_made", b, 1)
                dve.tensor_tensor(xc_lo[:, :], fa[:, :], xc_hi[:, :], sub).then_inc(S["xc_lo_made"], 1)
                q = wait_full(dve, b, "msg")
                dve.scalar_tensor_tensor(padv[:, :].rearrange("p (t d) -> p t d", t=T),
                                         q[:, :].rearrange("p (t d) -> p t d", t=T), 1 / WS,
                                         bias_row(R_BM), mul, add).then_inc(S["msg_pre"], 1)
                made(dve, "m_hi_made", b, 1)
                dve.scalar_tensor_tensor(flat(m_lo[:, :, :]), padv[:, :], 0.0, flat(m_hi[:, :, :]),
                                         mx, sub).then_inc(S["m_lo_made"], 1)
                for t in range(T):
                    q = wait_full(dve, b, f"mask{t}")
                    made(dve, "exp_made", b, t + 1)
                    dve.tensor_tensor(gw[:, t % 2, :], expd[:, t % 2, :], q[:, :], mul)\
                        .then_inc(S["g_made"], 1)
                    made(dve, "g_hi_made", b, t + 1)
                    dve.tensor_tensor(g_hl[:, t % 2, 1, :], gw[:, t % 2, :], g_hl[:, t % 2, 0, :], sub)\
                        .then_inc(S["g_lo_made"], 1)
                made(dve, "xn_made", b, 1)
                dve.tensor_copy(xn_hi[:, :], fa[:, :]).then_inc(S["xn_hi_made"], 1)
                made(dve, "xn_hi_made", b, 1)
                dve.tensor_tensor(xn_lo[:, :], fa[:, :], xn_hi[:, :], sub).then_inc(S["xn_lo_made"], 1)
                q = wait_full(dve, b, "hid_n")
                dve.tensor_scalar(hid[:, :], q[:, :], hid_b[:, 0:1], None, add)\
                    .then_inc(S["hid_made"], 1)
                made(dve, "hid_made", b, 1)
                made(dve, "tanh_r", b, 1)
                dve.scalar_tensor_tensor(hid[:, :], gate_t[:, 0, :], 1.0, hid[:, :], add, mul)\
                    .then_inc(S["u_made"], 1)
                q = wait_full(dve, b, "in_n")
                made(dve, "u_made", b, 1)
                dve.scalar_tensor_tensor(hid[:, :], hid[:, :], 0.5, q[:, :], mul, add)\
                    .then_inc(S["v_made"], 1)
                made(dve, "cand_made", b, 1)
                dve.tensor_tensor(fa[:, :], xT[:, :], cand[:, :], sub).then_inc(S["w_made"], 1)
                made(dve, "w_made", b, 1)
                made(dve, "tanh_z", b, 1)
                dve.scalar_tensor_tensor(fa[:, :], gate_t[:, 1, :], 1.0, fa[:, :], add, mul)\
                    .then_inc(S["w2_made"], 1)
                made(dve, "w2_made", b, 1)
                dve.scalar_tensor_tensor(fa[:, :], fa[:, :], 0.5, cand[:, :], mul, add)\
                    .then_inc(S["o_made"], 1)
                made(dve, "o_made", b, 1)
                dve.tensor_tensor(fa[:, :], fa[:, :], xT[:, :], add).then_inc(S["r1_made"], 1)
                made(dve, "r1_nat", b, 1)
                layer_norm(b, 1, xb)

                split_xT(b, 2)
                dve.tensor_tensor(fa[:, :].rearrange("p (t d) -> p t d", t=T), xb[:, :, :],
                                  bias_row(R_B2), add).then_inc(S["x2b_made"], 1)
                made(dve, "sl_made", b, 1)

                def attention_out(t):
                    if t == 0:
                        made(dve, "x2b_made", b, 1)
                    q = wait_full(dve, b, f"attT{t}")
                    made(dve, "rs_inv", b, t + 1)
                    if t:
                        made(dve, "r2_made", b, t)
                    heads = lambda x: x.rearrange("p (h d) -> p h d", h=H)
                    dve.tensor_tensor(heads(attn[:, :]), heads(q[:, 0:P]),
                                      rsum[:, t, :].unsqueeze(2).to_broadcast([P, H, DH]), mul)\
                        .then_inc(S["att_scaled"], 1)
                    made(dve, "att_scaled", b, t + 1)
                    dve.tensor_tensor(attn[:, :], attn[:, :], fa[:, t * P:(t + 1) * P], add)\
                        .then_inc(S["att_pre"], 1)
                    made(dve, "att_pre", b, t + 1)
                    dve.scalar_tensor_tensor(attn[:, :], attn[:, :], SLOPE2_OUT, attn[:, :], mul, mx)\
                        .then_inc(S["att_leak"], 1)
                    made(dve, "att_leak", b, t + 1)
                    dve.tensor_tensor(xb[:, t, :], xb[:, t, :], attn[:, :], add)\
                        .then_inc(S["r2_made"], 1)

                for t in range(T):
                    e = escore[:, t % 2, :]
                    dve.wait_ge(S[f"e_loaded{t % 2}"], b * (8 * T) + 16 * (t // 2 + 1))
                    if t:
                        made(dve, "e_made", b, t)
                    dve.tensor_scalar(padv[:, :], e, 1e-5, MASKED, ALU.is_le, mul)\
                        .then_inc(S["pad_made"], 1)
                    made(dve, "pad_made", b, t + 1)
                    dve.scalar_tensor_tensor(e, e, rowc[:, R_AW + 2 * DH:NR], padv[:, :], mul, add)\
                        .then_inc(S["e_made"], 1)
                    for h in range(H):
                        i = t * H + h
                        waits = [(S["e_made"], b * T + t + 1)]
                        if t == 0:
                            waits.append((S["sr_made"], b * H + h + 1))
                        else:
                            q, j = WHERE[f"pT{i - H}"]
                            waits.append((filled[q], b * len(USES[q]) + j + 1))
                        wait_apart(dve, *waits)
                        dve.tensor_tensor_reduce(out=zbuf[:, h, :], in0=e, in1=sr[:, h, :], scale=1.0,
                                                 scalar=-3e38, op0=add, op1=mx,
                                                 accum_out=zmax[:, t, h:h + 1])\
                            .then_inc(S["z_made"], 1)
                    made(dve, "z_made", b, H * (t + 1))
                    dve.tensor_tensor(etmp[:, t, :], zmax[:, t, :], sl[:, t, :], add)\
                        .then_inc(S["zsum"], 1)
                    made(dve, "zsum", b, t + 1)
                    dve.scalar_tensor_tensor(etmp[:, t, :], etmp[:, t, :], SLOPE2, etmp[:, t, :], mul,
                                             mx).then_inc(S["leak"], 1)
                    made(dve, "leak", b, t + 1)
                    dve.scalar_tensor_tensor(ebias[:, t, :], sl[:, t, :], SLOPE2, etmp[:, t, :], mul,
                                             sub).then_inc(S["eb"], 1)
                    for h in range(H):
                        i = t * H + h
                        made(dve, "relu_made", b, i + 1)
                        dve.tensor_tensor(zbuf[:, h, :], zbuf[:, h, :], relu[:, h % 2, :], add)\
                            .then_inc(S["zr_made"], 1)
                    made(dve, "p_made", b, H * (t + 1))
                    dve.reciprocal(rsum[:, t, :], rsum[:, t, :]).then_inc(S["rs_inv"], 1)
                    if t:
                        attention_out(t - 1)
                attention_out(T - 1)
                made(dve, "r2_made", b, T)
                layer_norm(b, 2, xb)

                split_xT(b, 3)
                made(dve, "h3_made", b, 1)
                for g in range(2):
                    tiles = slice(4 * g, 4 * g + 4)
                    dve.tensor_scalar(flat(vk[:, tiles, :]), flat(h3[:, tiles, :]),
                                      rowc[:, R_CW + 3:R_CW + 4], None, mul).then_inc(S["vk_made"], 1)

                def split_vk(k, g):
                    tiles = slice(4 * g, 4 * g + 4)
                    made(dve, "vk_hi_made", b, 2 * k + g + 1)
                    dve.tensor_tensor(flat(vk_lo[:, tiles, :]), flat(vk[:, tiles, :]),
                                      flat(vk_hi[:, tiles, :]), sub).then_inc(S["vk_lo_made"], 1)

                split_vk(0, 0)
                split_vk(0, 1)
                for k in range(3):
                    w = rowc[:, R_CW + 2 - k:R_CW + 3 - k]
                    shift, op = (rowc[:, R_CB:R_CB + 1], add) if k == 2 else (None, ALU.bypass)
                    if k:
                        made(dve, "hop_read", b, 2 * k)
                    dve.tensor_scalar(fa[:, :], flat(h3[:, :, :]), w, shift, mul, op)\
                        .then_inc(S["wh_made"], 1)
                    made(dve, "wh_made", b, k + 1)
                    if k == 0:
                        made(dve, "vk_lo_made", b, 2)
                    for g in range(2):
                        q = wait_full(dve, b, f"hop{k}_{g}")
                        for i in range(4):
                            t = 4 * g + i
                            ins = dve.scalar_tensor_tensor(
                                vk[:, t, :], q[:, i * P:(i + 1) * P], rinv[:, t:t + 1],
                                fa[:, t * P:(t + 1) * P], mul, add)
                        ins.then_inc(S["hop_read"], 1)
                        if k < 2:
                            made(dve, "hop_read", b, 2 * k + g + 1)
                            split_vk(k + 1, g)
                made(dve, "hop_read", b, 6)
                dve.scalar_tensor_tensor(flat(vk[:, :, :]), flat(vk[:, :, :]), SLOPE3,
                                         flat(vk[:, :, :]), mul, mx).then_inc(S["out_leak"], 1)
                made(dve, "out_leak", b, 1)
                dve.tensor_tensor(flat(xb[:, :, :]), flat(xb[:, :, :]), flat(vk[:, :, :]), add)\
                    .then_inc(S["r3_made"], 1)
                made(dve, "r3_made", b, 1)
                layer_norm(b, 3, xb)


def kernel(**inputs):
    import numpy as np
    import concourse.bacc as bacc
    from concourse.bass_utils import run_bass_kernel_spmd

    nc = bacc.Bacc("TRN2", target_bir_lowering=False, num_devices=1)
    arrays, aps = {}, {}
    for name, value in inputs.items():
        value = np.ascontiguousarray(value)
        arrays[f"in_{name}"] = value
        aps[name] = nc.dram_tensor(f"in_{name}", value.shape, mybir.dt.from_np(value.dtype),
                                   kind="ExternalInput").ap()
    shape = inputs["x"].shape
    out = nc.dram_tensor("out", shape, mybir.dt.float32, kind="ExternalOutput").ap()
    gnn_stack_kernel(nc, aps, out)
    r = run_bass_kernel_spmd(nc, [arrays], core_ids=[0])
    return r.results[0]["out"]
```

```python
import concourse.bass as bass
from concourse import mybir
from contextlib import ExitStack


def gnn_stack_kernel(nc: bass.Bass, a, out: bass.AP):
    f32 = mybir.dt.float32
    f16 = mybir.dt.float16
    bf16 = mybir.dt.bfloat16
    ALU = mybir.AluOpType
    ACT = mybir.ActivationFunctionType

    B, N, D = a["x"].shape
    P = 128
    T = N // P
    H = 4
    DH = D // H
    TAPS = a["L1_gnn_conv2_w"].shape[2]
    PAD = TAPS // 2
    HALF = 512
    NS = float(N)
    WS = 64.0
    LN_EPS = 1e-5
    BN_EPS = 1e-5
    ROW_EPS = 1e-9
    SLOPE2 = 0.2
    SLOPE2_OUT = 0.5
    SLOPE3 = 0.2
    MASKED = -float(2 ** 55)

    W_SELF, W_AGG = 0, 1
    W_CONV1 = 2
    W_CONV2 = 3
    W_MSG = W_CONV2 + TAPS
    W_IH = W_MSG + 1
    W_HH = W_IH + 6
    W_PROJ = W_HH + 3
    W_HOP = W_PROJ + 1
    NW = W_HOP + 1
    NT = NW - 2

    R_B0, R_BM, R_B2, R_CW, R_CB, R_AW = 0, D, 2 * D, 3 * D, 3 * D + 4, 3 * D + 5
    NR = R_AW + 2 * DH + 1

    PARTS = 3
    NC = a["L1_gnn_w_se"].shape[0]
    PAIRS0 = 2
    KD = 64

    USES = {
        ("QA", "first"): ["x0T"] + [f"adj{t}" for t in range(T)]
                         + ["y", "l0_0", "l0_1", "x1T", "conv1", "conv2", "msg"],
        ("QA", "hops"): ["x3T", "h3"],
        ("QA", "mid"): ["nmp", "gate_r", "hid_n", "l1r", "x2T", "h2", "sr_0", "sr_1", "sr_2", "sr_3"],
        ("QB0", "mid"): ["s"] + [f"dist{t}" for t in range(T)] + ["gate_z"],
        ("QB1", "mid"): ["nsqr"] + [f"mask{t}" for t in range(T)] + ["in_n", "sl"],
        ("QB0", "att"): [f"pT{i}" for i in range(0, T * H, 2)],
        ("QB1", "att"): [f"pT{i}" for i in range(1, T * H, 2)],
        ("R0", "att"): [f"att{t}" for t in range(T)],
        ("R1", "att"): [f"attT{t}" for t in range(T)],
        ("R0", "hops"): [f"hop{k}_0" for k in range(3)],
        ("R1", "hops"): [f"hop{k}_1" for k in range(3)],
    }
    WHERE = {use: (key, j) for key, uses in USES.items() for j, use in enumerate(uses)}

    ctx = ExitStack()
    with ctx:
        def sb(name, shape, dt=f32):
            return ctx.enter_context(nc.sbuf_tensor(name, shape, dt))

        def sem(name):
            return ctx.enter_context(nc.semaphore(name))

        slot = {q: ctx.enter_context(nc.psum_tensor(q, [P, N if q[0] == "Q" else HALF], f32))
                for q in ("QA", "QB0", "QB1", "R0", "R1")}
        filled = {key: sem(f"filled_{key[0]}_{key[1]}") for key in USES}

        ident = sb("ident", [P, P])
        ident16 = sb("ident16", [P, P], f16)
        dist_c = sb("dist_c", [KD, KD + 2 * PARTS + 2])
        w_hi = sb("w_hi", [P, NW, P], f16)
        w_lo = sb("w_lo", [P, NW, P], f16)
        w_seT = sb("w_seT", [P, KD])
        rowc = sb("rowc", [P, NR])
        bn = sb("bn", [P, 4, 2])
        bn_scale = sb("bn_scale", [P, 2])
        bn_shift = sb("bn_shift", [P, 2])
        bn_tmp = sb("bn_tmp", [P, 2])
        minus_half = sb("minus_half", [P, T])
        gate_b = sb("gate_b", [P, 2, 3])
        half_b = sb("half_b", [P, 2])
        hid_b = sb("hid_b", [P, 1])
        b_se = sb("b_se", [KD, 1])
        a_blk = sb("a_blk", [P, 2 * H])
        v_lr = sb("v_lr", [P, 2 * H])
        vr_hi = sb("vr_hi", [P, H, P], f16)
        vr_lo = sb("vr_lo", [P, H, P], f16)

        adj_in = sb("adj_in", [P, 2, N])
        t_hi2 = sb("t_hi", [P, 2, T, N], f16)
        t_lo2 = sb("t_lo", [P, 2, T, N], f16)
        xa = sb("xa", [P, T, D])
        xb2 = sb("xb", [P, 2, T, D])
        xT = sb("xT", [P, N])
        xT_hi = sb("xT_hi", [P, N], f16)
        xT_lo = sb("xT_lo", [P, N], f16)
        x3_hi = sb("x3_hi", [P, N], f16)
        x3_lo = sb("x3_lo", [P, N], f16)
        y_hi = sb("y_hi", [P, T, D + 1], f16)
        y_lo = sb("y_lo", [P, T, D], f16)
        m_hi, m_lo = y_hi[:, :, 0:D], y_lo
        rinv2 = sb("rinv", [P, 2, T])
        stats = sb("stats", [P, T, 6])
        mv = sb("mv", [P, T, 2])
        rstd = sb("rstd", [P, T])
        fa = sb("fa", [P, N])
        c_hi = sb("c_hi", [P, N + 2 * PAD], f16)
        c_lo = sb("c_lo", [P, N + 2 * PAD], f16)
        inner = slice(PAD, PAD + N)
        xc_hi = sb("xc_hi", [P, N], f16)
        xc_lo = sb("xc_lo", [P, N], f16)
        xn_hi, xn_lo = c_hi[:, inner], c_lo[:, inner]
        work = sb("work", [P, 10, N])
        expd, gw = work[:, 0:2, :], work[:, 2:4, :]
        g_hl = work[:, 4:6, :].bitcast(f16).rearrange("p k (h n) -> p k h n", h=2)
        gate_t, hid, cand = work[:, 0:2, :], work[:, 2, :], work[:, 3, :]
        zbuf, relu, pT = work[:, 0:4, :], work[:, 4:6, :], work[:, 6:10, :]
        by_tile = lambda x: x.rearrange("p (t d) -> p t d", t=T)
        h3, vk, wh = by_tile(work[:, 6, :]), by_tile(work[:, 7, :]), work[:, 8, :]
        vk_hl = work[:, 9, :].bitcast(f16).rearrange("p (k t d) -> p k t d", k=2, t=T)
        vk_hi, vk_lo = vk_hl[:, 0, :, :], vk_hl[:, 1, :, :]
        sr = sb("sr", [P, H, N])
        sv, sq = sr[0:KD, 0, :], sr[0:KD, 3, :]
        halves = lambda x: x.bitcast(bf16).rearrange("p (k n) -> p k n", k=2)
        s_p = halves(sr[0:KD, 1, :])
        d_l, d_r = halves(sr[0:KD, 2, :])[:, 0, :], halves(sr[0:KD, 2, :])[:, 1, :]
        d_t = halves(sr[0:KD, 3, :])
        escore = sb("escore", [P, 2, N])
        ones_row = escore[0:1, 0, HALF:HALF + P]
        padv = sb("padv", [P, N])
        rows = padv[0:1, 0:NR]
        h2 = sb("h2", [P, T, D])
        sl = sb("sl", [P, T, H])
        sl4 = sb("sl4", [P, T, H])
        zmax = sb("zmax", [P, T, H])
        ebias = sb("ebias", [P, T, H])
        etmp = sb("etmp", [P, T, H])
        rsum = sb("rsum", [P, T, H])
        attT = sb("attT", [P, P])
        attn = sb("attn", [P, P])

        S = {n: sem(n) for n in (
            "const_loaded pool_const w_filled w_hi_made w_lo_made vec_made bn_ready dve_once apart "
            "adj_loaded0 adj_loaded1 x_loaded e_loaded0 e_loaded1 out_stored xb_free "
            "x0T_hi x0T_lo x1T_f x1T_hi x1T_lo x2T_f x2T_hi x2T_lo x3T_hi x3T_lo "
            "t_hi_made t_lo_made y_hi_made y_lo_made l0_pre l0_sum rs_made rinv_made "
            "conv1_made c_hi_made c_lo_made c2_made xc_made xc_hi_made xc_lo_made msg_pre "
            "m_hi_made m_lo_made s_made sq_made sv_made sp1_made sv1_made sp2_made "
            "sv2_made d_first d_second d_made exp_made g_made g_used g_hi_made g_lo_made "
            "xn_made xn_hi_made xn_lo_made tanh_r tanh_z hid_made u_made v_made cand_made "
            "w_made w2_made o_made r1_made r1_nat h2_made sl_made sl4_made sr_made "
            "pad_made e_made z_made relu_made zr_made zsum leak eb p_made pT_made attT_made "
            "rs_inv att_scaled att_pre att_leak r2_made h3_made vk_made hop_read wh_made "
            "vk_hi_made vk_lo_made out_leak r3_made").split()
            + [f"ln{k}_{n}" for k in range(4) for n in ("stats", "mv", "eps", "rstd", "done")]}

        N_CONST = 34 - 2 + 1 + 2 * PARTS * PARTS
        N_GROUPS = (NT + T - 1) // T
        W_DONE = N_GROUPS + 3

        PER = {"t_hi_made": T, "t_lo_made": T, "rs_made": 2, "l0_pre": 2, "l0_sum": 2,
               "d_first": 2, "d_second": 2, "d_made": 2,
               "exp_made": T, "g_made": T, "g_used": T - 1, "g_hi_made": T, "g_lo_made": T,
               "sr_made": H, "pad_made": T, "e_made": T, "z_made": T * H, "relu_made": T * H,
               "zr_made": T * H, "zsum": T, "leak": T, "eb": T, "p_made": T * H,
               "pT_made": T * H, "attT_made": T, "att_scaled": T, "att_pre": T, "att_leak": T,
               "r2_made": T, "wh_made": 3, "vk_made": 2, "hop_read": 6, "vk_hi_made": 6,
               "vk_lo_made": 6, "rs_inv": T}
        READ_BY = {"x0T": ("x0T_lo", 1), "y": ("y_lo_made", 1), "l0_0": ("rs_made", 1),
                   "l0_1": ("rs_made", 2), "x1T": ("x1T_lo", 1), "conv1": ("conv1_made", 1),
                   "conv2": ("c2_made", 1), "msg": ("msg_pre", 1), "nmp": ("xn_made", 1),
                   "gate_r": ("tanh_r", 1), "hid_n": ("hid_made", 1), "l1r": ("r1_nat", 1),
                   "x2T": ("x2T_lo", 1), "h2": ("h2_made", 1), "x3T": ("x3T_lo", 1),
                   "h3": ("h3_made", 1), "gate_z": ("tanh_z", 1), "in_n": ("v_made", 1),
                   "s": ("s_made", 1), "nsqr": ("sv_made", 1),
                   "sl": ("sl_made", 1)}
        READ_BY |= {f"sr_{h}": ("sr_made", h + 1) for h in range(H)}
        READ_BY |= {f"adj{t}": ("t_lo_made", t + 1) for t in range(T)}
        READ_BY |= {f"dist{t}": ("exp_made", t + 1) for t in range(T)}
        READ_BY |= {f"mask{t}": ("g_made", t + 1) for t in range(T)}
        READ_BY |= {f"pT{i}": ("pT_made", i + 1) for i in range(T * H)}
        READ_BY |= {f"att{t}": ("attT_made", t + 1) for t in range(T)}
        READ_BY |= {f"attT{t}": ("att_scaled", t + 1) for t in range(T)}
        READ_BY |= {f"hop{k}_{g}": ("hop_read", 2 * k + g + 1) for k in range(3) for g in range(2)}
        BEFORE = {("QA", "first"): [("sr_made", 0)], ("QA", "hops"): [("sr_made", H)],
                  ("QA", "mid"): [("msg_pre", 1), ("h3_made", 0)],
                  ("QB0", "mid"): [("pT_made", 0)], ("QB1", "mid"): [("pT_made", 0)],
                  ("QB0", "att"): [("tanh_z", 1)], ("QB1", "att"): [("sl_made", 1)],
                  ("R0", "att"): [("hop_read", 0)], ("R1", "att"): [("hop_read", 0)],
                  ("R0", "hops"): [("attT_made", T)], ("R1", "hops"): [("att_scaled", T)]}

        ACT_START = ("t_hi_made", "h3_made", "pT_made", "sr_made", "x1T_hi")
        DVE_START = ("z_made", "zr_made", "hop_read")
        PE_START = ("g_used",)
        POOL_START = ("xb_free",)
        START_AT_1 = ACT_START + DVE_START + PE_START + POOL_START

        block = ctx.enter_context(nc.Block())

        def wait_apart(eng, *waits):
            for semaphore, value in waits:
                eng.wait_ge(semaphore, value)
            eng.sem_inc(S["apart"], 1)

        def count(name, b, k):
            return b * PER.get(name, 1) + k + (name in START_AT_1)

        def start(eng, *names):
            for name in names:
                assert name in START_AT_1
                eng.sem_inc(S[name], 1)

        def may_fill(eng, b, use):
            key, j = WHERE[use]
            for name, k in [READ_BY[USES[key][j - 1]]] if j else BEFORE[key]:
                eng.wait_ge(S[name], count(name, b, k))
            return slot[key[0]]

        def fill_done(ins, use):
            ins.then_inc(filled[WHERE[use][0]], 1)

        def full_count(b, use):
            key, j = WHERE[use]
            return filled[key], b * len(USES[key]) + j + 1

        def wait_full(eng, b, use):
            eng.wait_ge(*full_count(b, use))
            return slot[WHERE[use][0][0]]

        def made(eng, name, b, k):
            eng.wait_ge(S[name], count(name, b, k))

        x_dram, adj_dram = a["x"], a["adj"]

        def in_order(eng, step):
            def first_part(a, pa, t):
                if t < 2:
                    if t == 0:
                        step("x0T", a, pa)
                    for i in range(T // 2):
                        step("adjacency", a, pa, T // 2 * t + i)
                elif t == 2:
                    step("aggregate_in", a, pa)
                    step("aggregate", a, pa, 0)
                elif t == 3:
                    step("aggregate", a, pa, 1)
                    step("norm0", a, pa)
                elif t == 4:
                    step("x1T", a, pa)
                    step("conv1", a, pa)
                elif t < 7:
                    step("conv2", a, pa, t - 5)
                else:
                    step("message_in", a, pa)

            def cycle(a, b, pa):
                pb = 1 - pa
                for t in range(T):
                    if b is not None:
                        step("scores", b, pb, t)
                    if a is not None:
                        first_part(a, pa, t)
                    if b is not None:
                        if t:
                            step("attend", b, pb, t - 1)
                        step("probs", b, pb, t)
                        if t:
                            step("turn", b, pb, t - 1)
                if b is not None:
                    step("attend", b, pb, T - 1)
                    step("turn", b, pb, T - 1)
                    step("norm2", b, pb)
                if a is not None:
                    step("s_rows", a, pa)
                if b is not None:
                    if a is not None:
                        step("after_first", a, pa)
                    step("x3T", b, pb)
                    step("h3", b, pb)
                hops = [(k, g) for k in range(3) for g in range(2)]

                def hop():
                    if b is not None:
                        step("hop", b, pb, *hops.pop(0))

                if a is not None:
                    step("distance", a, pa, 0)
                    for t in range(T):
                        if t + 1 < T:
                            step("distance", a, pa, t + 1)
                        step("message", a, pa, t)
                        if t == 3:
                            hop()
                    hop()
                    step("gates", a, pa)
                    hop()
                    step("candidate", a, pa)
                    hop()
                    step("norm1", a, pa)
                    hop()
                    step("x2T", a, pa)
                    hop()
                    step("project", a, pa)
                while hops and b is not None:
                    hop()
                if b is not None:
                    step("finish", b, pb)

            cycle(0, None, 0)
            with eng.Fori(0, B // 2 - 1) as i:
                cycle(i * 2 + 1, i * 2, 1)
                cycle(i * 2 + 2, i * 2 + 1, 0)
            cycle(B - 1, B - 2, 1)
            cycle(None, B - 1, 0)

        def run(eng, **steps):
            def step(name, *args):
                if name in steps:
                    steps[name](*args)
            in_order(eng, step)

        @block.sync
        def _(sp):
            raw = work[:, 0:4, :].rearrange("p a n -> p (a n)")
            w0raw = escore[:, 0, 0:2 * P].rearrange("p (a f) -> p a f", a=2)

            def load(dst, src, to="const_loaded"):
                sp.dma_start(dst, src).then_inc(S[to], 16)

            o = P * (1 + TAPS)
            load(raw[:, 0:P], a["L1_gnn_conv1_w"].rearrange("o c k -> o (c k)"))
            load(raw[:, P:o], a["L1_gnn_conv2_w"].rearrange("o c k -> o (c k)"))
            load(raw[:, o:o + P], a["L1_gnn_w_msg"])
            load(raw[:, o + P:o + 7 * P].rearrange("p (g k) -> p g k", g=3),
                 a["L1_gnn_w_ih"].rearrange("(g p) k -> p g k", p=P))
            load(raw[:, o + 7 * P:o + 10 * P].rearrange("p (g k) -> p g k", g=3),
                 a["L1_gnn_w_hh"].rearrange("(g p) k -> p g k", p=P))
            load(raw[:, o + 10 * P:o + 11 * P], a["L2_gnn_W_proj"])
            load(raw[:, o + 11 * P:o + 12 * P], a["L3_gnn_W"])
            load(w0raw, a["L0_gnn_weight"].rearrange("(a p) f -> p a f", p=P))
            for off, name in ((R_B0, "L0_gnn_bias"), (R_BM, "L1_gnn_b_msg"), (R_B2, "L2_gnn_bias"),
                              (R_CW, "L3_gnn_conv_w"), (R_CB, "L3_gnn_conv_b")):
                load(rows[0:1, off:off + a[name].shape[0]], a[name].rearrange("(a n) -> a n", a=1))
            load(rows[0:1, R_AW:NR], a["L2_gnn_a_w"])
            for i, kind in enumerate("gbmv"):
                for j in (1, 2):
                    load(bn[:, i, j - 1:j], a[f"L1_gnn_bn{j}_{kind}"].rearrange("(p a) -> p a", a=1))
            with nc.allow_non_contiguous_dma(reason="768 bias values, once"):
                load(gate_b[:, 0, :], a["L1_gnn_b_ih"].rearrange("(g p) -> p g", p=P))
                load(gate_b[:, 1, :], a["L1_gnn_b_hh"].rearrange("(g p) -> p g", p=P))
            load(dist_c[:, :], a["dist_c"])
            sp.wait_ge(S["pool_const"], 3)
            for i in range(PARTS * PARTS):
                at = slice(PAIRS0 + i * NC, PAIRS0 + (i + 1) * NC)
                load(escore[at, 1, 0:P], a["L1_gnn_w_se"])
                load(b_se[at, :], a["L1_gnn_b_se"].rearrange("(p a) -> p a", a=1))
            for h in range(H):
                for side in range(2):
                    load(a_blk[h * DH:(h + 1) * DH, side * H + h:side * H + h + 1],
                         a["L2_gnn_a_w"][0:1, side * DH:(side + 1) * DH].rearrange("a p -> p a"))

            def row_tile(b, t):
                return adj_dram[bass.ds(b, 1), t * P:(t + 1) * P, :].rearrange("a p m -> p (a m)")

            def load_x(a, pa):
                made(sp, "x1T_hi", a, 0)
                sp.dma_start(xa[:, :, :], x_dram[bass.ds(a, 1), :, :].rearrange(
                    "a (t p) d -> p (a t) d", p=P)).then_inc(S["x_loaded"], 16)

            def load_adj(a, pa, t):
                made(sp, "t_hi_made", a, max(t - 1, 0))
                sp.dma_start(adj_in[:, t % 2, :], row_tile(a, t)).then_inc(S[f"adj_loaded{t % 2}"], 16)

            def load_e(b, pb, t):
                if t == 0:
                    sp.wait_ge(S["w_lo_made"], W_DONE)
                made(sp, "z_made", b, H * max(t - 1, 0))
                sp.dma_start(escore[:, t % 2, :], row_tile(b, t)).then_inc(S[f"e_loaded{t % 2}"], 16)

            run(sp, x0T=load_x, adjacency=load_adj, scores=load_e)
            sp.wait_ge(S["out_stored"], 16 * B)

        @block.gpsimd
        def _(pool):
            for tile, value in ((a_blk[:, :], 0.0), (escore[0:KD, 1, 0:P], 0.0), (b_se[:, :], 0.0),
                                (ident[:, :], 0.0), (ones_row, 1.0), (minus_half[:, :], -0.5),
                                (c_hi[:, :], 0.0), (c_lo[:, :], 0.0), (y_hi[:, :, D:D + 1], 1.0)):
                pool.memset(tile, value).then_inc(S["pool_const"], 1)
            pool.wait_ge(S["pool_const"], 4)
            pool.affine_select(out=ident[:, :], in_=ident[:, :], compare_op=ALU.not_equal, fill=1.0,
                               base=0, pattern=[[-1, P]], channel_multiplier=1)\
                .then_inc(S["pool_const"], 1)
            for name in POOL_START:
                pool.sem_inc(S[name], 1)
            pool.wait_ge(S["const_loaded"], 16 * N_CONST)
            pool.wait_ge(S["pool_const"], 6)
            pool.tensor_scalar(bn_tmp[:, :], bn[:, 3, :], BN_EPS, None, ALU.add)\
                .then_inc(S["bn_ready"], 1)
            pool.wait_ge(S["bn_ready"], 1)
            pool.tensor_tensor(bn_tmp[:, :], bn_tmp[:, :], minus_half[:, 0:2], ALU.pow)\
                .then_inc(S["bn_ready"], 1)

            def inv_std(k):
                def norm(b, p):
                    wait_apart(pool, (S[f"ln{k}_mv"], count(f"ln{k}_mv", b, 1)))
                    pool.tensor_scalar(rstd[:, :], mv[:, :, 1], LN_EPS, None, ALU.add)\
                        .then_inc(S[f"ln{k}_eps"], 1)
                    made(pool, f"ln{k}_eps", b, 1)
                    pool.tensor_tensor(rstd[:, :], rstd[:, :], minus_half[:, :], ALU.pow)\
                        .then_inc(S[f"ln{k}_rstd"], 1)
                return norm

            def finish(b, p):
                inv_std(3)(b, p)
                made(pool, "ln3_done", b, 1)
                pool.dma_start(out[bass.ds(b, 1), :, :].rearrange("a (t p) d -> p (a t) d", p=P),
                               xb2[:, p, :, :]).then_inc(S["out_stored"], 16)
                pool.wait_ge(S["out_stored"], b * 16 + 16)
                pool.sem_inc(S["xb_free"], 1)

            run(pool, norm0=inv_std(0), norm1=inv_std(1), norm2=inv_std(2), finish=finish)

        @block.tensor
        def _(pe):
            raw = work[:, 0:4, :].rearrange("p a n -> p (a n)")
            start(pe, *PE_START)

            def mm(o, lhsT, rhs, start, stop):
                return pe.matmul(o, lhsT, rhs, start=start, stop=stop)

            def three(o, l_hi, l_lo, r_hi, r_lo, start=True, stop=True):
                mm(o, l_hi, r_hi, start, False)
                mm(o, l_hi, r_lo, False, False)
                return mm(o, l_lo, r_hi, False, stop)

            def col(t):
                return slice(t * P, (t + 1) * P)

            def half(i):
                return slice(i * HALF, (i + 1) * HALF)

            pe.wait_ge(S["const_loaded"], 16 * N_CONST)
            pe.wait_ge(S["pool_const"], 10)
            for g in range(0, NT, T):
                q = slot["QB0"] if g // T % 2 == 0 else slot["QB1"]
                if g >= 2 * T:
                    pe.wait_ge(S["w_lo_made"], g // T - 1)
                for i in range(g, min(g + T, NT)):
                    if 1 <= i <= TAPS:
                        src = raw[:, P:P * (1 + TAPS)].rearrange("p (c k) -> p k c", k=TAPS)[:, i - 1, :]
                    else:
                        src = raw[:, col(i)]
                    last = pe.transpose(q[:, col(i - g)], src, ident[:, :])
                last.then_inc(S["w_filled"], 1)
            pe.transpose(slot["QA"][:, 0:KD], escore[0:KD, 1, 0:P], ident[0:KD, 0:KD])
            mm(slot["QA"][:, HALF:HALF + NR], ones_row, rows, True, True)
            proj = raw[:, col(NT - 2)]
            mm(slot["R0"][:, 0:2 * H], proj, a_blk[:, :], True, True).then_inc(S["w_filled"], 1)
            pe.wait_ge(S["vec_made"], 4)
            pe.wait_ge(S["w_lo_made"], W_DONE)

            def transposed(b, use, src):
                q = may_fill(pe, b, use)
                for t in range(T):
                    last = pe.transpose(q[:, col(t)], src[:, t, :], ident[:, :])
                fill_done(last, use)

            def rows_times(b, use, w, x_hi=xT_hi, x_lo=xT_lo):
                q = may_fill(pe, b, use)
                for t in range(T):
                    last = three(q[:, col(t)], x_hi[:, col(t)], x_lo[:, col(t)],
                                 w_hi[:, w, :], w_lo[:, w, :])
                fill_done(last, use)

            def both(b, *names):
                for name in names:
                    made(pe, name, b, PER.get(name, 1))

            def x0T(a, pa):
                pe.wait_ge(S["x_loaded"], a * 16 + 16)
                transposed(a, "x0T", xa)

            def adjacency(a, pa, t):
                pe.wait_ge(S[f"adj_loaded{t % 2}"], a * (8 * T) + 16 * (t // 2 + 1))
                q = may_fill(pe, a, f"adj{t}")
                for m in range(T):
                    last = pe.transpose(q[:, col(m)], adj_in[:, t % 2, col(m)], ident[:, :])
                fill_done(last, f"adj{t}")

            def aggregate_in(a, pa):
                both(a, "x0T_hi", "x0T_lo")
                rows_times(a, "y", W_AGG)

            def aggregate(a, pa, g):
                if g == 0:
                    both(a, "y_hi_made", "y_lo_made", "t_hi_made", "t_lo_made")
                t_hi, t_lo = t_hi2[:, pa, :, :], t_lo2[:, pa, :, :]
                q = may_fill(pe, a, f"l0_{g}")
                for i in range(4):
                    t = 4 * g + i
                    o = q[:, 256 * i:256 * i + D + 1]
                    for m in range(T):
                        mm(o, t_hi[:, m, col(t)], y_hi[:, m, :], m == 0, False)
                        mm(o[:, 0:D], t_hi[:, m, col(t)], y_lo[:, m, :], False, False)
                        mm(o, t_lo[:, m, col(t)], y_hi[:, m, :], False, False)
                    last = three(o[:, 0:D], xT_hi[:, col(t)], xT_lo[:, col(t)],
                                 w_hi[:, W_SELF, :], w_lo[:, W_SELF, :], start=False)
                fill_done(last, f"l0_{g}")

            def x1T(a, pa):
                both(a, "ln0_done")
                transposed(a, "x1T", xa)

            def conv1(a, pa):
                both(a, "x1T_hi", "x1T_lo")
                q = may_fill(pe, a, "conv1")
                for i in range(2):
                    last = three(q[:, half(i)], w_hi[:, W_CONV1, :], w_lo[:, W_CONV1, :],
                                 xT_hi[:, half(i)], xT_lo[:, half(i)])
                fill_done(last, "conv1")

            def conv2(a, pa, i):
                if i == 0:
                    both(a, "c_hi_made", "c_lo_made")
                    may_fill(pe, a, "conv2")
                for k in range(TAPS):
                    at = slice(i * HALF + k, i * HALF + k + HALF)
                    last = three(slot["QA"][:, half(i)], w_hi[:, W_CONV2 + k, :],
                                 w_lo[:, W_CONV2 + k, :], c_hi[:, at], c_lo[:, at],
                                 start=k == 0, stop=k == TAPS - 1)
                if i == 1:
                    fill_done(last, "conv2")

            def message_in(a, pa):
                rows_times(a, "msg", W_MSG)

            def s_rows(a, pa):
                both(a, "x1T_f")
                q = may_fill(pe, a, "s")
                for i in range(2):
                    last = mm(q[0:KD, half(i)], w_seT[:, :], xT[:, half(i)], True, True)
                fill_done(last, "s")
                both(a, "sq_made")
                q = may_fill(pe, a, "nsqr")
                pe.sem_inc(S["apart"], 1)
                for i in range(2):
                    last = mm(q[0:KD, half(i)], dist_c[:, 0:KD], sq[:, half(i)], True, True)
                fill_done(last, "nsqr")

            def distance(a, pa, t):
                if t == 0:
                    both(a, "d_made")
                q = may_fill(pe, a, f"dist{t}")
                for i in range(2):
                    last = mm(q[:, half(i)], d_l[:, col(t)], d_r[:, half(i)], True, True)
                fill_done(last, f"dist{t}")
                q = may_fill(pe, a, f"mask{t}")
                for i in range(2):
                    mm(q[:, half(i)], ident16[:, :], t_hi2[:, pa, t, half(i)], True, False)
                    last = mm(q[:, half(i)], ident16[:, :], t_lo2[:, pa, t, half(i)], False, True)
                fill_done(last, f"mask{t}")

            def message(a, pa, t):
                if t == 0:
                    both(a, "m_hi_made", "m_lo_made")
                    may_fill(pe, a, "nmp")
                made(pe, "g_hi_made", a, t + 1)
                made(pe, "g_lo_made", a, t + 1)
                for i in range(2):
                    last = three(slot["QA"][:, half(i)], m_hi[:, t, :], m_lo[:, t, :],
                                 g_hl[:, t % 2, 0, half(i)], g_hl[:, t % 2, 1, half(i)],
                                 start=t == 0, stop=t == T - 1)
                if t < T - 1:
                    last.then_inc(S["g_used"], 1)
                else:
                    fill_done(last, "nmp")

            def gate(b, use, blocks):
                q = may_fill(pe, b, use)
                for i in range(2):
                    for j, (w, r_hi, r_lo) in enumerate(blocks):
                        last = three(q[:, half(i)], w_hi[:, w, :], w_lo[:, w, :],
                                     r_hi[:, half(i)], r_lo[:, half(i)],
                                     start=j == 0, stop=j == len(blocks) - 1)
                fill_done(last, use)

            def gates(a, pa):
                both(a, "xc_hi_made", "xc_lo_made", "xn_hi_made", "xn_lo_made")
                gate(a, "gate_r", [(W_IH, xc_hi, xc_lo), (W_HH, xT_hi, xT_lo), (W_IH + 1, xn_hi, xn_lo)])
                gate(a, "hid_n", [(W_HH + 2, xT_hi, xT_lo)])
                gate(a, "in_n", [(W_IH + 4, xc_hi, xc_lo), (W_IH + 5, xn_hi, xn_lo)])
                gate(a, "gate_z", [(W_IH + 2, xc_hi, xc_lo), (W_IH + 3, xn_hi, xn_lo),
                                   (W_HH + 1, xT_hi, xT_lo)])

            def norm1(a, pa):
                both(a, "r1_made")
                q = may_fill(pe, a, "l1r")
                for t in range(T):
                    last = pe.transpose(q[:, col(t)], fa[:, col(t)], ident[:, :])
                fill_done(last, "l1r")

            def x2T(a, pa):
                both(a, "ln1_done")
                transposed(a, "x2T", xb2[:, pa, :, :])

            def project(a, pa):
                both(a, "x2T_hi", "x2T_lo")
                rows_times(a, "h2", W_PROJ)
                q = may_fill(pe, a, "sl")
                for t in range(T):
                    last = mm(q[:, H * t:H * t + H], xT[:, col(t)], v_lr[:, 0:H], True, True)
                fill_done(last, "sl")
                for h in range(H):
                    q = may_fill(pe, a, f"sr_{h}")
                    for i in range(2):
                        last = three(q[:, half(i)], vr_hi[:, h, :], vr_lo[:, h, :],
                                     xT_hi[:, half(i)], xT_lo[:, half(i)])
                    fill_done(last, f"sr_{h}")

            def probs(b, pb, t):
                for h in range(H):
                    i = t * H + h
                    made(pe, "p_made", b, i + 1)
                    q = may_fill(pe, b, f"pT{i}")
                    for j in range(T):
                        last = pe.transpose(q[:, col(j)], zbuf[:, h, col(j)], ident[:, :])
                    fill_done(last, f"pT{i}")

            def attend(b, pb, t):
                made(pe, "pT_made", b, H * (t + 1))
                if t == 0:
                    both(b, "h2_made")
                q = may_fill(pe, b, f"att{t}")
                for j in range(T):
                    for h in range(H):
                        last = mm(q[h * DH:(h + 1) * DH, 0:P], h2[:, j, h * DH:(h + 1) * DH],
                                  pT[:, h, col(j)], j == 0, j == T - 1)
                fill_done(last, f"att{t}")

            def turn(b, pb, t):
                made(pe, "attT_made", b, t + 1)
                q = may_fill(pe, b, f"attT{t}")
                fill_done(pe.transpose(q[:, 0:P], attT[:, :], ident[:, :]), f"attT{t}")

            def after_first(a, pa):
                made(pe, "msg_pre", a, 1)

            def x3T(b, pb):
                both(b, "ln2_done")
                transposed(b, "x3T", xb2[:, pb, :, :])

            def h3_(b, pb):
                both(b, "x3T_hi", "x3T_lo")
                rows_times(b, "h3", W_HOP, x3_hi, x3_lo)

            def hop(b, pb, k, g):
                t_hi, t_lo = t_hi2[:, pb, :, :], t_lo2[:, pb, :, :]
                made(pe, "vk_hi_made", b, 2 * k + 2)
                made(pe, "vk_lo_made", b, 2 * k + 2)
                q = may_fill(pe, b, f"hop{k}_{g}")
                for i in range(4):
                    t = 4 * g + i
                    for m in range(T):
                        last = three(q[:, col(i)], t_hi[:, m, col(t)], t_lo[:, m, col(t)],
                                     vk_hi[:, m, :], vk_lo[:, m, :], m == 0, m == T - 1)
                fill_done(last, f"hop{k}_{g}")

            run(pe, x0T=x0T, adjacency=adjacency, aggregate_in=aggregate_in, aggregate=aggregate,
                x1T=x1T, conv1=conv1, conv2=conv2, message_in=message_in, s_rows=s_rows,
                distance=distance, message=message, gates=gates, norm1=norm1, x2T=x2T,
                project=project, probs=probs, attend=attend, turn=turn, after_first=after_first, x3T=x3T,
                h3=h3_, hop=hop)

        @block.scalar
        def _(act):
            start(act, *ACT_START)
            for g in range(0, NT, T):
                q = slot["QB0"] if g // T % 2 == 0 else slot["QB1"]
                n = min(T, NT - g)
                act.wait_ge(S["w_filled"], g // T + 1)
                act.activation(w_hi[:, 2 + g:2 + g + n, :].rearrange("p a f -> p (a f)"),
                               q[:, 0:n * P], ACT.Copy, scale=WS).then_inc(S["w_hi_made"], 1)
            act.wait_ge(S["w_filled"], N_GROUPS + 1)
            act.activation(w_seT[:, :], slot["QA"][:, 0:KD], ACT.Copy).then_inc(S["vec_made"], 1)
            act.activation(rowc[:, :], slot["QA"][:, HALF:HALF + NR], ACT.Copy)\
                .then_inc(S["vec_made"], 1)
            act.activation(v_lr[:, :], slot["R0"][:, 0:2 * H], ACT.Copy).then_inc(S["vec_made"], 1)
            act.activation(ident16[:, :], ident[:, :], ACT.Copy).then_inc(S["vec_made"], 1)

            def copy(dst, src, name, scale=1.0):
                act.activation(dst, src, ACT.Copy, scale=scale).then_inc(S[name], 1)

            flat = lambda x: x.rearrange("p t d -> p (t d)")

            def halves_of(b, use, hi, f=None):
                q = wait_full(act, b, use)
                if f is not None:
                    copy(f[:, :], q[:, :], f"{use}_f")
                copy(hi[:, :], q[:, :], f"{use}_hi")

            def x0T(a, pa):
                halves_of(a, "x0T", xT_hi)

            def adjacency(a, pa, t):
                q = wait_full(act, a, f"adj{t}")
                copy(t_hi2[:, pa, :, t * P:(t + 1) * P], q[:, :].rearrange("p (m n) -> p m n", m=T),
                     "t_hi_made", scale=NS)

            def aggregate_in(a, pa):
                q = wait_full(act, a, "y")
                copy(y_hi[:, :, 0:D], by_tile(q[:, :]), "y_hi_made", scale=1 / WS)

            def x1T(a, pa):
                halves_of(a, "x1T", xT_hi, xT)

            def conv1(a, pa):
                q = wait_full(act, a, "conv1")
                act.activation(fa[:, :], q[:, :], ACT.Relu, bias=bn_shift[:, 0:1],
                               scale=bn_scale[:, 0:1]).then_inc(S["conv1_made"], 1)
                made(act, "conv1_made", a, 1)
                copy(c_hi[:, inner], fa[:, :], "c_hi_made")

            def conv2(a, pa, i):
                if i == 1:
                    made(act, "c2_made", a, 1)
                    act.activation(fa[:, :], fa[:, :], ACT.Relu, bias=bn_shift[:, 1:2])\
                        .then_inc(S["xc_made"], 1)
                    made(act, "xc_made", a, 1)
                    copy(xc_hi[:, :], fa[:, :], "xc_hi_made")

            def message_in(a, pa):
                made(act, "msg_pre", a, 1)
                act.activation(m_hi, by_tile(fa[:, :]), ACT.Relu).then_inc(S["m_hi_made"], 1)

            def s_rows(a, pa):
                q = wait_full(act, a, "s")
                act.activation(sv, q[0:KD, :], ACT.Identity, bias=b_se[:, 0:1])\
                    .then_inc(S["s_made"], 1)

            def message(a, pa, t):
                q = wait_full(act, a, f"dist{t}")
                if t >= 2:
                    made(act, "g_made", a, t - 1)
                act.activation(expd[:, t % 2, :], q[:, :], ACT.Exp)\
                    .then_inc(S["exp_made"], 1)
                made(act, "g_made", a, t + 1)
                made(act, "g_used", a, max(t - 1, 0))
                copy(g_hl[:, t % 2, 0, :], gw[:, t % 2, :], "g_hi_made")

            def gates(a, pa):
                q = wait_full(act, a, "nmp")
                copy(fa[:, :], q[:, :], "xn_made", scale=1 / NS)
                made(act, "xn_made", a, 1)
                copy(xn_hi, fa[:, :], "xn_hi_made")
                q = wait_full(act, a, "gate_r")
                act.activation(gate_t[:, 0, :], q[:, :], ACT.Tanh, bias=half_b[:, 0:1],
                               scale=0.5 / WS).then_inc(S["tanh_r"], 1)

            def candidate(a, pa):
                q = wait_full(act, a, "gate_z")
                act.activation(gate_t[:, 1, :], q[:, :], ACT.Tanh, bias=half_b[:, 1:2],
                               scale=0.5 / WS).then_inc(S["tanh_z"], 1)
                made(act, "v_made", a, 1)
                act.activation(cand, hid, ACT.Tanh, bias=gate_b[:, 0, 2:3],
                               scale=1 / WS).then_inc(S["cand_made"], 1)

            def norm1(a, pa):
                q = wait_full(act, a, "l1r")
                if not isinstance(a, int) or a > 0:
                    made(act, "xb_free", a - 1, 0)
                copy(flat(xb2[:, pa, :, :]), q[:, :], "r1_nat")

            def x2T(a, pa):
                halves_of(a, "x2T", xT_hi, xT)

            def project(a, pa):
                q = wait_full(act, a, "sl")
                copy(flat(sl[:, :, :]), q[:, 0:T * H], "sl_made")
                made(act, "sl_made", a, 1)
                copy(flat(sl4[:, :, :]), flat(sl[:, :, :]), "sl4_made", scale=4.0)
                for h in range(H):
                    q = wait_full(act, a, f"sr_{h}")
                    copy(sr[:, h, :], q[:, :], "sr_made", scale=1 / WS)

            def scores(b, pb, t):
                for h in range(H):
                    i = t * H + h
                    if i == 0:
                        made(act, "sl4_made", b, 1)
                    made(act, "z_made", b, i + 1)
                    made(act, "zr_made", b, max(i - 1, 0))
                    act.activation(relu[:, h % 2, :], zbuf[:, h, :], ACT.Relu,
                                   bias=sl4[:, t, h:h + 1], scale=4.0)\
                        .then_inc(S["relu_made"], 1)

            def probs(b, pb, t):
                def to_sbuf(h):
                    q = wait_full(act, b, f"pT{t * H + h}")
                    if t >= 1:
                        wait_full(act, b, f"att{t - 1}")
                    copy(pT[:, h, :], q[:, :], "pT_made")

                made(act, "eb", b, t + 1)
                for h in range(H):
                    made(act, "zr_made", b, t * H + h + 1)
                    act.activation(zbuf[:, h, :], zbuf[:, h, :], ACT.Exp, bias=ebias[:, t, h:h + 1],
                                   scale=SLOPE2, accum_out=rsum[:, t, h:h + 1])\
                        .then_inc(S["p_made"], 1)
                    if h:
                        to_sbuf(h - 1)
                to_sbuf(H - 1)

            def attend(b, pb, t):
                q = wait_full(act, b, f"att{t}")
                copy(attT[:, :], q[:, 0:P], "attT_made")

            def x3T(b, pb):
                halves_of(b, "x3T", x3_hi)

            def h3_(b, pb):
                q = wait_full(act, b, "h3")
                copy(flat(h3), q[:, :], "h3_made", scale=1 / WS)
                for g in range(2):
                    made(act, "vk_made", b, g + 1)
                    copy(flat(vk_hi[:, 4 * g:4 * g + 4, :]), flat(vk[:, 4 * g:4 * g + 4, :]),
                         "vk_hi_made")

            def hop(b, pb, k, g):
                if k < 2 and g == 1:
                    for g in range(2):
                        made(act, "hop_read", b, 2 * k + g + 1)
                        wait_full(act, b, f"hop{k}_1")
                        copy(flat(vk_hi[:, 4 * g:4 * g + 4, :]), flat(vk[:, 4 * g:4 * g + 4, :]),
                             "vk_hi_made")

            run(act, x0T=x0T, adjacency=adjacency, aggregate_in=aggregate_in, x1T=x1T, conv1=conv1,
                conv2=conv2, message_in=message_in, s_rows=s_rows, message=message, gates=gates,
                candidate=candidate, norm1=norm1, x2T=x2T, project=project, scores=scores,
                probs=probs, attend=attend, x3T=x3T, h3=h3_, hop=hop)

        @block.vector
        def _(dve):
            mul, add, sub, mx = ALU.mult, ALU.add, ALU.subtract, ALU.max
            start(dve, *DVE_START)

            def once(ins, name):
                ins.then_inc(S[name], 1)

            for g in range(0, NT, T):
                q = slot["QB0"] if g // T % 2 == 0 else slot["QB1"]
                n = min(T, NT - g)
                dve.wait_ge(S["w_hi_made"], g // T + 1)
                fl = lambda w: w[:, 2 + g:2 + g + n, :].rearrange("p a f -> p (a f)")
                once(dve.scalar_tensor_tensor(fl(w_lo), q[:, 0:n * P], WS, fl(w_hi), mul, sub),
                     "w_lo_made")
            dve.wait_ge(S["const_loaded"], 16 * N_CONST)
            for j, scale in ((W_SELF, NS), (W_AGG, WS)):
                w0raw = escore[:, 0, j * P:(j + 1) * P]
                once(dve.tensor_scalar(w_hi[:, j, :], w0raw, scale, None, mul), "dve_once")
                dve.wait_ge(S["dve_once"], j + 1)
                once(dve.scalar_tensor_tensor(w_lo[:, j, :], w0raw, scale, w_hi[:, j, :], mul, sub),
                     "w_lo_made")
            dve.wait_ge(S["vec_made"], 4)
            for h in range(H):
                vec = v_lr[:, H + h:H + h + 1].to_broadcast([P, P])
                once(dve.tensor_scalar(vr_hi[:, h, :], vec, WS, None, mul), "dve_once")
                dve.wait_ge(S["dve_once"], 3 + h)
                ins = dve.scalar_tensor_tensor(vr_lo[:, h, :], vec, WS, vr_hi[:, h, :], mul, sub)
            once(ins, "w_lo_made")
            dve.wait_ge(S["bn_ready"], 2)
            once(dve.tensor_tensor(bn_tmp[:, :], bn_tmp[:, :], bn[:, 0, :], mul), "dve_once")
            dve.wait_ge(S["dve_once"], 7)
            once(dve.tensor_scalar(bn_scale[:, :], bn_tmp[:, :], 1 / WS, None, mul), "dve_once")
            once(dve.tensor_tensor(bn_tmp[:, :], bn_tmp[:, :], bn[:, 2, :], mul), "dve_once")
            dve.wait_ge(S["dve_once"], 9)
            once(dve.tensor_tensor(bn_shift[:, :], bn[:, 1, :], bn_tmp[:, :], sub), "dve_once")
            once(dve.tensor_tensor(half_b[:, :], gate_b[:, 0, 0:2], gate_b[:, 1, 0:2], add), "dve_once")
            once(dve.tensor_scalar(hid_b[:, :], gate_b[:, 1, 2:3], WS, None, mul), "dve_once")
            dve.wait_ge(S["dve_once"], 12)
            once(dve.tensor_scalar(half_b[:, :], half_b[:, :], 0.5, None, mul), "dve_once")
            dve.wait_ge(S["dve_once"], 13)

            flat = lambda x: x.rearrange("p t d -> p (t d)")

            def bias_row(at, n=T):
                return rowc[:, at:at + D].unsqueeze(1).to_broadcast([P, n, D])

            def low(dst, src, scale, hi, name):
                dve.scalar_tensor_tensor(dst, src, scale, hi, mul, sub).then_inc(S[name], 1)

            def minus(dst, x, y, name):
                dve.tensor_tensor(dst, x, y, sub).then_inc(S[name], 1)

            def low_of(b, use, hi, lo):
                made(dve, f"{use}_hi", b, 1)
                minus(lo[:, :], slot["QA"][:, :], hi[:, :], f"{use}_lo")

            def layer_norm(b, k, x):
                for t in range(T):
                    ins = dve.bn_stats(stats[:, t, :], x[:, t, :])
                ins.then_inc(S[f"ln{k}_stats"], 1)
                wait_apart(dve, (S[f"ln{k}_stats"], count(f"ln{k}_stats", b, 1)))
                for t in range(T):
                    ins = dve.bn_aggr(mv[:, t, :], stats[:, t, :])
                ins.then_inc(S[f"ln{k}_mv"], 1)
                made(dve, f"ln{k}_rstd", b, 1)
                for t in range(T):
                    ins = dve.tensor_scalar(x[:, t, :], x[:, t, :], mv[:, t, 0:1], rstd[:, t:t + 1],
                                            sub, mul)
                ins.then_inc(S[f"ln{k}_done"], 1)

            def x0T(a, pa):
                low_of(a, "x0T", xT_hi, xT_lo)

            def adjacency(a, pa, t):
                made(dve, "t_hi_made", a, t + 1)
                at = slice(t * P, (t + 1) * P)
                low(t_lo2[:, pa, :, at], slot["QA"][:, :].rearrange("p (m n) -> p m n", m=T), NS,
                    t_hi2[:, pa, :, at], "t_lo_made")

            def aggregate_in(a, pa):
                made(dve, "y_hi_made", a, 1)
                low(y_lo[:, :, :], by_tile(slot["QA"][:, :]), 1 / WS, y_hi[:, :, 0:D], "y_lo_made")

            def aggregate(a, pa, g):
                q = wait_full(dve, a, f"l0_{g}")[:, :].rearrange("p (t c) -> p t c", c=256)
                tiles = slice(4 * g, 4 * g + 4)
                pre = fa[:, 0:HALF].rearrange("p (t d) -> p t d", t=4)
                if g:
                    made(dve, "l0_sum", a, g)
                dve.scalar_tensor_tensor(pre, q[:, :, 0:D], 1 / NS, bias_row(R_B0, 4), mul, add)\
                    .then_inc(S["l0_pre"], 1)
                dve.tensor_scalar(rinv2[:, pa, tiles], q[:, :, D], NS * ROW_EPS, None, add)\
                    .then_inc(S["rs_made"], 1)
                made(dve, "l0_pre", a, g + 1)
                dve.scalar_tensor_tensor(xa[:, tiles, :], pre, 0.0, xa[:, tiles, :], mx, add)\
                    .then_inc(S["l0_sum"], 1)

            def norm0(a, pa):
                made(dve, "rs_made", a, 2)
                dve.reciprocal(rinv2[:, pa, :], rinv2[:, pa, :]).then_inc(S["rinv_made"], 1)
                wait_apart(dve, (S["l0_sum"], count("l0_sum", a, 2)))
                layer_norm(a, 0, xa)

            def x1T(a, pa):
                low_of(a, "x1T", xT_hi, xT_lo)

            def conv1(a, pa):
                made(dve, "c_hi_made", a, 1)
                minus(c_lo[:, inner], fa[:, :], c_hi[:, inner], "c_lo_made")

            def conv2(a, pa, i):
                if i == 1:
                    q = wait_full(dve, a, "conv2")
                    made(dve, "c_lo_made", a, 1)
                    dve.scalar_tensor_tensor(fa[:, :], q[:, :], bn_scale[:, 1:2], xT[:, :], mul, add)\
                        .then_inc(S["c2_made"], 1)
                    made(dve, "xc_hi_made", a, 1)
                    minus(xc_lo[:, :], fa[:, :], xc_hi[:, :], "xc_lo_made")

            def message_in(a, pa):
                q = wait_full(dve, a, "msg")
                made(dve, "xc_lo_made", a, 1)
                dve.scalar_tensor_tensor(by_tile(fa[:, :]), by_tile(q[:, :]), 1 / WS,
                                         bias_row(R_BM), mul, add).then_inc(S["msg_pre"], 1)
                made(dve, "m_hi_made", a, 1)
                dve.scalar_tensor_tensor(m_lo[:, :, :], by_tile(fa[:, :]), 0.0, m_hi, mx, sub)\
                    .then_inc(S["m_lo_made"], 1)

            def s_rows(a, pa):
                made(dve, "s_made", a, 1)
                dve.tensor_tensor(sq, sv, sv, mul).then_inc(S["sq_made"], 1)
                q = wait_full(dve, a, "nsqr")
                dve.tensor_tensor(sv, sv, q[0:KD, :], add).then_inc(S["sv_made"], 1)
                made(dve, "sv_made", a, 1)
                dve.tensor_copy(s_p[:, 0, :], sv).then_inc(S["sp1_made"], 1)
                made(dve, "sp1_made", a, 1)
                minus(sv, sv, s_p[:, 0, :], "sv1_made")
                made(dve, "sv1_made", a, 1)
                dve.tensor_copy(s_p[:, 1, :], sv).then_inc(S["sp2_made"], 1)
                made(dve, "sp2_made", a, 1)
                minus(sv, sv, s_p[:, 1, :], "sv2_made")
                pick = lambda side, part: dist_c[:, KD + PARTS * side + part:KD + PARTS * side + part + 1]
                ones = (dist_c[:, KD + 2 * PARTS + 1:KD + 2 * PARTS + 2],
                        dist_c[:, KD + 2 * PARTS:KD + 2 * PARTS + 1])
                for side in range(2):
                    dve.tensor_scalar(d_t[:, side, :], s_p[:, 0, :], pick(side, 0),
                                      ones[side], mul, add).then_inc(S["d_first"], 1)
                for side in range(2):
                    made(dve, "d_first", a, side + 1)
                    dve.scalar_tensor_tensor(d_t[:, side, :], s_p[:, 1, :], pick(side, 1),
                                             d_t[:, side, :], mul, add).then_inc(S["d_second"], 1)
                made(dve, "sv2_made", a, 1)
                for side, d in enumerate((d_l, d_r)):
                    made(dve, "d_second", a, side + 1)
                    dve.scalar_tensor_tensor(d, sv, pick(side, 2), d_t[:, side, :], mul, add)\
                        .then_inc(S["d_made"], 1)

            def message(a, pa, t):
                q = wait_full(dve, a, f"mask{t}")
                made(dve, "exp_made", a, t + 1)
                dve.tensor_tensor(gw[:, t % 2, :], expd[:, t % 2, :], q[:, :], mul)\
                    .then_inc(S["g_made"], 1)
                made(dve, "g_hi_made", a, t + 1)
                minus(g_hl[:, t % 2, 1, :], gw[:, t % 2, :], g_hl[:, t % 2, 0, :], "g_lo_made")

            def gates(a, pa):
                made(dve, "xn_hi_made", a, 1)
                minus(xn_lo, fa[:, :], xn_hi, "xn_lo_made")
                q = wait_full(dve, a, "hid_n")
                dve.tensor_scalar(hid, q[:, :], hid_b[:, 0:1], None, add).then_inc(S["hid_made"], 1)
                made(dve, "hid_made", a, 1)
                made(dve, "tanh_r", a, 1)
                dve.scalar_tensor_tensor(hid, gate_t[:, 0, :], 1.0, hid, add, mul)\
                    .then_inc(S["u_made"], 1)
                q = wait_full(dve, a, "in_n")
                made(dve, "u_made", a, 1)
                dve.scalar_tensor_tensor(hid, hid, 0.5, q[:, :], mul, add).then_inc(S["v_made"], 1)

            def candidate(a, pa):
                made(dve, "cand_made", a, 1)
                minus(fa[:, :], xT[:, :], cand, "w_made")
                made(dve, "w_made", a, 1)
                made(dve, "tanh_z", a, 1)
                dve.scalar_tensor_tensor(fa[:, :], gate_t[:, 1, :], 1.0, fa[:, :], add, mul)\
                    .then_inc(S["w2_made"], 1)
                made(dve, "w2_made", a, 1)
                dve.scalar_tensor_tensor(fa[:, :], fa[:, :], 0.5, cand, mul, add)\
                    .then_inc(S["o_made"], 1)
                made(dve, "o_made", a, 1)
                dve.tensor_tensor(fa[:, :], fa[:, :], xT[:, :], add).then_inc(S["r1_made"], 1)

            def norm1(a, pa):
                wait_apart(dve, (S["r1_nat"], count("r1_nat", a, 1)))
                layer_norm(a, 1, xb2[:, pa, :, :])

            def x2T(a, pa):
                low_of(a, "x2T", xT_hi, xT_lo)

            def project(a, pa):
                q = wait_full(dve, a, "h2")
                dve.scalar_tensor_tensor(h2[:, :, :], by_tile(q[:, :]), 1 / WS, bias_row(R_B2),
                                         mul, add).then_inc(S["h2_made"], 1)

            def scores(b, pb, t):
                e = escore[:, t % 2, :]
                dve.wait_ge(S[f"e_loaded{t % 2}"], b * (8 * T) + 16 * (t // 2 + 1))
                if t:
                    made(dve, "e_made", b, t)
                dve.tensor_scalar(padv[:, :], e, 1e-5, MASKED, ALU.is_le, mul)\
                    .then_inc(S["pad_made"], 1)
                made(dve, "pad_made", b, t + 1)
                dve.scalar_tensor_tensor(e, e, rowc[:, R_AW + 2 * DH:NR], padv[:, :], mul, add)\
                    .then_inc(S["e_made"], 1)
                for h in range(H):
                    i = t * H + h
                    waits = [(S["e_made"], count("e_made", b, t + 1))]
                    if t == 0:
                        waits.append((S["sr_made"], count("sr_made", b, h + 1)))
                    else:
                        waits.append(full_count(b, f"pT{i - H}"))
                    wait_apart(dve, *waits)
                    dve.tensor_tensor_reduce(out=zbuf[:, h, :], in0=e, in1=sr[:, h, :], scale=1.0,
                                             scalar=-3e38, op0=add, op1=mx,
                                             accum_out=zmax[:, t, h:h + 1])\
                        .then_inc(S["z_made"], 1)
                if t == 0:
                    made(dve, "sl_made", b, 1)
                made(dve, "z_made", b, H * (t + 1))
                dve.tensor_tensor(etmp[:, t, :], zmax[:, t, :], sl[:, t, :], add)\
                    .then_inc(S["zsum"], 1)
                made(dve, "zsum", b, t + 1)
                dve.scalar_tensor_tensor(etmp[:, t, :], etmp[:, t, :], SLOPE2, etmp[:, t, :], mul,
                                         mx).then_inc(S["leak"], 1)
                made(dve, "leak", b, t + 1)
                dve.scalar_tensor_tensor(ebias[:, t, :], sl[:, t, :], SLOPE2, etmp[:, t, :], mul,
                                         sub).then_inc(S["eb"], 1)
                for h in range(H):
                    made(dve, "relu_made", b, t * H + h + 1)
                    dve.tensor_tensor(zbuf[:, h, :], zbuf[:, h, :], relu[:, h % 2, :], add)\
                        .then_inc(S["zr_made"], 1)

            def turn(b, pb, t):
                xb = xb2[:, pb, :, :]
                made(dve, "p_made", b, H * (t + 1))
                dve.reciprocal(rsum[:, t, :], rsum[:, t, :]).then_inc(S["rs_inv"], 1)
                q = wait_full(dve, b, f"attT{t}")
                made(dve, "rs_inv", b, t + 1)
                if t:
                    made(dve, "r2_made", b, t)
                heads = lambda x: x.rearrange("p (h d) -> p h d", h=H)
                dve.tensor_tensor(heads(attn[:, :]), heads(q[:, 0:P]),
                                  rsum[:, t, :].unsqueeze(2).to_broadcast([P, H, DH]), mul)\
                    .then_inc(S["att_scaled"], 1)
                made(dve, "att_scaled", b, t + 1)
                dve.tensor_tensor(attn[:, :], attn[:, :], xb[:, t, :], add)\
                    .then_inc(S["att_pre"], 1)
                made(dve, "att_pre", b, t + 1)
                dve.scalar_tensor_tensor(attn[:, :], attn[:, :], SLOPE2_OUT, attn[:, :], mul, mx)\
                    .then_inc(S["att_leak"], 1)
                made(dve, "att_leak", b, t + 1)
                dve.tensor_tensor(xb[:, t, :], xb[:, t, :], attn[:, :], add)\
                    .then_inc(S["r2_made"], 1)

            def norm2(b, pb):
                wait_apart(dve, (S["r2_made"], count("r2_made", b, T)))
                layer_norm(b, 2, xb2[:, pb, :, :])

            def x3T(b, pb):
                low_of(b, "x3T", x3_hi, x3_lo)

            def split_v(b, k, g):
                tiles = slice(4 * g, 4 * g + 4)
                made(dve, "vk_hi_made", b, 2 * k + g + 1)
                minus(flat(vk_lo[:, tiles, :]), flat(vk[:, tiles, :]), flat(vk_hi[:, tiles, :]),
                      "vk_lo_made")

            def own_term(b, k):
                w = rowc[:, R_CW + 2 - k:R_CW + 3 - k]
                shift, op = (rowc[:, R_CB:R_CB + 1], add) if k == 2 else (None, ALU.bypass)
                dve.tensor_scalar(wh, flat(h3), w, shift, mul, op).then_inc(S["wh_made"], 1)

            def h3_(b, pb):
                made(dve, "h3_made", b, 1)
                for g in range(2):
                    tiles = slice(4 * g, 4 * g + 4)
                    dve.tensor_scalar(flat(vk[:, tiles, :]), flat(h3[:, tiles, :]),
                                      rowc[:, R_CW + 3:R_CW + 4], None, mul).then_inc(S["vk_made"], 1)
                own_term(b, 0)
                split_v(b, 0, 0)
                split_v(b, 0, 1)

            def hop(b, pb, k, g):
                q = wait_full(dve, b, f"hop{k}_{g}")
                if g == 0:
                    made(dve, "wh_made", b, k + 1)
                    made(dve, "vk_lo_made", b, 2 * k + 2)
                for i in range(4):
                    t = 4 * g + i
                    ins = dve.scalar_tensor_tensor(
                        vk[:, t, :], q[:, i * P:(i + 1) * P], rinv2[:, pb, t:t + 1],
                        wh[:, t * P:(t + 1) * P], mul, add)
                ins.then_inc(S["hop_read"], 1)
                if g == 1:
                    made(dve, "hop_read", b, 2 * k + 2)
                    if k < 2:
                        own_term(b, k + 1)
                        split_v(b, k + 1, 0)
                        split_v(b, k + 1, 1)

            def finish(b, pb):
                xb = xb2[:, pb, :, :]
                made(dve, "hop_read", b, 6)
                dve.scalar_tensor_tensor(flat(vk), flat(vk), SLOPE3, flat(vk), mul, mx)\
                    .then_inc(S["out_leak"], 1)
                made(dve, "out_leak", b, 1)
                dve.tensor_tensor(flat(xb), flat(xb), flat(vk), add).then_inc(S["r3_made"], 1)
                wait_apart(dve, (S["r3_made"], count("r3_made", b, 1)))
                layer_norm(b, 3, xb)

            run(dve, x0T=x0T, adjacency=adjacency, aggregate_in=aggregate_in, aggregate=aggregate,
                norm0=norm0, x1T=x1T, conv1=conv1, conv2=conv2, message_in=message_in,
                s_rows=s_rows, message=message, gates=gates, candidate=candidate, norm1=norm1,
                x2T=x2T, project=project, scores=scores, turn=turn, norm2=norm2, x3T=x3T,
                h3=h3_, hop=hop, finish=finish)


def distance_constants(kd=64, parts=3, nc=3):
    import numpy as np
    c = np.zeros((kd, kd + 2 * parts + 2), np.float32)
    left, right, ones = kd, kd + parts, (kd + 2 * parts, kd + 2 * parts + 1)
    pairs = sorted(((i, j) for i in range(parts) for j in range(parts)), key=sum)
    for g, (i, j) in enumerate(pairs):
        rows = slice(2 + g * nc, 2 + (g + 1) * nc)
        c[rows, left + i] = 2.0
        c[rows, right + j] = 1.0
    last = 2 + nc * len(pairs)
    for k in range(parts):
        r = 2 * k if k == 0 else last + 2 * (k - 1)
        c[2:2 + nc, r:r + 2] = -1.0
        c[r, left + k] = 1.0
        c[r, ones[0]] = 1.0
        c[r + 1, right + k] = 1.0
        c[r + 1, ones[1]] = 1.0
    return c


def kernel(**inputs):
    import numpy as np
    import concourse.bacc as bacc
    from concourse.bass_utils import run_bass_kernel_spmd

    nc = bacc.Bacc("TRN2", target_bir_lowering=False, num_devices=1)
    arrays, aps = {}, {}
    for name, value in [*inputs.items(), ("dist_c", distance_constants())]:
        value = np.ascontiguousarray(value)
        arrays[f"in_{name}"] = value
        aps[name] = nc.dram_tensor(f"in_{name}", value.shape, mybir.dt.from_np(value.dtype),
                                   kind="ExternalInput").ap()
    shape = inputs["x"].shape
    out = nc.dram_tensor("out", shape, mybir.dt.float32, kind="ExternalOutput").ap()
    gnn_stack_kernel(nc, aps, out)
    r = run_bass_kernel_spmd(nc, [arrays], core_ids=[0])
    return r.results[0]["out"]
```

```python
import concourse.bass as bass
from concourse import mybir
from contextlib import ExitStack


def gnn_stack_kernel(nc: bass.Bass, a, out: bass.AP):
    f32 = mybir.dt.float32
    f16 = mybir.dt.float16
    bf16 = mybir.dt.bfloat16
    ALU = mybir.AluOpType
    ACT = mybir.ActivationFunctionType

    B, N, D = a["x"].shape
    P = 128
    T = N // P
    H = 4
    DH = D // H
    TAPS = a["L1_gnn_conv2_w"].shape[2]
    PAD = TAPS // 2
    HALF = 512
    NS = float(N)
    WS = 64.0
    LN_EPS = 1e-5
    BN_EPS = 1e-5
    ROW_EPS = 1e-9
    SLOPE2 = 0.2
    SLOPE2_OUT = 0.5
    SLOPE3 = 0.2
    MASKED = -float(2 ** 55)

    W_SELF, W_AGG = 0, 1
    W_CONV1 = 2
    W_CONV2 = 3
    W_MSG = W_CONV2 + TAPS
    W_IH = W_MSG + 1
    W_HH = W_IH + 6
    W_PROJ = W_HH + 3
    W_HOP = W_PROJ + 1
    NW = W_HOP + 1
    NT = NW - 2

    R_B0, R_BM, R_B2, R_CW, R_CB, R_AW = 0, D, 2 * D, 3 * D, 3 * D + 4, 3 * D + 5
    NR = R_AW + 2 * DH + 1

    PARTS = 3
    NC = a["L1_gnn_w_se"].shape[0]
    PAIRS0 = 2
    KD = 64

    UNITS = 2 * T

    USES = {
        ("QA0", "adj"): [f"adj{t}_0" for t in range(T)],
        ("QA1", "adj"): [f"adj{t}_1" for t in range(T)],
        ("QA", "first"): ["x0T", "y", "l0_0", "l0_1", "x1T", "s", "conv1", "nsqr", "conv2", "msg"],
        ("QA0", "msg"): ["nmp0", "nmp1"],
        ("QA1", "msg"): [f"mask{u}" for u in range(UNITS)],
        ("R1", "msg"): [f"dist{u}" for u in range(UNITS)],
        ("QA", "hops"): ["x3T", "h3"],
        ("QA", "gates"): ["gate_r", "hid_n"],
        ("QA", "mid"): ["l1r", "x2T", "h2", "sr_0", "sr_2"],
        ("QB0", "mid"): ["gate_z", "sr_1", "sr_3"],
        ("QB1", "mid"): ["in_n", "sl"],
        ("QB0", "att"): [f"pT{i}" for i in range(0, T * H, 2)],
        ("QB1", "att"): [f"pT{i}" for i in range(1, T * H, 2)],
        ("R0", "att"): [f"att{t // 2}" if t % 2 == 0 else f"attT{t // 2}" for t in range(2 * T)],
        ("R0", "hops"): [f"hop{k}_0" for k in range(3)],
        ("R1", "hops"): [f"hop{k}_1" for k in range(3)],
    }
    WHERE = {use: (key, j) for key, uses in USES.items() for j, use in enumerate(uses)}

    ctx = ExitStack()
    with ctx:
        def sb(name, shape, dt=f32):
            return ctx.enter_context(nc.sbuf_tensor(name, shape, dt))

        def sem(name):
            return ctx.enter_context(nc.semaphore(name))

        slot = {q: ctx.enter_context(nc.psum_tensor(q, [P, N if q[0] == "Q" else HALF], f32))
                for q in ("QA", "QB0", "QB1", "R0", "R1")}
        slot["QA0"], slot["QA1"] = slot["QA"][:, 0:HALF], slot["QA"][:, HALF:N]
        filled = {key: sem(f"filled_{key[0]}_{key[1]}") for key in USES}

        ident = sb("ident", [P, P])
        ident16 = sb("ident16", [P, P], f16)
        dist_c = sb("dist_c", [KD, KD + 2 * PARTS + 2])
        w_hi = sb("w_hi", [P, NW, P], f16)
        w_lo = sb("w_lo", [P, NW, P], f16)
        w_seT = sb("w_seT", [P, KD])
        rowc = sb("rowc", [P, NR])
        bn = sb("bn", [P, 4, 2])
        bn_scale = sb("bn_scale", [P, 2])
        bn_shift = sb("bn_shift", [P, 2])
        bn_tmp = sb("bn_tmp", [P, 2])
        minus_half = sb("minus_half", [P, T])
        gate_b = sb("gate_b", [P, 2, 3])
        half_b = sb("half_b", [P, 2])
        hid_b = sb("hid_b", [P, 1])
        b_se = sb("b_se", [KD, 1])
        a_blk = sb("a_blk", [P, 2 * H])
        v_lr = sb("v_lr", [P, 2 * H])
        vr_hi = sb("vr_hi", [P, H, P], f16)
        vr_lo = sb("vr_lo", [P, H, P], f16)

        side = sb("side", [P, 4, N])
        adj_in = side[:, 0:2, :]
        t_hi2 = sb("t_hi", [P, 2, T, N], f16)
        t_lo2 = sb("t_lo", [P, 2, T, N], f16)
        x2 = sb("x", [P, 2, T, D])
        xT = sb("xT", [P, N])
        xT_hi = sb("xT_hi", [P, N], f16)
        xT_lo = sb("xT_lo", [P, N], f16)
        y_hi = sb("y_hi", [P, T, D + 1], f16)
        y_lo = sb("y_lo", [P, T, D], f16)
        m_hi, m_lo = y_hi[:, :, 0:D], y_lo
        rinv2 = sb("rinv", [P, 2, T])
        stats = sb("stats", [P, T, 6])
        mvs = sb("mv", [P, 2, T, 2])
        rstds = sb("rstd", [P, 2, T])
        shift = sb("shift", [P, T])
        fa = sb("fa", [P, N])
        c_hi = sb("c_hi", [P, N + 2 * PAD], f16)
        c_lo = sb("c_lo", [P, N + 2 * PAD], f16)
        inner = slice(PAD, PAD + N)
        xc_hi = sb("xc_hi", [P, N], f16)
        xc_lo = sb("xc_lo", [P, N], f16)
        xn_hi, xn_lo = c_hi[:, inner], c_lo[:, inner]
        work = sb("work", [P, 10, N])
        gate_t, hid, cand = work[:, 0:2, :], work[:, 2, :], work[:, 3, :]
        zbuf, relu, pT = work[:, 0:4, :], work[:, 4:6, :], work[:, 6:10, :]
        by_tile = lambda x: x.rearrange("p (t d) -> p t d", t=T)
        h3, vk, wh = by_tile(work[:, 6, :]), by_tile(work[:, 7, :]), work[:, 8, :]
        vk_hl = [x.bitcast(f16).rearrange("p (k t d) -> p k t d", k=2, t=T)
                 for x in (work[:, 9, :], side[:, 2, :])]
        x3_hl = side[:, 3, :].bitcast(f16).rearrange("p (k n) -> p k n", k=2)
        x3_hi, x3_lo = x3_hl[:, 0, :], x3_hl[:, 1, :]
        sr = sb("sr", [P, H, N])
        sv, sq = side[0:KD, 0, :], side[0:KD, 1, :]
        halves = lambda x: x.bitcast(bf16).rearrange("p (k n) -> p k n", k=2)
        s_p = halves(side[0:KD, 2, :])
        d_t = halves(side[0:KD, 1, :])
        d_l, d_r = halves(side[0:KD, 3, :])[:, 0, :], halves(side[0:KD, 3, :])[:, 1, :]
        expd = side[:, 0, :].rearrange("p (k n) -> p k n", k=2)
        gw = side[:, 1, :].rearrange("p (k n) -> p k n", k=2)
        g_hl = side[:, 2, :].bitcast(f16).rearrange("p (k h n) -> p k h n", k=2, h=2)
        escore = sb("escore", [P, 2, N])
        ones_row = escore[0:1, 0, HALF:HALF + P]
        padv = sb("padv", [P, N])
        rows = padv[0:1, 0:NR]
        h2 = sb("h2", [P, T, D])
        sl = sb("sl", [P, T, H])
        sl4 = sb("sl4", [P, T, H])
        zmax = sb("zmax", [P, T, H])
        ebias = sb("ebias", [P, T, H])
        etmp = sb("etmp", [P, T, H])
        rsum = sb("rsum", [P, T, H])
        attT = sb("attT", [P, P])
        attn = sb("attn", [P, P])

        CONV_CHUNKS = 14
        S = {n: sem(n) for n in (
            "const_loaded pool_const w_filled w_hi_made w_lo_made vec_made bn_ready dve_once apart "
            "adj_loaded0 adj_loaded1 x_loaded e_loaded0 e_loaded1 out_stored x_free "
            "x0T_hi x0T_lo x1T_f x1T_hi x1T_lo x2T_f x2T_hi x2T_lo x3T_hi x3T_lo "
            "t_hi_made t_lo_made y_hi_made y_lo_made l0_pre l0_sum rs_made rinv_made "
            "conv1_made c_hi_made c_lo_made c2_made xc_made xc_hi_made xc_lo_made msg_pre "
            "m_hi_made m_lo_made s_made sq_made sv_made sp1_made sv1_made sp2_made "
            "sv2_made d_first d_second d_made exp_made g_made g_used g_hi_made g_lo_made "
            "xn_made xn_hi_made xn_lo_made tanh_r tanh_z hid_made u_made v_made cand_made "
            "w_made w2_made o_made r1_made r1_nat h2_made sl_made sl4_made sr_made "
            "pad_made e_made z_made relu_made zr_made zsum leak eb p_made pT_made attT_made "
            "rs_inv att_scaled att_pre att_leak r2_made h3_made vk_made hop_read wh_made "
            "vk_hi_made vk_lo_made pT_used out_leak r3_made").split()
            + [f"ln{k}_{n}" for k in range(4)
               for n in ("stats", "mv", "eps", "pow", "neg", "rstd", "done")]}

        N_CONST = 34 - 2 + 1 + 2 * PARTS * PARTS
        N_GROUPS = (NT + T - 1) // T
        W_DONE = N_GROUPS + 3

        PER = {"t_hi_made": 2 * T, "t_lo_made": 2 * T, "rs_made": 2, "l0_pre": 2, "l0_sum": 2,
               "d_first": 2, "d_second": 2, "d_made": 2,
               "exp_made": UNITS, "g_made": UNITS, "g_used": UNITS - 2, "g_hi_made": UNITS,
               "g_lo_made": UNITS, "xn_made": 2, "xn_hi_made": 2, "xn_lo_made": 2,
               "sr_made": H, "pad_made": T, "e_made": T, "z_made": T * H, "relu_made": T * H,
               "zr_made": T * H, "zsum": 2 * T, "leak": 2 * T, "eb": 2 * T, "p_made": T * H,
               "pT_made": T * H, "attT_made": T, "att_scaled": T, "att_pre": T, "att_leak": T,
               "r2_made": T, "wh_made": 6, "vk_made": 2, "hop_read": 6, "vk_hi_made": 6,
               "vk_lo_made": 6, "rs_inv": T, "pT_used": T}
        READ_BY = {"x0T": ("x0T_lo", 1), "y": ("y_lo_made", 1), "l0_0": ("rs_made", 1),
                   "l0_1": ("rs_made", 2), "x1T": ("x1T_lo", 1), "conv1": ("conv1_made", 1),
                   "conv2": ("c2_made", 1), "msg": ("msg_pre", 1), "nmp0": ("xn_made", 1),
                   "nmp1": ("xn_made", 2),
                   "gate_r": ("tanh_r", 1), "hid_n": ("hid_made", 1), "l1r": ("r1_nat", 1),
                   "x2T": ("x2T_lo", 1), "h2": ("h2_made", 1), "x3T": ("x3T_lo", 1),
                   "h3": ("h3_made", 1), "gate_z": ("tanh_z", 1), "in_n": ("v_made", 1),
                   "s": ("s_made", 1), "nsqr": ("sv_made", 1),
                   "sl": ("sl_made", 1)}
        READ_BY |= {f"sr_{h}": ("sr_made", h + 1) for h in range(H)}
        READ_BY |= {f"adj{t}_{i}": ("t_lo_made", 2 * t + i + 1) for t in range(T) for i in range(2)}
        READ_BY |= {f"dist{u}": ("exp_made", u + 1) for u in range(UNITS)}
        READ_BY |= {f"mask{u}": ("g_made", u + 1) for u in range(UNITS)}
        READ_BY |= {f"pT{i}": ("pT_made", i + 1) for i in range(T * H)}
        READ_BY |= {f"att{t}": ("attT_made", t + 1) for t in range(T)}
        READ_BY |= {f"attT{t}": ("att_scaled", t + 1) for t in range(T)}
        READ_BY |= {f"hop{k}_{g}": ("hop_read", 2 * k + g + 1) for k in range(3) for g in range(2)}
        BEFORE = {("QA0", "adj"): [("sr_made", 0)], ("QA1", "adj"): [("sr_made", 0)],
                  ("QA", "first"): [("t_lo_made", 2 * T)], ("QA", "hops"): [("sr_made", H)],
                  ("QA0", "msg"): [("msg_pre", 1)], ("QA1", "msg"): [("msg_pre", 1)],
                  ("R1", "msg"): [("hop_read", -6)],
                  ("QA", "gates"): [("xn_made", 2), ("g_made", UNITS)],
                  ("QA", "mid"): [("hid_made", 1), ("h3_made", 0)],
                  ("QB0", "mid"): [("pT_made", 0)], ("QB1", "mid"): [("pT_made", 0)],
                  ("QB0", "att"): [("sr_made", H)], ("QB1", "att"): [("sl_made", 1)],
                  ("R0", "att"): [("hop_read", 0)],
                  ("R0", "hops"): [("att_scaled", T)], ("R1", "hops"): [("att_scaled", T)]}

        ACT_START = ("t_hi_made", "h3_made", "pT_made", "sr_made", "x1T_hi")
        DVE_START = ("z_made", "zr_made", "hop_read", "g_lo_made", "r3_made")
        POOL_START = ("x_free",)
        START_AT_1 = ACT_START + DVE_START + POOL_START

        block = ctx.enter_context(nc.Block())

        def wait_apart(eng, *waits):
            for semaphore, value in waits:
                eng.wait_ge(semaphore, value)
            eng.sem_inc(S["apart"], 1)

        def count(name, b, k):
            return b * PER.get(name, 1) + k + (name in START_AT_1)

        def start(eng, *names):
            for name in names:
                assert name in START_AT_1
                eng.sem_inc(S[name], 1)

        def may_fill(eng, b, use):
            key, j = WHERE[use]
            for name, k in [READ_BY[USES[key][j - 1]]] if j else BEFORE[key]:
                value = count(name, b, k)
                if not isinstance(value, int) or value > 0:
                    eng.wait_ge(S[name], value)
            return slot[key[0]]

        def fill_done(ins, use):
            ins.then_inc(filled[WHERE[use][0]], 1)

        def full_count(b, use):
            key, j = WHERE[use]
            return filled[key], b * len(USES[key]) + j + 1

        def wait_full(eng, b, use):
            eng.wait_ge(*full_count(b, use))
            return slot[WHERE[use][0][0]]

        def made(eng, name, b, k):
            eng.wait_ge(S[name], count(name, b, k))

        x_dram, adj_dram = a["x"], a["adj"]

        SLOW = {"x0T": 1, "x1T": 1, "aggregate_in": 1, "aggregate": 2, "conv1": 1, "conv2": 2}

        def in_order(eng, step, late):
            def beside(a, pa):
                parts = []

                def then(*steps, rest=0):
                    parts.append(list(steps))
                    parts.extend([] for _ in range(rest))

                for t in range(T):
                    then(("adjacency", t), rest=int(t == T - 1))
                then(("x0T",), rest=1)
                then(("aggregate_in",), rest=1)
                for c in range(4):
                    then(("aggregate", c), rest=(0, 2, 0, 1)[c])
                then(("norm0",), rest=1)
                then(("norm0_b",), rest=1)
                then(("x1T",), rest=1)
                then(("s_rows",), ("conv1",), rest=1)
                then(("s_sum",))
                then(("conv2", 0))
                then(("conv2", 1), ("s_parts",))
                then(("conv2", 2))
                then(("conv2", 3), ("s_sides", 0))
                then(("conv2", 4))
                then(("conv2", 5), ("s_sides", 1))
                for c in range(6, CONV_CHUNKS):
                    then(("conv2", c), rest=2 * int(c == CONV_CHUNKS - 1))
                then(("conv2_b",), ("message_in",))
                then(("message_in_b",))
                first = len(parts)
                parts += [[] for _ in range(UNITS + 3)]
                for u in range(UNITS):
                    at = first + u
                    parts[at].append(("unit", u))
                    parts[at + 1].append(("unit_halves", u))
                    parts[at + 3].insert(0, ("message", u))
                    if u % T == T - 1:
                        parts[at + 3].insert(1, ("received", u // T))
                return [[(name, a, pa, *args) for name, *args in part] for part in parts]

            BY_TILE = ("to_turn", "turn", "turned")

            def cycle(a, b, pa):
                pb = 1 - pa
                parts = beside(a, pa) if a is not None else []

                def filler(i):
                    for behind in (3, 2, 1, 0):
                        if 0 <= i - behind < len(parts):
                            for args in parts[i - behind]:
                                if late(args[0]) == behind:
                                    step(*args)

                def at(name, p, *args):
                    ahead = p < 2 and name in ("scores", "probs")
                    if b is not None and 0 <= p < (T if name in BY_TILE else 2 * T) and not ahead:
                        args = (p,) if name in BY_TILE else (p // 2, p % 2, *args)
                        step(name, b, pb, *args)

                for p in range(1, 2 * T + 2):
                    turning = (p - 3) // 2 if p % 2 else -1
                    turned = (p - 4) // 2 if p % 2 == 0 else -1
                    at("scores", p, 0)
                    at("transpose", p - 1, 0)
                    filler(4 * p - 4)
                    at("scores", p, 1)
                    at("transpose", p - 1, 1)
                    filler(4 * p - 3)
                    at("turned", turned)
                    at("attend", p - 2)
                    at("to_sbuf", p - 1, 0)
                    at("probs", p, 0)
                    at("to_turn", turning)
                    filler(4 * p - 2)
                    at("to_sbuf", p - 1, 1)
                    at("probs", p, 1)
                    filler(4 * p - 1)
                    at("turn", turning)
                at("turned", T - 1)
                for i in range(8 * T + 4, len(parts) + 3):
                    filler(i)

                def both(on_a="", on_b="", *args):
                    if on_a and a is not None:
                        step(on_a, a, pa)
                    if on_b and b is not None:
                        step(on_b, b, pb, *args)

                def start_attention(name, g):
                    if a is not None:
                        for j in range(2):
                            step(name, a, pa, 0, g, j)

                both("", "norm2")
                both("", "norm2_b")
                both("gates")
                if b is not None and a is not None:
                    step("after_first", a, pa)
                both("", "x3T")
                both("gates_b", "h3")
                both("gates_c")
                both("candidate", "hop", 0, 0)
                both("norm1")
                both("norm1_b", "hop", 0, 1)
                both("x2T", "hop", 1, 0)
                both("project")
                both("", "hop", 1, 1)
                both("s_right")
                start_attention("scores", 0)
                start_attention("probs", 0)
                start_attention("scores", 1)
                both("", "hop", 2, 0)
                start_attention("probs", 1)
                both("", "hop", 2, 1)
                both("", "finish")

            cycle(0, None, 0)
            with eng.Fori(0, B // 2 - 1) as i:
                cycle(i * 2 + 1, i * 2, 1)
                cycle(i * 2 + 2, i * 2 + 1, 0)
            cycle(B - 1, B - 2, 1)
            cycle(None, B - 1, 0)

        def run(eng, late=lambda name: 0, **steps):
            def step(name, *args):
                if name in steps:
                    steps[name](*args)
            in_order(eng, step, late)

        @block.sync
        def _(sp):
            raw = work[:, 0:4, :].rearrange("p a n -> p (a n)")
            w0raw = escore[:, 0, 0:2 * P].rearrange("p (a f) -> p a f", a=2)

            def load(dst, src, to="const_loaded"):
                sp.dma_start(dst, src).then_inc(S[to], 16)

            o = P * (1 + TAPS)
            load(raw[:, 0:P], a["L1_gnn_conv1_w"].rearrange("o c k -> o (c k)"))
            load(raw[:, P:o], a["L1_gnn_conv2_w"].rearrange("o c k -> o (c k)"))
            load(raw[:, o:o + P], a["L1_gnn_w_msg"])
            load(raw[:, o + P:o + 7 * P].rearrange("p (g k) -> p g k", g=3),
                 a["L1_gnn_w_ih"].rearrange("(g p) k -> p g k", p=P))
            load(raw[:, o + 7 * P:o + 10 * P].rearrange("p (g k) -> p g k", g=3),
                 a["L1_gnn_w_hh"].rearrange("(g p) k -> p g k", p=P))
            load(raw[:, o + 10 * P:o + 11 * P], a["L2_gnn_W_proj"])
            load(raw[:, o + 11 * P:o + 12 * P], a["L3_gnn_W"])
            load(w0raw, a["L0_gnn_weight"].rearrange("(a p) f -> p a f", p=P))
            for off, name in ((R_B0, "L0_gnn_bias"), (R_BM, "L1_gnn_b_msg"), (R_B2, "L2_gnn_bias"),
                              (R_CW, "L3_gnn_conv_w"), (R_CB, "L3_gnn_conv_b")):
                load(rows[0:1, off:off + a[name].shape[0]], a[name].rearrange("(a n) -> a n", a=1))
            load(rows[0:1, R_AW:NR], a["L2_gnn_a_w"])
            for i, kind in enumerate("gbmv"):
                for j in (1, 2):
                    load(bn[:, i, j - 1:j], a[f"L1_gnn_bn{j}_{kind}"].rearrange("(p a) -> p a", a=1))
            with nc.allow_non_contiguous_dma(reason="768 bias values, once"):
                load(gate_b[:, 0, :], a["L1_gnn_b_ih"].rearrange("(g p) -> p g", p=P))
                load(gate_b[:, 1, :], a["L1_gnn_b_hh"].rearrange("(g p) -> p g", p=P))
            load(dist_c[:, :], a["dist_c"])
            sp.wait_ge(S["pool_const"], 3)
            for i in range(PARTS * PARTS):
                at = slice(PAIRS0 + i * NC, PAIRS0 + (i + 1) * NC)
                load(escore[at, 1, 0:P], a["L1_gnn_w_se"])
                load(b_se[at, :], a["L1_gnn_b_se"].rearrange("(p a) -> p a", a=1))
            for h in range(H):
                for side in range(2):
                    load(a_blk[h * DH:(h + 1) * DH, side * H + h:side * H + h + 1],
                         a["L2_gnn_a_w"][0:1, side * DH:(side + 1) * DH].rearrange("a p -> p a"))

            def row_tile(b, t):
                return adj_dram[bass.ds(b, 1), t * P:(t + 1) * P, :].rearrange("a p m -> p (a m)")

            def load_x(a, pa):
                if not isinstance(a, int) or a > 0:
                    made(sp, "x_free", a - 1, 0)
                sp.dma_start(x2[:, pa, :, :], x_dram[bass.ds(a, 1), :, :].rearrange(
                    "a (t p) d -> p (a t) d", p=P)).then_inc(S["x_loaded"], 16)

            def load_adj(a, pa, t):
                if t == 0:
                    made(sp, "g_lo_made", a, 0)
                made(sp, "t_hi_made", a, 2 * max(t - 1, 0))
                sp.dma_start(adj_in[:, t % 2, :], row_tile(a, t)).then_inc(S[f"adj_loaded{t % 2}"], 16)

            def load_e(b, pb, t, g, j):
                if g == 0 and j == 0:
                    for t in (0, 1) if t == 0 else (t + 1,) if t + 1 < T else ():
                        made(sp, "z_made", b, H * max(t - 1, 0))
                        sp.dma_start(escore[:, t % 2, :], row_tile(b, t))\
                            .then_inc(S[f"e_loaded{t % 2}"], 16)

            sp.wait_ge(S["w_lo_made"], W_DONE)
            run(sp, x0T=load_x, adjacency=load_adj, scores=load_e)
            sp.wait_ge(S["out_stored"], 16 * B)

        @block.gpsimd
        def _(pool):
            for tile, value in ((a_blk[:, :], 0.0), (escore[0:KD, 1, 0:P], 0.0), (b_se[:, :], 0.0),
                                (ident[:, :], 0.0), (ones_row, 1.0), (minus_half[:, :], -0.5),
                                (c_hi[:, :], 0.0), (c_lo[:, :], 0.0), (y_hi[:, :, D:D + 1], 1.0)):
                pool.memset(tile, value).then_inc(S["pool_const"], 1)
            pool.wait_ge(S["pool_const"], 4)
            pool.affine_select(out=ident[:, :], in_=ident[:, :], compare_op=ALU.not_equal, fill=1.0,
                               base=0, pattern=[[-1, P]], channel_multiplier=1)\
                .then_inc(S["pool_const"], 1)
            for name in POOL_START:
                pool.sem_inc(S[name], 1)
            pool.wait_ge(S["const_loaded"], 16 * N_CONST)
            pool.wait_ge(S["pool_const"], 6)
            pool.tensor_scalar(bn_tmp[:, :], bn[:, 3, :], BN_EPS, None, ALU.add)\
                .then_inc(S["bn_ready"], 1)
            pool.wait_ge(S["bn_ready"], 1)
            pool.tensor_tensor(bn_tmp[:, :], bn_tmp[:, :], minus_half[:, 0:2], ALU.pow)\
                .then_inc(S["bn_ready"], 1)

            def inv_std(k):
                mv, rstd = mvs[:, k // 3, :, :], rstds[:, k // 3, :]

                def norm(b, p):
                    wait_apart(pool, (S[f"ln{k}_mv"], count(f"ln{k}_mv", b, 1)))
                    pool.tensor_scalar(rstd, mv[:, :, 1], LN_EPS, None, ALU.add)\
                        .then_inc(S[f"ln{k}_eps"], 1)
                    made(pool, f"ln{k}_eps", b, 1)
                    made_rstd = pool.tensor_tensor(rstd, rstd, minus_half[:, :], ALU.pow)
                    if k:
                        made_rstd.then_inc(S[f"ln{k}_rstd"], 1)
                        return
                    made_rstd.then_inc(S["ln0_pow"], 1)
                    wait_apart(pool, (S["ln0_pow"], count("ln0_pow", b, 1)))
                    pool.tensor_scalar(mv[:, :, 1], mv[:, :, 0], -1.0, None, ALU.mult)\
                        .then_inc(S["ln0_neg"], 1)
                    made(pool, "ln0_neg", b, 1)
                    pool.tensor_tensor(shift[:, :], mv[:, :, 1], rstd, ALU.mult)\
                        .then_inc(S["ln0_rstd"], 1)
                return norm

            def finish(b, p):
                inv_std(3)(b, p)
                wait_apart(pool, (S["ln3_rstd"], count("ln3_rstd", b, 1)))
                mv, rstd = mvs[:, 1, :, :], rstds[:, 1, :]
                for t in range(T):
                    x = x2[:, p, t, :]
                    ins = pool.tensor_scalar(x, x, mv[:, t, 0:1], rstd[:, t:t + 1], ALU.subtract,
                                             ALU.mult)
                ins.then_inc(S["ln3_done"], 1)
                made(pool, "ln3_done", b, 1)
                pool.dma_start(out[bass.ds(b, 1), :, :].rearrange("a (t p) d -> p (a t) d", p=P),
                               x2[:, p, :, :]).then_inc(S["out_stored"], 16)
                pool.wait_ge(S["out_stored"], b * 16 + 16)
                pool.sem_inc(S["x_free"], 1)

            run(pool, norm0=inv_std(0), norm1=inv_std(1), norm2=inv_std(2), finish=finish)

        @block.tensor
        def _(pe):
            raw = work[:, 0:4, :].rearrange("p a n -> p (a n)")

            def mm(o, lhsT, rhs, start, stop):
                return pe.matmul(o, lhsT, rhs, start=start, stop=stop)

            def three(o, l_hi, l_lo, r_hi, r_lo, start=True, stop=True):
                mm(o, l_hi, r_hi, start, False)
                mm(o, l_hi, r_lo, False, False)
                return mm(o, l_lo, r_hi, False, stop)

            def col(t):
                return slice(t * P, (t + 1) * P)

            def half(i):
                return slice(i * HALF, (i + 1) * HALF)

            pe.wait_ge(S["const_loaded"], 16 * N_CONST)
            pe.wait_ge(S["pool_const"], 10)
            for g in range(0, NT, T):
                q = slot["QB0"] if g // T % 2 == 0 else slot["QB1"]
                if g >= 2 * T:
                    pe.wait_ge(S["w_lo_made"], g // T - 1)
                for i in range(g, min(g + T, NT)):
                    if 1 <= i <= TAPS:
                        taps = raw[:, P:P * (1 + TAPS)].rearrange("p (c k) -> p k c", k=TAPS)
                        src = taps[:, i - 1, :]
                    else:
                        src = raw[:, col(i)]
                    last = pe.transpose(q[:, col(i - g)], src, ident[:, :])
                last.then_inc(S["w_filled"], 1)
            pe.transpose(slot["QA"][:, 0:KD], escore[0:KD, 1, 0:P], ident[0:KD, 0:KD])
            mm(slot["QA"][:, HALF:HALF + NR], ones_row, rows, True, True)
            proj = raw[:, col(NT - 2)]
            mm(slot["R0"][:, 0:2 * H], proj, a_blk[:, :], True, True).then_inc(S["w_filled"], 1)
            pe.wait_ge(S["vec_made"], 4)
            pe.wait_ge(S["w_lo_made"], W_DONE)

            def transposed(b, use, src):
                q = may_fill(pe, b, use)
                for t in range(T):
                    last = pe.transpose(q[:, col(t)], src[:, t, :], ident[:, :])
                fill_done(last, use)

            def rows_times(b, use, w, x_hi=xT_hi, x_lo=xT_lo):
                q = may_fill(pe, b, use)
                for t in range(T):
                    last = three(q[:, col(t)], x_hi[:, col(t)], x_lo[:, col(t)],
                                 w_hi[:, w, :], w_lo[:, w, :])
                fill_done(last, use)

            def both(b, *names):
                for name in names:
                    made(pe, name, b, PER.get(name, 1))

            def x0T(a, pa):
                pe.wait_ge(S["x_loaded"], a * 16 + 16)
                transposed(a, "x0T", x2[:, pa, :, :])

            def adjacency(a, pa, t):
                pe.wait_ge(S[f"adj_loaded{t % 2}"], a * (8 * T) + 16 * (t // 2 + 1))
                for i in range(2):
                    q = may_fill(pe, a, f"adj{t}_{i}")
                    for m in range(T // 2):
                        last = pe.transpose(q[:, col(m)], adj_in[:, t % 2, col(4 * i + m)], ident[:, :])
                    fill_done(last, f"adj{t}_{i}")

            def aggregate_in(a, pa):
                both(a, "x0T_hi", "x0T_lo")
                rows_times(a, "y", W_AGG)

            def aggregate(a, pa, c):
                g = c // 2
                if c == 0:
                    both(a, "y_hi_made", "y_lo_made", "t_hi_made", "t_lo_made")
                t_hi, t_lo = t_hi2[:, pa, :, :], t_lo2[:, pa, :, :]
                if c % 2 == 0:
                    may_fill(pe, a, f"l0_{g}")
                q = slot["QA"]
                for i in range(2 * (c % 2), 2 * (c % 2) + 2):
                    t = 4 * g + i
                    o = q[:, 256 * i:256 * i + D + 1]
                    for m in range(T):
                        mm(o, t_hi[:, m, col(t)], y_hi[:, m, :], m == 0, False)
                        mm(o[:, 0:D], t_hi[:, m, col(t)], y_lo[:, m, :], False, False)
                        mm(o, t_lo[:, m, col(t)], y_hi[:, m, :], False, False)
                    last = three(o[:, 0:D], xT_hi[:, col(t)], xT_lo[:, col(t)],
                                 w_hi[:, W_SELF, :], w_lo[:, W_SELF, :], start=False)
                if c % 2:
                    fill_done(last, f"l0_{g}")

            def x1T(a, pa):
                both(a, "ln0_done")
                transposed(a, "x1T", x2[:, pa, :, :])

            def conv1(a, pa):
                both(a, "x1T_hi", "x1T_lo")
                q = may_fill(pe, a, "conv1")
                for i in range(2):
                    last = three(q[:, half(i)], w_hi[:, W_CONV1, :], w_lo[:, W_CONV1, :],
                                 xT_hi[:, half(i)], xT_lo[:, half(i)])
                fill_done(last, "conv1")

            def conv2(a, pa, c):
                if c == 0:
                    both(a, "c_hi_made", "c_lo_made")
                    may_fill(pe, a, "conv2")
                for j in range(2 * TAPS * c // CONV_CHUNKS, 2 * TAPS * (c + 1) // CONV_CHUNKS):
                    i, k = j // TAPS, j % TAPS
                    at = slice(i * HALF + k, i * HALF + k + HALF)
                    last = three(slot["QA"][:, half(i)], w_hi[:, W_CONV2 + k, :],
                                 w_lo[:, W_CONV2 + k, :], c_hi[:, at], c_lo[:, at],
                                 start=k == 0, stop=k == TAPS - 1)
                if c == CONV_CHUNKS - 1:
                    fill_done(last, "conv2")

            def message_in(a, pa):
                rows_times(a, "msg", W_MSG)

            def s_rows(a, pa):
                both(a, "x1T_f")
                q = may_fill(pe, a, "s")
                for i in range(2):
                    last = mm(q[0:KD, half(i)], w_seT[:, :], xT[:, half(i)], True, True)
                fill_done(last, "s")

            def s_sum(a, pa):
                both(a, "sq_made")
                q = may_fill(pe, a, "nsqr")
                pe.sem_inc(S["apart"], 1)
                for i in range(2):
                    last = mm(q[0:KD, half(i)], dist_c[:, 0:KD], sq[:, half(i)], True, True)
                fill_done(last, "nsqr")

            def unit(a, pa, u):
                i, t = u // T, u % T
                if u == 0:
                    both(a, "d_made")
                q = may_fill(pe, a, f"dist{u}")
                fill_done(mm(q[:, :], d_l[:, col(t)], d_r[:, half(i)], True, True), f"dist{u}")
                q = may_fill(pe, a, f"mask{u}")
                mm(q, ident16[:, :], t_hi2[:, pa, t, half(i)], True, False)
                fill_done(mm(q, ident16[:, :], t_lo2[:, pa, t, half(i)], False, True), f"mask{u}")

            def message(a, pa, u):
                i, t = u // T, u % T
                if u == 0:
                    both(a, "m_hi_made", "m_lo_made")
                if t == 0:
                    may_fill(pe, a, f"nmp{i}")
                made(pe, "g_hi_made", a, u + 1)
                made(pe, "g_lo_made", a, u + 1)
                last = three(slot["QA0"], m_hi[:, t, :], m_lo[:, t, :],
                             g_hl[:, u % 2, 0, :], g_hl[:, u % 2, 1, :],
                             start=t == 0, stop=t == T - 1)
                if t < T - 1:
                    last.then_inc(S["g_used"], 1)
                else:
                    fill_done(last, f"nmp{i}")

            def gate(b, use, blocks):
                q = may_fill(pe, b, use)
                for i in range(2):
                    for j, (w, r_hi, r_lo) in enumerate(blocks):
                        last = three(q[:, half(i)], w_hi[:, w, :], w_lo[:, w, :],
                                     r_hi[:, half(i)], r_lo[:, half(i)],
                                     start=j == 0, stop=j == len(blocks) - 1)
                fill_done(last, use)

            def gates(a, pa):
                both(a, "xc_hi_made", "xc_lo_made", "xn_hi_made", "xn_lo_made")
                gate(a, "gate_r", [(W_IH, xc_hi, xc_lo), (W_HH, xT_hi, xT_lo),
                                   (W_IH + 1, xn_hi, xn_lo)])
                gate(a, "hid_n", [(W_HH + 2, xT_hi, xT_lo)])

            def gates_b(a, pa):
                gate(a, "in_n", [(W_IH + 4, xc_hi, xc_lo), (W_IH + 5, xn_hi, xn_lo)])

            def gates_c(a, pa):
                gate(a, "gate_z", [(W_IH + 2, xc_hi, xc_lo), (W_IH + 3, xn_hi, xn_lo),
                                   (W_HH + 1, xT_hi, xT_lo)])

            def norm1(a, pa):
                both(a, "r1_made")
                q = may_fill(pe, a, "l1r")
                for t in range(T):
                    last = pe.transpose(q[:, col(t)], fa[:, col(t)], ident[:, :])
                fill_done(last, "l1r")

            def x2T(a, pa):
                both(a, "ln1_done")
                transposed(a, "x2T", x2[:, pa, :, :])

            def project(a, pa):
                both(a, "x2T_hi", "x2T_lo")
                rows_times(a, "h2", W_PROJ)
                q = may_fill(pe, a, "sl")
                for t in range(T):
                    last = mm(q[:, H * t:H * t + H], xT[:, col(t)], v_lr[:, 0:H], True, True)
                fill_done(last, "sl")

            def s_right(a, pa):
                for h in range(H):
                    q = may_fill(pe, a, f"sr_{h}")
                    for i in range(2):
                        last = three(q[:, half(i)], vr_hi[:, h, :], vr_lo[:, h, :],
                                     xT_hi[:, half(i)], xT_lo[:, half(i)])
                    fill_done(last, f"sr_{h}")

            def transpose(b, pb, t, g, j):
                h = 2 * g + j
                i = t * H + h
                made(pe, "p_made", b, i + 1)
                q = may_fill(pe, b, f"pT{i}")
                for j in range(T):
                    last = pe.transpose(q[:, col(j)], zbuf[:, h, col(j)], ident[:, :])
                fill_done(last, f"pT{i}")

            def attend(b, pb, t, g):
                made(pe, "pT_made", b, H * t + 2 * g + 2)
                if t == 0 and g == 0:
                    both(b, "h2_made")
                if g == 0:
                    may_fill(pe, b, f"att{t}")
                q = slot["R0"]
                for j in range(T):
                    for h in (2 * g, 2 * g + 1):
                        last = mm(q[h * DH:(h + 1) * DH, 0:P], h2[:, j, h * DH:(h + 1) * DH],
                                  pT[:, h, col(j)], j == 0, j == T - 1)
                if g:
                    fill_done(last, f"att{t}")
                else:
                    last.then_inc(S["pT_used"], 1)

            def turn(b, pb, t):
                made(pe, "attT_made", b, t + 1)
                q = may_fill(pe, b, f"attT{t}")
                fill_done(pe.transpose(q[:, 0:P], attT[:, :], ident[:, :]), f"attT{t}")

            def after_first(a, pa):
                made(pe, "hid_made", a, 1)
                made(pe, "exp_made", a, UNITS)

            def x3T(b, pb):
                both(b, "ln2_done")
                transposed(b, "x3T", x2[:, pb, :, :])

            def h3_(b, pb):
                both(b, "x3T_hi", "x3T_lo")
                rows_times(b, "h3", W_HOP, x3_hi, x3_lo)

            def hop(b, pb, k, g):
                t_hi, t_lo = t_hi2[:, pb, :, :], t_lo2[:, pb, :, :]
                q = may_fill(pe, b, f"hop{k}_{g}")
                for i in range(4):
                    t = 4 * g + i
                    for m in range(T):
                        if g == 0 and i == 0 and m % 4 == 0:
                            made(pe, "vk_hi_made", b, 2 * k + m // 4 + 1)
                            made(pe, "vk_lo_made", b, 2 * k + m // 4 + 1)
                        last = three(q[:, col(i)], t_hi[:, m, col(t)], t_lo[:, m, col(t)],
                                     vk_hl[k % 2][:, 0, m, :], vk_hl[k % 2][:, 1, m, :],
                                     m == 0, m == T - 1)
                fill_done(last, f"hop{k}_{g}")

            run(pe, x0T=x0T, adjacency=adjacency, aggregate_in=aggregate_in, aggregate=aggregate,
                x1T=x1T, conv1=conv1, conv2=conv2, message_in=message_in, s_rows=s_rows,
                s_sum=s_sum, unit=unit, message=message, gates=gates, gates_b=gates_b,
                gates_c=gates_c, norm1=norm1, x2T=x2T, project=project, s_right=s_right,
                transpose=transpose, attend=attend, turn=turn, after_first=after_first, x3T=x3T,
                h3=h3_, hop=hop)

        @block.scalar
        def _(act):
            start(act, *ACT_START)
            for g in range(0, NT, T):
                q = slot["QB0"] if g // T % 2 == 0 else slot["QB1"]
                n = min(T, NT - g)
                act.wait_ge(S["w_filled"], g // T + 1)
                act.activation(w_hi[:, 2 + g:2 + g + n, :].rearrange("p a f -> p (a f)"),
                               q[:, 0:n * P], ACT.Copy, scale=WS).then_inc(S["w_hi_made"], 1)
            act.wait_ge(S["w_filled"], N_GROUPS + 1)
            act.activation(w_seT[:, :], slot["QA"][:, 0:KD], ACT.Copy).then_inc(S["vec_made"], 1)
            act.activation(rowc[:, :], slot["QA"][:, HALF:HALF + NR], ACT.Copy)\
                .then_inc(S["vec_made"], 1)
            act.activation(v_lr[:, :], slot["R0"][:, 0:2 * H], ACT.Copy).then_inc(S["vec_made"], 1)
            act.activation(ident16[:, :], ident[:, :], ACT.Copy).then_inc(S["vec_made"], 1)

            def copy(dst, src, name, scale=1.0):
                act.activation(dst, src, ACT.Copy, scale=scale).then_inc(S[name], 1)

            flat = lambda x: x.rearrange("p t d -> p (t d)")

            def halves_of(b, use, hi, f=None):
                q = wait_full(act, b, use)
                if f is not None:
                    copy(f[:, :], q[:, :], f"{use}_f")
                copy(hi[:, :], q[:, :], f"{use}_hi")

            def norm0_b(a, pa):
                rstd = rstds[:, 0, :]
                made(act, "ln0_rstd", a, 1)
                for t in range(T):
                    x = x2[:, pa, t, :]
                    ins = act.activation(x, x, ACT.Identity, bias=shift[:, t:t + 1],
                                         scale=rstd[:, t:t + 1])
                ins.then_inc(S["ln0_done"], 1)

            def x0T(a, pa):
                halves_of(a, "x0T", xT_hi)

            def adjacency(a, pa, t):
                for i in range(2):
                    q = wait_full(act, a, f"adj{t}_{i}")
                    copy(t_hi2[:, pa, 4 * i:4 * i + 4, t * P:(t + 1) * P],
                         q.rearrange("p (m n) -> p m n", m=T // 2), "t_hi_made", scale=NS)

            def aggregate_in(a, pa):
                q = wait_full(act, a, "y")
                copy(y_hi[:, :, 0:D], by_tile(q[:, :]), "y_hi_made", scale=1 / WS)

            def x1T(a, pa):
                halves_of(a, "x1T", xT_hi, xT)

            def conv1(a, pa):
                q = wait_full(act, a, "conv1")
                act.activation(fa[:, :], q[:, :], ACT.Relu, bias=bn_shift[:, 0:1],
                               scale=bn_scale[:, 0:1]).then_inc(S["conv1_made"], 1)
                made(act, "conv1_made", a, 1)
                copy(c_hi[:, inner], fa[:, :], "c_hi_made")

            def conv2_b(a, pa):
                made(act, "c2_made", a, 1)
                act.activation(fa[:, :], fa[:, :], ACT.Relu, bias=bn_shift[:, 1:2])\
                    .then_inc(S["xc_made"], 1)
                made(act, "xc_made", a, 1)
                copy(xc_hi[:, :], fa[:, :], "xc_hi_made")

            def message_in_b(a, pa):
                made(act, "msg_pre", a, 1)
                act.activation(m_hi, by_tile(fa[:, :]), ACT.Relu).then_inc(S["m_hi_made"], 1)

            def s_rows(a, pa):
                q = wait_full(act, a, "s")
                act.activation(sv, q[0:KD, :], ACT.Identity, bias=b_se[:, 0:1])\
                    .then_inc(S["s_made"], 1)

            def unit(a, pa, u):
                q = wait_full(act, a, f"dist{u}")
                if u >= 2:
                    made(act, "g_made", a, u - 1)
                act.activation(expd[:, u % 2, :], q[:, :], ACT.Exp).then_inc(S["exp_made"], 1)

            def unit_halves(a, pa, u):
                made(act, "g_made", a, u + 1)
                if u - 2 == T - 1:
                    wait_full(act, a, "nmp0")
                elif u >= 2:
                    made(act, "g_used", a, u - 1 - (u - 2 >= T))
                copy(g_hl[:, u % 2, 0, :], gw[:, u % 2, :], "g_hi_made")

            def received(a, pa, i):
                q = wait_full(act, a, f"nmp{i}")
                at = slice(i * HALF, (i + 1) * HALF)
                copy(fa[:, at], q, "xn_made", scale=1 / NS)
                made(act, "xn_made", a, i + 1)
                copy(xn_hi[:, at], fa[:, at], "xn_hi_made")

            def gates(a, pa):
                q = wait_full(act, a, "gate_r")
                act.activation(gate_t[:, 0, :], q[:, :], ACT.Tanh, bias=half_b[:, 0:1],
                               scale=0.5 / WS).then_inc(S["tanh_r"], 1)

            def candidate(a, pa):
                q = wait_full(act, a, "gate_z")
                act.activation(gate_t[:, 1, :], q[:, :], ACT.Tanh, bias=half_b[:, 1:2],
                               scale=0.5 / WS).then_inc(S["tanh_z"], 1)
                made(act, "v_made", a, 1)
                act.activation(cand, hid, ACT.Tanh, bias=gate_b[:, 0, 2:3],
                               scale=1 / WS).then_inc(S["cand_made"], 1)

            def norm1(a, pa):
                q = wait_full(act, a, "l1r")
                copy(flat(x2[:, pa, :, :]), q[:, :], "r1_nat")

            def x2T(a, pa):
                halves_of(a, "x2T", xT_hi, xT)

            def project(a, pa):
                q = wait_full(act, a, "sl")
                copy(flat(sl[:, :, :]), q[:, 0:T * H], "sl_made")
                made(act, "sl_made", a, 1)
                copy(flat(sl4[:, :, :]), flat(sl[:, :, :]), "sl4_made", scale=4.0)

            def s_right(a, pa):
                for h in range(H):
                    q = wait_full(act, a, f"sr_{h}")
                    copy(sr[:, h, :], q[:, :], "sr_made", scale=1 / WS)

            def to_sbuf(b, pb, t, g, j):
                h = 2 * g + j
                i = t * H + h
                q = wait_full(act, b, f"pT{i}")
                if i == 0:
                    made(act, "r3_made", b, 0)
                if t and h < 2:
                    made(act, "pT_used", b, t)
                elif t:
                    wait_full(act, b, f"att{t - 1}")
                copy(pT[:, h, :], q[:, :], "pT_made")

            def scores(b, pb, t, g, j):
                h = 2 * g + j
                i = t * H + h
                if i == 0:
                    made(act, "sl4_made", b, 1)
                made(act, "z_made", b, i + 1)
                made(act, "zr_made", b, max(i - 1, 0))
                act.activation(relu[:, h % 2, :], zbuf[:, h, :], ACT.Relu,
                               bias=sl4[:, t, h:h + 1], scale=4.0).then_inc(S["relu_made"], 1)

            def probs(b, pb, t, g, j):
                h = 2 * g + j
                made(act, "eb", b, (t * H + h) // 2 + 1)
                made(act, "zr_made", b, t * H + h + 1)
                act.activation(zbuf[:, h, :], zbuf[:, h, :], ACT.Exp, bias=ebias[:, t, h:h + 1],
                               scale=SLOPE2, accum_out=rsum[:, t, h:h + 1])\
                    .then_inc(S["p_made"], 1)

            def to_turn(b, pb, t):
                q = wait_full(act, b, f"att{t}")
                copy(attT[:, :], q[:, 0:P], "attT_made")

            def x3T(b, pb):
                halves_of(b, "x3T", x3_hi)

            def h3_(b, pb):
                q = wait_full(act, b, "h3")
                copy(flat(h3), q[:, :], "h3_made", scale=1 / WS)
                for g in range(2):
                    made(act, "vk_made", b, g + 1)
                    vk_high(0, g)

            def vk_high(k, g):
                tiles = slice(4 * g, 4 * g + 4)
                copy(flat(vk_hl[k % 2][:, 0, tiles, :]), flat(vk[:, tiles, :]), "vk_hi_made")

            def hop(b, pb, k, g):
                if k < 2:
                    made(act, "hop_read", b, 2 * k + g + 1)
                    if k == 1:
                        wait_full(act, b, "hop0_1")
                    vk_high(k + 1, g)

            run(act, norm0_b=norm0_b, late=lambda name: int(name in SLOW), x0T=x0T,
                adjacency=adjacency, aggregate_in=aggregate_in, x1T=x1T, conv1=conv1,
                conv2_b=conv2_b, message_in_b=message_in_b, s_rows=s_rows, unit=unit,
                unit_halves=unit_halves, received=received, gates=gates, candidate=candidate,
                norm1=norm1, x2T=x2T, project=project, s_right=s_right, scores=scores,
                probs=probs, to_sbuf=to_sbuf, to_turn=to_turn, x3T=x3T, h3=h3_, hop=hop)

        @block.vector
        def _(dve):
            mul, add, sub, mx = ALU.mult, ALU.add, ALU.subtract, ALU.max
            start(dve, *DVE_START)

            def once(ins, name):
                ins.then_inc(S[name], 1)

            for g in range(0, NT, T):
                q = slot["QB0"] if g // T % 2 == 0 else slot["QB1"]
                n = min(T, NT - g)
                dve.wait_ge(S["w_hi_made"], g // T + 1)
                fl = lambda w: w[:, 2 + g:2 + g + n, :].rearrange("p a f -> p (a f)")
                once(dve.scalar_tensor_tensor(fl(w_lo), q[:, 0:n * P], WS, fl(w_hi), mul, sub),
                     "w_lo_made")
            dve.wait_ge(S["const_loaded"], 16 * N_CONST)
            for j, scale in ((W_SELF, NS), (W_AGG, WS)):
                w0raw = escore[:, 0, j * P:(j + 1) * P]
                once(dve.tensor_scalar(w_hi[:, j, :], w0raw, scale, None, mul), "dve_once")
                dve.wait_ge(S["dve_once"], j + 1)
                once(dve.scalar_tensor_tensor(w_lo[:, j, :], w0raw, scale, w_hi[:, j, :], mul, sub),
                     "w_lo_made")
            dve.wait_ge(S["vec_made"], 4)
            for h in range(H):
                vec = v_lr[:, H + h:H + h + 1].to_broadcast([P, P])
                once(dve.tensor_scalar(vr_hi[:, h, :], vec, WS, None, mul), "dve_once")
                dve.wait_ge(S["dve_once"], 3 + h)
                ins = dve.scalar_tensor_tensor(vr_lo[:, h, :], vec, WS, vr_hi[:, h, :], mul, sub)
            once(ins, "w_lo_made")
            dve.wait_ge(S["bn_ready"], 2)
            once(dve.tensor_tensor(bn_tmp[:, :], bn_tmp[:, :], bn[:, 0, :], mul), "dve_once")
            dve.wait_ge(S["dve_once"], 7)
            once(dve.tensor_scalar(bn_scale[:, :], bn_tmp[:, :], 1 / WS, None, mul), "dve_once")
            once(dve.tensor_tensor(bn_tmp[:, :], bn_tmp[:, :], bn[:, 2, :], mul), "dve_once")
            dve.wait_ge(S["dve_once"], 9)
            once(dve.tensor_tensor(bn_shift[:, :], bn[:, 1, :], bn_tmp[:, :], sub), "dve_once")
            once(dve.tensor_tensor(half_b[:, :], gate_b[:, 0, 0:2], gate_b[:, 1, 0:2], add), "dve_once")
            once(dve.tensor_scalar(hid_b[:, :], gate_b[:, 1, 2:3], WS, None, mul), "dve_once")
            dve.wait_ge(S["dve_once"], 12)
            once(dve.tensor_scalar(half_b[:, :], half_b[:, :], 0.5, None, mul), "dve_once")
            dve.wait_ge(S["dve_once"], 13)

            flat = lambda x: x.rearrange("p t d -> p (t d)")

            def bias_row(at, n=T):
                return rowc[:, at:at + D].unsqueeze(1).to_broadcast([P, n, D])

            def low(dst, src, scale, hi, name):
                dve.scalar_tensor_tensor(dst, src, scale, hi, mul, sub).then_inc(S[name], 1)

            def minus(dst, x, y, name):
                dve.tensor_tensor(dst, x, y, sub).then_inc(S[name], 1)

            def low_of(b, use, hi, lo):
                made(dve, f"{use}_hi", b, 1)
                minus(lo[:, :], slot["QA"][:, :], hi[:, :], f"{use}_lo")

            def layer_norm(b, k, x):
                mv = mvs[:, k // 3, :, :]
                for t in range(T):
                    ins = dve.bn_stats(stats[:, t, :], x[:, t, :])
                ins.then_inc(S[f"ln{k}_stats"], 1)
                wait_apart(dve, (S[f"ln{k}_stats"], count(f"ln{k}_stats", b, 1)))
                for t in range(T):
                    ins = dve.bn_aggr(mv[:, t, :], stats[:, t, :])
                ins.then_inc(S[f"ln{k}_mv"], 1)

            def scaled(k):
                mv, rstd = mvs[:, 0, :, :], rstds[:, 0, :]

                def norm(b, p):
                    made(dve, f"ln{k}_rstd", b, 1)
                    for t in range(T):
                        x = x2[:, p, t, :]
                        ins = dve.tensor_scalar(x, x, mv[:, t, 0:1], rstd[:, t:t + 1], sub, mul)
                    ins.then_inc(S[f"ln{k}_done"], 1)
                return norm

            def x0T(a, pa):
                low_of(a, "x0T", xT_hi, xT_lo)

            def adjacency(a, pa, t):
                at = slice(t * P, (t + 1) * P)
                for i in range(2):
                    made(dve, "t_hi_made", a, 2 * t + i + 1)
                    low(t_lo2[:, pa, 4 * i:4 * i + 4, at],
                        slot[f"QA{i}"].rearrange("p (m n) -> p m n", m=T // 2), NS,
                        t_hi2[:, pa, 4 * i:4 * i + 4, at], "t_lo_made")

            def aggregate_in(a, pa):
                made(dve, "y_hi_made", a, 1)
                low(y_lo[:, :, :], by_tile(slot["QA"][:, :]), 1 / WS, y_hi[:, :, 0:D], "y_lo_made")

            def aggregate(a, pa, c):
                if c % 2 == 0:
                    return
                g = c // 2
                q = wait_full(dve, a, f"l0_{g}")[:, :].rearrange("p (t c) -> p t c", c=256)
                tiles = slice(4 * g, 4 * g + 4)
                pre = fa[:, 0:HALF].rearrange("p (t d) -> p t d", t=4)
                if g:
                    made(dve, "l0_sum", a, g)
                dve.scalar_tensor_tensor(pre, q[:, :, 0:D], 1 / NS, bias_row(R_B0, 4), mul, add)\
                    .then_inc(S["l0_pre"], 1)
                dve.tensor_scalar(rinv2[:, pa, tiles], q[:, :, D], NS * ROW_EPS, None, add)\
                    .then_inc(S["rs_made"], 1)
                made(dve, "l0_pre", a, g + 1)
                dve.scalar_tensor_tensor(x2[:, pa, tiles, :], pre, 0.0, x2[:, pa, tiles, :], mx, add)\
                    .then_inc(S["l0_sum"], 1)

            def norm0(a, pa):
                made(dve, "rs_made", a, 2)
                dve.reciprocal(rinv2[:, pa, :], rinv2[:, pa, :]).then_inc(S["rinv_made"], 1)
                wait_apart(dve, (S["l0_sum"], count("l0_sum", a, 2)))
                layer_norm(a, 0, x2[:, pa, :, :])

            def x1T(a, pa):
                low_of(a, "x1T", xT_hi, xT_lo)

            def conv1(a, pa):
                made(dve, "c_hi_made", a, 1)
                minus(c_lo[:, inner], fa[:, :], c_hi[:, inner], "c_lo_made")

            def conv2(a, pa, c):
                if c == CONV_CHUNKS - 1:
                    q = wait_full(dve, a, "conv2")
                    made(dve, "c_lo_made", a, 1)
                    dve.scalar_tensor_tensor(fa[:, :], q[:, :], bn_scale[:, 1:2], xT[:, :], mul, add)\
                        .then_inc(S["c2_made"], 1)

            def conv2_b(a, pa):
                made(dve, "xc_hi_made", a, 1)
                minus(xc_lo[:, :], fa[:, :], xc_hi[:, :], "xc_lo_made")

            def message_in(a, pa):
                q = wait_full(dve, a, "msg")
                made(dve, "xc_lo_made", a, 1)
                dve.scalar_tensor_tensor(by_tile(fa[:, :]), by_tile(q[:, :]), 1 / WS,
                                         bias_row(R_BM), mul, add).then_inc(S["msg_pre"], 1)

            def message_in_b(a, pa):
                made(dve, "m_hi_made", a, 1)
                dve.scalar_tensor_tensor(m_lo[:, :, :], by_tile(fa[:, :]), 0.0, m_hi, mx, sub)\
                    .then_inc(S["m_lo_made"], 1)

            def s_rows(a, pa):
                made(dve, "s_made", a, 1)
                dve.tensor_tensor(sq, sv, sv, mul).then_inc(S["sq_made"], 1)

            def s_sum(a, pa):
                q = wait_full(dve, a, "nsqr")
                dve.tensor_tensor(sv, sv, q[0:KD, :], add).then_inc(S["sv_made"], 1)
                made(dve, "sv_made", a, 1)
                dve.tensor_copy(s_p[:, 0, :], sv).then_inc(S["sp1_made"], 1)
                made(dve, "sp1_made", a, 1)
                minus(sv, sv, s_p[:, 0, :], "sv1_made")

            def s_parts(a, pa):
                made(dve, "sv1_made", a, 1)
                dve.tensor_copy(s_p[:, 1, :], sv).then_inc(S["sp2_made"], 1)
                made(dve, "sp2_made", a, 1)
                minus(sv, sv, s_p[:, 1, :], "sv2_made")

            def s_sides(a, pa, side):
                pick = lambda part: dist_c[:, KD + PARTS * side + part:KD + PARTS * side + part + 1]
                ones = dist_c[:, KD + 2 * PARTS + 1 - side:KD + 2 * PARTS + 2 - side]
                dve.tensor_scalar(d_t[:, side, :], s_p[:, 0, :], pick(0), ones, mul, add)\
                    .then_inc(S["d_first"], 1)
                made(dve, "d_first", a, side + 1)
                dve.scalar_tensor_tensor(d_t[:, side, :], s_p[:, 1, :], pick(1), d_t[:, side, :],
                                         mul, add).then_inc(S["d_second"], 1)
                made(dve, "sv2_made", a, 1)
                made(dve, "d_second", a, side + 1)
                dve.scalar_tensor_tensor((d_l, d_r)[side], sv, pick(2), d_t[:, side, :], mul, add)\
                    .then_inc(S["d_made"], 1)

            def unit(a, pa, u):
                q = wait_full(dve, a, f"mask{u}")
                made(dve, "exp_made", a, u + 1)
                if u >= 2:
                    made(dve, "g_lo_made", a, u - 1)
                dve.tensor_tensor(gw[:, u % 2, :], expd[:, u % 2, :], q, mul)\
                    .then_inc(S["g_made"], 1)

            def unit_halves(a, pa, u):
                made(dve, "g_hi_made", a, u + 1)
                minus(g_hl[:, u % 2, 1, :], gw[:, u % 2, :], g_hl[:, u % 2, 0, :], "g_lo_made")

            def received(a, pa, i):
                at = slice(i * HALF, (i + 1) * HALF)
                made(dve, "xn_hi_made", a, i + 1)
                minus(xn_lo[:, at], fa[:, at], xn_hi[:, at], "xn_lo_made")

            def gates(a, pa):
                q = wait_full(dve, a, "hid_n")
                dve.tensor_scalar(hid, q[:, :], hid_b[:, 0:1], None, add).then_inc(S["hid_made"], 1)
                made(dve, "hid_made", a, 1)
                made(dve, "tanh_r", a, 1)
                dve.scalar_tensor_tensor(hid, gate_t[:, 0, :], 1.0, hid, add, mul)\
                    .then_inc(S["u_made"], 1)

            def gates_b(a, pa):
                q = wait_full(dve, a, "in_n")
                made(dve, "u_made", a, 1)
                dve.scalar_tensor_tensor(hid, hid, 0.5, q[:, :], mul, add).then_inc(S["v_made"], 1)

            def candidate(a, pa):
                made(dve, "cand_made", a, 1)
                minus(fa[:, :], xT[:, :], cand, "w_made")
                made(dve, "w_made", a, 1)
                made(dve, "tanh_z", a, 1)
                dve.scalar_tensor_tensor(fa[:, :], gate_t[:, 1, :], 1.0, fa[:, :], add, mul)\
                    .then_inc(S["w2_made"], 1)
                made(dve, "w2_made", a, 1)
                dve.scalar_tensor_tensor(fa[:, :], fa[:, :], 0.5, cand, mul, add)\
                    .then_inc(S["o_made"], 1)
                made(dve, "o_made", a, 1)
                dve.tensor_tensor(fa[:, :], fa[:, :], xT[:, :], add).then_inc(S["r1_made"], 1)

            def norm1(a, pa):
                wait_apart(dve, (S["r1_nat"], count("r1_nat", a, 1)))
                layer_norm(a, 1, x2[:, pa, :, :])

            def x2T(a, pa):
                low_of(a, "x2T", xT_hi, xT_lo)

            def project(a, pa):
                q = wait_full(dve, a, "h2")
                dve.scalar_tensor_tensor(h2[:, :, :], by_tile(q[:, :]), 1 / WS, bias_row(R_B2),
                                         mul, add).then_inc(S["h2_made"], 1)

            def prepare(b, t):
                e = escore[:, t % 2, :]
                dve.wait_ge(S[f"e_loaded{t % 2}"], b * (8 * T) + 16 * (t // 2 + 1))
                if t:
                    made(dve, "e_made", b, t)
                dve.tensor_scalar(padv[:, :], e, 1e-5, MASKED, ALU.is_le, mul)\
                    .then_inc(S["pad_made"], 1)
                made(dve, "pad_made", b, t + 1)
                dve.scalar_tensor_tensor(e, e, rowc[:, R_AW + 2 * DH:NR], padv[:, :], mul, add)\
                    .then_inc(S["e_made"], 1)

            def scores(b, pb, t, g, j):
                h = 2 * g + j
                if t == 0 and h == 0:
                    prepare(b, 0)
                e = escore[:, t % 2, :]
                i = t * H + h
                waits = [(S["e_made"], count("e_made", b, t + 1))]
                if t == 0:
                    waits.append((S["sr_made"], count("sr_made", b, h + 1)))
                else:
                    waits.append(full_count(b, f"pT{i - H}"))
                wait_apart(dve, *waits)
                dve.tensor_tensor_reduce(out=zbuf[:, h, :], in0=e, in1=sr[:, h, :], scale=1.0,
                                         scalar=-3e38, op0=add, op1=mx,
                                         accum_out=zmax[:, t, h:h + 1])\
                    .then_inc(S["z_made"], 1)
                if h == H - 1 and t + 1 < T:
                    prepare(b, t + 1)

            def exp_bias(b, t, g):
                if t == 0 and g == 0:
                    made(dve, "sl_made", b, 1)
                two = slice(2 * g, 2 * g + 2)
                done = 2 * t + g + 1
                made(dve, "z_made", b, 2 * done)
                dve.tensor_tensor(etmp[:, t, two], zmax[:, t, two], sl[:, t, two], add)\
                    .then_inc(S["zsum"], 1)
                made(dve, "zsum", b, done)
                dve.scalar_tensor_tensor(etmp[:, t, two], etmp[:, t, two], SLOPE2, etmp[:, t, two],
                                         mul, mx).then_inc(S["leak"], 1)
                made(dve, "leak", b, done)
                dve.scalar_tensor_tensor(ebias[:, t, two], sl[:, t, two], SLOPE2, etmp[:, t, two],
                                         mul, sub).then_inc(S["eb"], 1)

            def probs(b, pb, t, g, j):
                h = 2 * g + j
                if h % 2 == 0:
                    exp_bias(b, t, h // 2)
                made(dve, "relu_made", b, t * H + h + 1)
                dve.tensor_tensor(zbuf[:, h, :], zbuf[:, h, :], relu[:, h % 2, :], add)\
                    .then_inc(S["zr_made"], 1)

            def turned(b, pb, t):
                xb = x2[:, pb, :, :]
                made(dve, "p_made", b, H * (t + 1))
                dve.reciprocal(rsum[:, t, :], rsum[:, t, :]).then_inc(S["rs_inv"], 1)
                q = wait_full(dve, b, f"attT{t}")
                made(dve, "rs_inv", b, t + 1)
                if t:
                    made(dve, "r2_made", b, t)
                heads = lambda x: x.rearrange("p (h d) -> p h d", h=H)
                dve.tensor_tensor(heads(attn[:, :]), heads(q[:, 0:P]),
                                  rsum[:, t, :].unsqueeze(2).to_broadcast([P, H, DH]), mul)\
                    .then_inc(S["att_scaled"], 1)
                made(dve, "att_scaled", b, t + 1)
                dve.tensor_tensor(attn[:, :], attn[:, :], xb[:, t, :], add)\
                    .then_inc(S["att_pre"], 1)
                made(dve, "att_pre", b, t + 1)
                dve.scalar_tensor_tensor(attn[:, :], attn[:, :], SLOPE2_OUT, attn[:, :], mul, mx)\
                    .then_inc(S["att_leak"], 1)
                made(dve, "att_leak", b, t + 1)
                dve.tensor_tensor(xb[:, t, :], xb[:, t, :], attn[:, :], add)\
                    .then_inc(S["r2_made"], 1)

            def norm2(b, pb):
                wait_apart(dve, (S["r2_made"], count("r2_made", b, T)))
                layer_norm(b, 2, x2[:, pb, :, :])

            def x3T(b, pb):
                low_of(b, "x3T", x3_hi, x3_lo)

            def split_v(b, k, g):
                tiles = slice(4 * g, 4 * g + 4)
                made(dve, "vk_hi_made", b, 2 * k + g + 1)
                minus(flat(vk_hl[k % 2][:, 1, tiles, :]), flat(vk[:, tiles, :]),
                      flat(vk_hl[k % 2][:, 0, tiles, :]), "vk_lo_made")

            def own_term(b, k, g):
                w = rowc[:, R_CW + 2 - k:R_CW + 3 - k]
                shift, op = (rowc[:, R_CB:R_CB + 1], add) if k == 2 else (None, ALU.bypass)
                at = slice(g * HALF, (g + 1) * HALF)
                dve.tensor_scalar(wh[:, at], flat(h3)[:, at], w, shift, mul, op)\
                    .then_inc(S["wh_made"], 1)

            def h3_(b, pb):
                made(dve, "h3_made", b, 1)
                for g in range(2):
                    tiles = slice(4 * g, 4 * g + 4)
                    dve.tensor_scalar(flat(vk[:, tiles, :]), flat(h3[:, tiles, :]),
                                      rowc[:, R_CW + 3:R_CW + 4], None, mul).then_inc(S["vk_made"], 1)
                for g in range(2):
                    own_term(b, 0, g)
                    split_v(b, 0, g)

            def hop(b, pb, k, g):
                q = wait_full(dve, b, f"hop{k}_{g}")
                made(dve, "wh_made", b, 2 * k + g + 1)
                made(dve, "vk_lo_made", b, 2 * k + g + 1)
                for i in range(4):
                    t = 4 * g + i
                    ins = dve.scalar_tensor_tensor(
                        vk[:, t, :], q[:, i * P:(i + 1) * P], rinv2[:, pb, t:t + 1],
                        wh[:, t * P:(t + 1) * P], mul, add)
                ins.then_inc(S["hop_read"], 1)
                if k < 2:
                    made(dve, "hop_read", b, 2 * k + g + 1)
                    own_term(b, k + 1, g)
                    split_v(b, k + 1, g)

            def finish(b, pb):
                xb = x2[:, pb, :, :]
                made(dve, "hop_read", b, 6)
                dve.scalar_tensor_tensor(flat(vk), flat(vk), SLOPE3, flat(vk), mul, mx)\
                    .then_inc(S["out_leak"], 1)
                made(dve, "out_leak", b, 1)
                dve.tensor_tensor(flat(xb), flat(xb), flat(vk), add).then_inc(S["r3_made"], 1)
                wait_apart(dve, (S["r3_made"], count("r3_made", b, 1)))
                layer_norm(b, 3, xb)

            run(dve, late=lambda name: 1 + SLOW.get(name, 0), x0T=x0T, adjacency=adjacency,
                aggregate_in=aggregate_in, aggregate=aggregate, norm0=norm0, x1T=x1T, conv1=conv1,
                conv2=conv2, conv2_b=conv2_b, message_in=message_in, message_in_b=message_in_b,
                s_rows=s_rows, s_sum=s_sum, s_parts=s_parts, s_sides=s_sides, unit=unit,
                unit_halves=unit_halves, received=received, norm1_b=scaled(1), norm2_b=scaled(2),
                gates=gates, gates_b=gates_b, candidate=candidate, norm1=norm1, x2T=x2T,
                project=project, scores=scores, probs=probs, turned=turned, norm2=norm2, x3T=x3T,
                h3=h3_, hop=hop, finish=finish)


def distance_constants(kd=64, parts=3, nc=3):
    import numpy as np
    c = np.zeros((kd, kd + 2 * parts + 2), np.float32)
    left, right, ones = kd, kd + parts, (kd + 2 * parts, kd + 2 * parts + 1)
    pairs = sorted(((i, j) for i in range(parts) for j in range(parts)), key=sum)
    for g, (i, j) in enumerate(pairs):
        rows = slice(2 + g * nc, 2 + (g + 1) * nc)
        c[rows, left + i] = 2.0
        c[rows, right + j] = 1.0
    last = 2 + nc * len(pairs)
    for k in range(parts):
        r = 2 * k if k == 0 else last + 2 * (k - 1)
        c[2:2 + nc, r:r + 2] = -1.0
        c[r, left + k] = 1.0
        c[r, ones[0]] = 1.0
        c[r + 1, right + k] = 1.0
        c[r + 1, ones[1]] = 1.0
    return c


def kernel(**inputs):
    import numpy as np
    import concourse.bacc as bacc
    from concourse.bass_utils import run_bass_kernel_spmd

    nc = bacc.Bacc("TRN2", target_bir_lowering=False, num_devices=1)
    arrays, aps = {}, {}
    for name, value in [*inputs.items(), ("dist_c", distance_constants())]:
        value = np.ascontiguousarray(value)
        arrays[f"in_{name}"] = value
        aps[name] = nc.dram_tensor(f"in_{name}", value.shape, mybir.dt.from_np(value.dtype),
                                   kind="ExternalInput").ap()
    shape = inputs["x"].shape
    out = nc.dram_tensor("out", shape, mybir.dt.float32, kind="ExternalOutput").ap()
    gnn_stack_kernel(nc, aps, out)
    r = run_bass_kernel_spmd(nc, [arrays], core_ids=[0])
    return r.results[0]["out"]
```
